# Optimizing a Trainium2 kernel written in Bass

```python
import numpy as np
import jax
import jax.numpy as jnp

def _softmax(x, axis=-1):
    return jax.nn.softmax(x, axis=axis)

def _gelu(x):
    return jax.nn.gelu(x, approximate=True)

def _silu(x):
    return jax.nn.silu(x)

def _sigmoid(x):
    return jax.nn.sigmoid(x)

def _layernorm(x, axis=-1, eps=1e-05):
    m = jnp.mean(x, axis=axis, keepdims=True)
    v = jnp.var(x, axis=axis, keepdims=True)
    return (x - m) / jnp.sqrt(v + eps)

def _scatter_add(tgt, idx, src, axis=0):
    return tgt.at[idx].add(src)

def _segment_sum(src, seg, n):
    return jax.ops.segment_sum(src, seg, n)
kernel_name = 'mk_flamingo_gated_d2_seqx_r4_afc3c6'

def setup_inputs(seed: int=0):
    np.random.seed(seed)
    _w = jnp.asarray

    def _rec_inputs():
        import jax
        import jax.numpy as jnp
        _rk = jax.random.key(seed)
        x = -0.0002928 + 1 * jax.random.normal(jax.random.fold_in(_rk, 1), (32, 100, 256), jnp.float32)
        _lenS = 100 - jax.random.randint(jax.random.fold_in(_rk, 7), (32,), 0, max(1, 100 // 4) + 1, jnp.int32)
        _lenS2 = 361 - jax.random.randint(jax.random.fold_in(_rk, 8), (32,), 0, max(1, 361 // 4) + 1, jnp.int32)
        _ctx_768P = jax.random.normal(jax.random.fold_in(_rk, 11), (32, 16, 192), jnp.float32)
        _ctx_768c = jax.random.dirichlet(jax.random.fold_in(_rk, 511), 0.3 * jnp.ones((16,), jnp.float32), (32, 361))
        _ctx_768t = jnp.einsum('bsk,bkd->bsd', _ctx_768c, _ctx_768P)
        _ctx_768t = _ctx_768t * jax.lax.rsqrt(jnp.mean(jnp.square(_ctx_768t)) + 1e-12) * 0.953939
        ctx_768 = 2.09791e-05 + 1.00001 * (_ctx_768t + 0.3 * jax.random.normal(jax.random.fold_in(_rk, 611), (32, 361, 192), jnp.float32))
        _validS = jnp.arange(100)[None, :] < _lenS[:, None]
        _validS2 = jnp.arange(361)[None, :] < _lenS2[:, None]
        _causal = jnp.tril(jnp.ones((100, 100), dtype=bool))
        mask_BxS2_bk0 = jnp.logical_not(jnp.broadcast_to(_validS2[:, :], (32, 361)))
        _g = jax.random.normal(jax.random.fold_in(_rk, 9001), (2, 2), jnp.float32)
        _g = jnp.sign(_g) * jnp.maximum(jnp.abs(_g), 1.0) + (_g == 0) * 1.0
        g_xattn = _g[0]
        g_ffn = _g[1]
        return (x, ctx_768, mask_BxS2_bk0, g_xattn, g_ffn)
    x, ctx_768, mask_BxS2_bk0, g_xattn, g_ffn = _rec_inputs()

    def _L0_xattn_setup():
        import jax, jax.numpy as jnp
        import numpy as np
        H = 8
        D = 64
        SCALE = D ** (-0.5)
        key = jax.random.key(seed)
        ks = jax.random.split(key, 7)
        B, Nq, Nkv = (2, 512, 512)
        Cq, Ck, I = (256, 192, H * D)
        return {'x': jax.random.normal(ks[0], (B, Nq, Cq), jnp.float32), 'context': jax.random.normal(ks[1], (B, Nkv, Ck), jnp.float32), 'Wq': jax.random.normal(ks[2], (Cq, I), jnp.float32) * Cq ** (-0.5), 'Wk': jax.random.normal(ks[3], (Ck, I), jnp.float32) * Ck ** (-0.5), 'Wv': jax.random.normal(ks[4], (Ck, I), jnp.float32) * Ck ** (-0.5), 'Wo': jax.random.normal(ks[5], (I, Cq), jnp.float32) * I ** (-0.5), 'bo': jnp.zeros((Cq,), jnp.float32)}
    _L0_xattn_all = _L0_xattn_setup()
    _L0_xattn_in = {k: v for k, v in _L0_xattn_all.items() if k in ('Wq', 'Wk', 'Wv', 'Wo', 'bo')}
    del _L0_xattn_all

    def _L0_ffn_setup():
        import jax, jax.numpy as jnp
        import numpy as np
        NUM_EXPERTS = 8
        TOP_K = 2
        MOE_DIM = 512

        def _moe_forward(x, moe_router, moe_w13, moe_w2):
            b, s, d = x.shape
            x_flat = x.reshape(b * s, d)
            router_logits = jnp.einsum('td,de->te', x_flat, moe_router)
            topk_logits, topk_idx = jax.lax.top_k(router_logits, TOP_K)
            topk_weights = jax.nn.softmax(topk_logits, axis=-1).astype(x.dtype)
            tokens = x_flat.shape[0]
            expert_ids = topk_idx.reshape(tokens * TOP_K)
            dispatch_weights = topk_weights.reshape(tokens * TOP_K)
            sort_idx = jnp.argsort(expert_ids, axis=0)
            token_ids = jnp.arange(tokens * TOP_K, dtype=jnp.int32) // TOP_K
            token_ids_sort = token_ids[sort_idx]
            x_sort = x_flat[token_ids_sort]
            w_sort = dispatch_weights[sort_idx].astype(x_flat.dtype)
            group_sizes = jnp.bincount(expert_ids, length=NUM_EXPERTS).astype(jnp.int32)
            w13_out = jax.lax.ragged_dot(x_sort, moe_w13, group_sizes)
            gate, up = jnp.split(w13_out, [MOE_DIM], axis=-1)
            hidden = jax.nn.silu(gate) * up
            out_dispatch = jax.lax.ragged_dot(hidden, moe_w2, group_sizes)
            out_flat = jnp.zeros_like(x_flat).at[token_ids_sort].add(out_dispatch * w_sort[:, None], mode='drop')
            return out_flat.reshape(b, s, d)
        key = jax.random.key(seed)
        k1, k2, k3, k4 = jax.random.split(key, 4)
        B, S, D = (4, 512, 256)
        x = jax.random.normal(k1, (B, S, D), dtype=jnp.float32)
        moe_router = jax.random.normal(k2, (D, NUM_EXPERTS), dtype=jnp.float32) * 0.02
        moe_w13 = jax.random.normal(k3, (NUM_EXPERTS, D, 2 * MOE_DIM), dtype=jnp.float32) * 0.02
        moe_w2 = jax.random.normal(k4, (NUM_EXPERTS, MOE_DIM, D), dtype=jnp.float32) * 0.02
        return {'x': x, 'moe_router': moe_router, 'moe_w13': moe_w13, 'moe_w2': moe_w2}
    _L0_ffn_all = _L0_ffn_setup()
    _L0_ffn_in = {k: v for k, v in _L0_ffn_all.items() if k in ('moe_router', 'moe_w13', 'moe_w2')}
    del _L0_ffn_all

    def _L1_xattn_setup():
        import jax, jax.numpy as jnp
        import numpy as np
        DIM_IN, DIM_LAT, DIM_HEAD = (192, 256, 64)
        INNER = max(DIM_LAT, DIM_IN)
        HEADS = INNER // DIM_HEAD
        SCALE = DIM_HEAD ** (-0.5)
        RMS_EPS = 1e-08
        LN_EPS = 1e-05

        def layernorm(x, g, b):
            mu = jnp.mean(x, axis=-1, keepdims=True)
            var = jnp.mean((x - mu) ** 2, axis=-1, keepdims=True)
            return (x - mu) * jax.lax.rsqrt(var + LN_EPS) * g + b

        def rmsnorm(x, gamma):
            norm = jnp.sqrt(jnp.sum(x * x, axis=-1, keepdims=True)) * x.shape[-1] ** (-0.5)
            return x / jnp.maximum(norm, RMS_EPS) * gamma
        key = jax.random.key(seed)
        ks = jax.random.split(key, 12)
        b, n, m = (4, 1024, 128)
        x = jax.random.normal(ks[0], (b, n, DIM_IN), jnp.float32)
        latents = jax.random.normal(ks[1], (b, m, DIM_LAT), jnp.float32)
        mask = jax.random.randint(ks[2], (b, n), 0, 2).astype(bool)
        s = lambda k, sh, fan: jax.random.normal(k, sh, jnp.float32) * fan ** (-0.5)
        return {'x': x, 'latents': latents, 'mask': mask, 'ln_x_g': jnp.ones((DIM_IN,), jnp.float32), 'ln_x_b': jnp.zeros((DIM_IN,), jnp.float32), 'ln_l_g': jnp.ones((DIM_LAT,), jnp.float32), 'ln_l_b': jnp.zeros((DIM_LAT,), jnp.float32), 'qn_g': jnp.ones((DIM_HEAD,), jnp.float32), 'kn_g': jnp.ones((DIM_HEAD,), jnp.float32), 'Wq': s(ks[3], (INNER, DIM_LAT), DIM_LAT), 'Wkv': s(ks[4], (2 * INNER, DIM_IN), DIM_IN), 'Wlkv': s(ks[5], (2 * INNER, DIM_LAT), DIM_LAT), 'Wo': s(ks[6], (DIM_LAT, INNER), INNER), 'bo': jnp.zeros((DIM_LAT,), jnp.float32)}
    _L1_xattn_all = _L1_xattn_setup()
    _L1_xattn_in = {k: v for k, v in _L1_xattn_all.items() if k in ('ln_x_g', 'ln_x_b', 'ln_l_g', 'ln_l_b', 'qn_g', 'kn_g', 'Wq', 'Wkv', 'Wlkv', 'Wo', 'bo')}
    del _L1_xattn_all

    def _L1_ffn_setup():
        import jax, jax.numpy as jnp
        import numpy as np
        TOPK = 4
        N_GROUPS = 4
        TOPK_GROUPS = 2
        ROUTE_SCALE = 2.5

        def _gate(x2, Wg):
            T = x2.shape[0]
            E = Wg.shape[0]
            scores = x2 @ Wg.T
            s = jax.nn.sigmoid(scores)
            g = s.reshape(T, N_GROUPS, E // N_GROUPS)
            group_scores = g.max(axis=-1)
            _, gidx = jax.lax.top_k(group_scores, TOPK_GROUPS)
            group_mask = jnp.any(jax.nn.one_hot(gidx, N_GROUPS, dtype=jnp.bool_), axis=1)
            masked = jnp.where(group_mask[:, :, None], g, -jnp.inf).reshape(T, E)
            _, idx = jax.lax.top_k(masked, TOPK)
            w = jnp.take_along_axis(s, idx, axis=1)
            w = w / jnp.sum(w, axis=-1, keepdims=True)
            w = w * ROUTE_SCALE
            return (w.astype(x2.dtype), idx)
        key = jax.random.key(seed)
        ks = jax.random.split(key, 6)
        B, S, D, I, E = (2, 512, 256, 256, 16)
        scale = 0.02
        return {'x': jax.random.normal(ks[0], (B, S, D), dtype=jnp.float32), 'Wg': jax.random.normal(ks[1], (E, D), dtype=jnp.float32) * scale, 'W1': jax.random.normal(ks[2], (E, I, D), dtype=jnp.float32) * scale, 'b1': jnp.zeros((E, I), dtype=jnp.float32), 'W2': jax.random.normal(ks[3], (E, D, I), dtype=jnp.float32) * scale, 'b2': jnp.zeros((E, D), dtype=jnp.float32), 'W3': jax.random.normal(ks[4], (E, I, D), dtype=jnp.float32) * scale, 'b3': jnp.zeros((E, I), dtype=jnp.float32)}
    _L1_ffn_all = _L1_ffn_setup()
    _L1_ffn_in = {k: v for k, v in _L1_ffn_all.items() if k in ('Wg', 'W1', 'b1', 'W2', 'b2', 'W3', 'b3')}
    del _L1_ffn_all
    return {'x': x, 'ctx_768': ctx_768, 'mask_BxS2_bk0': mask_BxS2_bk0, 'g_xattn': g_xattn, 'g_ffn': g_ffn, 'L0_xattn_Wq': _L0_xattn_in['Wq'], 'L0_xattn_Wk': _L0_xattn_in['Wk'], 'L0_xattn_Wv': _L0_xattn_in['Wv'], 'L0_xattn_Wo': _L0_xattn_in['Wo'], 'L0_xattn_bo': _L0_xattn_in['bo'], 'L0_ffn_moe_router': _L0_ffn_in['moe_router'], 'L0_ffn_moe_w13': _L0_ffn_in['moe_w13'], 'L0_ffn_moe_w2': _L0_ffn_in['moe_w2'], 'L1_xattn_ln_x_g': _L1_xattn_in['ln_x_g'], 'L1_xattn_ln_x_b': _L1_xattn_in['ln_x_b'], 'L1_xattn_ln_l_g': _L1_xattn_in['ln_l_g'], 'L1_xattn_ln_l_b': _L1_xattn_in['ln_l_b'], 'L1_xattn_qn_g': _L1_xattn_in['qn_g'], 'L1_xattn_kn_g': _L1_xattn_in['kn_g'], 'L1_xattn_Wq': _L1_xattn_in['Wq'], 'L1_xattn_Wkv': _L1_xattn_in['Wkv'], 'L1_xattn_Wlkv': _L1_xattn_in['Wlkv'], 'L1_xattn_Wo': _L1_xattn_in['Wo'], 'L1_xattn_bo': _L1_xattn_in['bo'], 'L1_ffn_Wg': _L1_ffn_in['Wg'], 'L1_ffn_W1': _L1_ffn_in['W1'], 'L1_ffn_b1': _L1_ffn_in['b1'], 'L1_ffn_W2': _L1_ffn_in['W2'], 'L1_ffn_b2': _L1_ffn_in['b2'], 'L1_ffn_W3': _L1_ffn_in['W3'], 'L1_ffn_b3': _L1_ffn_in['b3']}

def reference(x, ctx_768, mask_BxS2_bk0, g_xattn, g_ffn, L0_xattn_Wq, L0_xattn_Wk, L0_xattn_Wv, L0_xattn_Wo, L0_xattn_bo, L0_ffn_moe_router, L0_ffn_moe_w13, L0_ffn_moe_w2, L1_xattn_ln_x_g, L1_xattn_ln_x_b, L1_xattn_ln_l_g, L1_xattn_ln_l_b, L1_xattn_qn_g, L1_xattn_kn_g, L1_xattn_Wq, L1_xattn_Wkv, L1_xattn_Wlkv, L1_xattn_Wo, L1_xattn_bo, L1_ffn_Wg, L1_ffn_W1, L1_ffn_b1, L1_ffn_W2, L1_ffn_b2, L1_ffn_W3, L1_ffn_b3):
    import jax
    import jax.numpy as jnp

    def _L0_xattn_ref(x, context, Wq, Wk, Wv, Wo, bo):
        import jax, jax.numpy as jnp
        import numpy as np
        H = 8
        D = 64
        SCALE = D ** (-0.5)
        B, Nq, _ = x.shape
        Nkv = context.shape[1]
        q = (x @ Wq).reshape(B, Nq, H, D)
        k = (context @ Wk).reshape(B, Nkv, H, D)
        v = (context @ Wv).reshape(B, Nkv, H, D)
        sim = jnp.einsum('bihd,bjhd->bhij', q, k) * SCALE
        attn = jax.nn.softmax(sim, axis=-1)
        out = jnp.einsum('bhij,bjhd->bihd', attn, v).reshape(B, Nq, H * D)
        return out @ Wo + bo

    def _L0_ffn_ref(x, moe_router, moe_w13, moe_w2):
        import jax, jax.numpy as jnp
        import numpy as np
        NUM_EXPERTS = 8
        TOP_K = 2
        MOE_DIM = 512

        def _moe_forward(x, moe_router, moe_w13, moe_w2):
            b, s, d = x.shape
            x_flat = x.reshape(b * s, d)
            router_logits = jnp.einsum('td,de->te', x_flat, moe_router)
            topk_logits, topk_idx = jax.lax.top_k(router_logits, TOP_K)
            topk_weights = jax.nn.softmax(topk_logits, axis=-1).astype(x.dtype)
            tokens = x_flat.shape[0]
            expert_ids = topk_idx.reshape(tokens * TOP_K)
            dispatch_weights = topk_weights.reshape(tokens * TOP_K)
            sort_idx = jnp.argsort(expert_ids, axis=0)
            token_ids = jnp.arange(tokens * TOP_K, dtype=jnp.int32) // TOP_K
            token_ids_sort = token_ids[sort_idx]
            x_sort = x_flat[token_ids_sort]
            w_sort = dispatch_weights[sort_idx].astype(x_flat.dtype)
            group_sizes = jnp.bincount(expert_ids, length=NUM_EXPERTS).astype(jnp.int32)
            w13_out = jax.lax.ragged_dot(x_sort, moe_w13, group_sizes)
            gate, up = jnp.split(w13_out, [MOE_DIM], axis=-1)
            hidden = jax.nn.silu(gate) * up
            out_dispatch = jax.lax.ragged_dot(hidden, moe_w2, group_sizes)
            out_flat = jnp.zeros_like(x_flat).at[token_ids_sort].add(out_dispatch * w_sort[:, None], mode='drop')
            return out_flat.reshape(b, s, d)
        return _moe_forward(x, moe_router, moe_w13, moe_w2)

    def _L1_xattn_ref(x, latents, mask, ln_x_g, ln_x_b, ln_l_g, ln_l_b, qn_g, kn_g, Wq, Wkv, Wlkv, Wo, bo):
        import jax, jax.numpy as jnp
        import numpy as np
        DIM_IN, DIM_LAT, DIM_HEAD = (192, 256, 64)
        INNER = max(DIM_LAT, DIM_IN)
        HEADS = INNER // DIM_HEAD
        SCALE = DIM_HEAD ** (-0.5)
        RMS_EPS = 1e-08
        LN_EPS = 1e-05

        def layernorm(x, g, b):
            mu = jnp.mean(x, axis=-1, keepdims=True)
            var = jnp.mean((x - mu) ** 2, axis=-1, keepdims=True)
            return (x - mu) * jax.lax.rsqrt(var + LN_EPS) * g + b

        def rmsnorm(x, gamma):
            norm = jnp.sqrt(jnp.sum(x * x, axis=-1, keepdims=True)) * x.shape[-1] ** (-0.5)
            return x / jnp.maximum(norm, RMS_EPS) * gamma
        b, n, _ = x.shape
        m = latents.shape[1]
        xn = layernorm(x, ln_x_g, ln_x_b)
        ln = layernorm(latents, ln_l_g, ln_l_b)
        q = ln @ Wq.T
        kv = jnp.concatenate([xn @ Wkv.T, ln @ Wlkv.T], axis=1)
        k, v = (kv[..., :INNER], kv[..., INNER:])
        split_heads = lambda t: t.reshape(t.shape[0], t.shape[1], HEADS, DIM_HEAD).transpose(0, 2, 1, 3)
        q, k, v = (split_heads(q), split_heads(k), split_heads(v))
        qn = rmsnorm(q, qn_g) * SCALE
        kn = rmsnorm(k, kn_g)
        attn = jnp.einsum('bhid,bhjd->bhij', qn, kn)
        full_mask = jnp.pad(mask, ((0, 0), (0, m)), constant_values=True)
        attn = jnp.where(full_mask[:, None, None, :], attn, -jnp.finfo(attn.dtype).max)
        attn = jax.nn.softmax(attn, axis=-1)
        out = jnp.einsum('bhij,bhjd->bhid', attn, v)
        out = out.transpose(0, 2, 1, 3).reshape(b, m, INNER)
        return out @ Wo.T + bo

    def _L1_ffn_ref(x, Wg, W1, b1, W2, b2, W3, b3):
        import jax, jax.numpy as jnp
        import numpy as np
        TOPK = 4
        N_GROUPS = 4
        TOPK_GROUPS = 2
        ROUTE_SCALE = 2.5

        def _gate(x2, Wg):
            T = x2.shape[0]
            E = Wg.shape[0]
            scores = x2 @ Wg.T
            s = jax.nn.sigmoid(scores)
            g = s.reshape(T, N_GROUPS, E // N_GROUPS)
            group_scores = g.max(axis=-1)
            _, gidx = jax.lax.top_k(group_scores, TOPK_GROUPS)
            group_mask = jnp.any(jax.nn.one_hot(gidx, N_GROUPS, dtype=jnp.bool_), axis=1)
            masked = jnp.where(group_mask[:, :, None], g, -jnp.inf).reshape(T, E)
            _, idx = jax.lax.top_k(masked, TOPK)
            w = jnp.take_along_axis(s, idx, axis=1)
            w = w / jnp.sum(w, axis=-1, keepdims=True)
            w = w * ROUTE_SCALE
            return (w.astype(x2.dtype), idx)
        shape = x.shape
        D = shape[-1]
        x2 = x.reshape(-1, D)
        weights, indices = _gate(x2, Wg)
        E = Wg.shape[0]
        y = jnp.zeros_like(x2)
        for e in range(E):
            we = jnp.sum(weights * (indices == e), axis=-1)
            h = jax.nn.silu(x2 @ W1[e].T + b1[e]) * (x2 @ W3[e].T + b3[e])
            y = y + (h @ W2[e].T + b2[e]) * we[:, None]
        return y.reshape(shape)
    x = x + jnp.tanh(g_xattn[0]) * _L0_xattn_ref(_layernorm(x, axis=-1), ctx_768, L0_xattn_Wq, L0_xattn_Wk, L0_xattn_Wv, L0_xattn_Wo, L0_xattn_bo)
    x = x + jnp.tanh(g_ffn[0]) * _L0_ffn_ref(_layernorm(x, axis=-1), L0_ffn_moe_router, L0_ffn_moe_w13, L0_ffn_moe_w2)
    x = x + jnp.tanh(g_xattn[1]) * _L1_xattn_ref(ctx_768, _layernorm(x, axis=-1), mask_BxS2_bk0, L1_xattn_ln_x_g, L1_xattn_ln_x_b, L1_xattn_ln_l_g, L1_xattn_ln_l_b, L1_xattn_qn_g, L1_xattn_kn_g, L1_xattn_Wq, L1_xattn_Wkv, L1_xattn_Wlkv, L1_xattn_Wo, L1_xattn_bo)
    x = x + jnp.tanh(g_ffn[1]) * _L1_ffn_ref(_layernorm(x, axis=-1), L1_ffn_Wg, L1_ffn_W1, L1_ffn_b1, L1_ffn_W2, L1_ffn_b2, L1_ffn_W3, L1_ffn_b3)
    return x

_drawn_inputs = setup_inputs


def setup_inputs(seed=0):
    import zlib

    import numpy as np

    out = dict(_drawn_inputs(seed))
    spreads = {'g_ffn': (-1.0, 0.6),
     'L0_xattn_bo': (0.0, 0.1),
     'L1_xattn_ln_x_g': (1.0, 0.2),
     'L1_xattn_ln_x_b': (0.0, 0.1),
     'L1_xattn_ln_l_g': (1.0, 0.2),
     'L1_xattn_ln_l_b': (0.0, 0.1),
     'L1_xattn_qn_g': (1.0, 0.2),
     'L1_xattn_kn_g': (1.0, 0.2),
     'L1_xattn_bo': (0.0, 0.1),
     'L1_ffn_b1': (0.0, 0.8),
     'L1_ffn_b2': (0.0, 0.1),
     'L1_ffn_b3': (0.0, 0.8)}
    factors = {'L0_ffn_moe_router': 4.157,
     'L0_ffn_moe_w13': 3.691,
     'L0_ffn_moe_w2': 3.733,
     'L1_ffn_W1': 3.619,
     'L1_ffn_W2': 3.412,
     'L1_ffn_W3': 3.57}
    for name, (base, spread) in spreads.items():
        noise = np.random.default_rng([zlib.crc32(name.encode()), seed]).standard_normal(out[name].shape)
        drawn = base * np.exp(spread * noise) if base else spread * noise
        out[name] = jnp.asarray(drawn.astype(out[name].dtype))
    for name, factor in factors.items():
        out[name] = (out[name] * factor).astype(out[name].dtype)
    return out
```

```python
from contextlib import ExitStack

import numpy as np

import concourse.bass as bass
from concourse import mybir

F32 = mybir.dt.float32
I32 = mybir.dt.int32
U32 = mybir.dt.uint32
U8 = mybir.dt.uint8
ALU = mybir.AluOpType
ACT = mybir.ActivationFunctionType
AX = mybir.AxisListType.X

B, N, D = 32, 100, 256
S, C = 361, 192
TOKENS = B * N
P = 128
SPARE = P
CH = 121
NCH = 3
SP = CH * NCH
CK = 96
H0, H1, DH = 8, 4, 64
I0, I1 = H0 * DH, H1 * DH
K1 = SP + N
REGION = TOKENS
E0, TOP0, F0 = 8, 2, 512
E1, TOP1, F1 = 16, 4, 256
GROUPS, TOPG = 4, 2
ROUTE_SCALE = 2.5
LN_EPS = 1e-5
RMS_EPS = 1e-8
NEG = -1e30


def most_tiles(experts, top):
    return (TOKENS * top + experts * (P - 1)) // P


class Lane:

    def __init__(self, sem, events, step=1):
        self.sem, self.events, self.step = sem, list(events), step
        self.seen = 0
        assert len(set(self.events)) == len(self.events)

    def post(self, ins, event):
        assert self.events[self.seen % len(self.events)] == event, (self.sem, event, self.seen)
        self.seen += 1
        ins.then_inc(self.sem, self.step)

    def wait(self, eng, rnd, event):
        k = (self.events.index(event) + 1) * self.step
        value = rnd * (len(self.events) * self.step) + k
        if isinstance(value, int) and value <= 0:
            return
        eng.wait_ge(self.sem, value)


def settle(eng, c):
    eng.sem_inc(c["settled"], 1)


def emit(steps, name, eng, base):
    for engine, off, fn in steps:
        if engine == name:
            fn(eng, base + off)


def run_rounds(name, eng, prologue, iteration, epilogue, rounds, unroll, head, tail):
    emit(prologue, name, eng, 0)
    for i in range(head):
        emit(iteration(i, i), name, eng, i)
    assert (rounds - head - tail) % unroll == 0
    bodies = [iteration(None, head + j) for j in range(unroll)]
    if any(e == name for body in bodies for e, _, _ in body):
        with eng.Fori(head, rounds - tail - unroll + 1, unroll) as i:
            for j, body in enumerate(bodies):
                emit(body, name, eng, i + j)
    for i in range(rounds - tail, rounds):
        emit(iteration(i, i), name, eng, i)
    emit(epilogue, name, eng, rounds)


def build(nc, a, out):
    top = ExitStack()
    dram = {}
    for n, e, t in ((0, E0, most_tiles(E0, TOP0)), (1, E1, most_tiles(E1, TOP1))):
        rows = e * REGION + (t + 3) * P
        dram[f"table{n}"] = nc.dram_tensor(f"table{n}", (rows, 2), I32, kind="Internal").ap()
        dram[f"xn{n}"] = nc.dram_tensor(f"xn{n}", (TOKENS + SPARE, D), F32, kind="Internal").ap()
    dram["acc0"] = nc.dram_tensor("acc0", (TOKENS + SPARE, D), F32, kind="Internal").ap()
    dram["acc1"] = out

    def maker(stack):
        def sb(name, shape, dt=F32):
            return stack.enter_context(nc.sbuf_tensor(name, list(shape), dt))

        def ps(name, shape):
            return stack.enter_context(nc.psum_tensor(name, list(shape), F32))

        def lane(name, events, step=1):
            return Lane(stack.enter_context(nc.semaphore(name)), events, step)

        return sb, ps, lane

    with top:
        sb, ps, lane = maker(top)
        c = dict(
            settled=top.enter_context(nc.semaphore("settled")),
            ident=sb("ident", [P, P]), before=sb("before", [N, N]), ones=sb("ones", [N, N]),
            iota=sb("iota", [N, E1]), neghalf=sb("neghalf", [P, 4]),
            gates=sb("gates", [P, 4]), tg=sb("tg", [P, 4]),
            token=sb("token", [N, 1], I32), base=sb("base", [N, E1]),
            expert_w=sb("expert_w", [P, 3 * E0 * 2 * F0]),
            wq0=sb("wq0", [P, 2, I0]), wk0=sb("wk0", [CK, 2, I0]), wv0=sb("wv0", [CK, 2, I0]),
            wo0=sb("wo0", [P, 4, D]), wr0=sb("wr0", [P, 2, E0]), bo0=sb("bo0", [N, D]),
            wq1=sb("wq1", [P, 2, I1]), wkv1=sb("wkv1", [CK, 2, 2 * I1]), wlkv1=sb("wlkv1", [P, 2, 2 * I1]),
            wo1=sb("wo1", [P, 2, D]), wr1=sb("wr1", [P, 2, E1]), bo1=sb("bo1", [N, D]),
            cx_g=sb("cx_g", [CK, 2]), cx_b=sb("cx_b", [CK, 2]), lt_g=sb("lt_g", [P, 2]), lt_b=sb("lt_b", [P, 2]),
            qk_g=sb("qk_g", [P, 2]), qk_s=sb("qk_s", [P, 1]),
            w_ready=lane("w_ready", ["all"], 16), x0_ready=lane("experts0_w", ["w"], 16),
            x1_ready=lane("experts1_w", ["w"], 16),
        )
        setup(nc, maker, a, dram, c)
        attention(nc, maker, a, dram, c, 0)
        experts(nc, maker, a, dram, c, 0)
        attention(nc, maker, a, dram, c, 1)
        experts(nc, maker, a, dram, c, 1)


def load_expert_weights(eng, a, c, n):
    w = c["expert_w"]
    if n == 0:
        w13 = w[:, 0:E0 * 2 * 2 * F0].rearrange("p (e k f) -> p e k f", e=E0, k=2)
        w2 = w[:, E0 * 4 * F0:E0 * 4 * F0 + E0 * 4 * D].rearrange("p (e k d) -> p e k d", e=E0, k=4)
        for e in range(E0):
            eng.dma_start(w13[:, e], a["L0_ffn_moe_w13"][e].rearrange("(k p) f -> p k f", p=P)).then_inc(c["x0_ready"].sem, 16)
            eng.dma_start(w2[:, e], a["L0_ffn_moe_w2"][e].rearrange("(k p) d -> p k d", p=P)).then_inc(c["x0_ready"].sem, 16)
        return 2 * E0
    w13 = w[:, 0:E1 * 2 * 2 * F1].rearrange("p (e k f) -> p e k f", e=E1, k=2)
    w2 = w[:, E1 * 4 * F1:E1 * 4 * F1 + E1 * 2 * D].rearrange("p (e k d) -> p e k d", e=E1, k=2)
    for e in range(E1):
        eng.dma_start(w13[:, e, :, 0:F1], a["L1_ffn_W1T"][e].rearrange("(k p) f -> p k f", p=P)).then_inc(c["x1_ready"].sem, 16)
        eng.dma_start(w13[:, e, :, F1:2 * F1], a["L1_ffn_W3T"][e].rearrange("(k p) f -> p k f", p=P)).then_inc(c["x1_ready"].sem, 16)
        eng.dma_start(w2[:, e], a["L1_ffn_W2T"][e].rearrange("(k p) d -> p k d", p=P)).then_inc(c["x1_ready"].sem, 16)
    return 3 * E1


def setup(nc, maker, a, dram, c):
    stack = ExitStack()
    with stack:
        sb, ps, lane = maker(stack)
        empty = sb("empty_slots", [P, P, 2], I32)
        zero = sb("zero_rows", [P, D])
        pool = lane("setup_pool", ["z0", "z1", "z2", "ident", "before", "i"])
        dve = lane("setup_dve", ["c0", "c1", "g"])
        act = lane("setup_act", ["tg"])
        st = lane("setup_stores", ["s"], 16)
        w_ready = c["w_ready"]
        with nc.Block() as block:

            @block.gpsimd
            def _(g):
                pool.post(g.memset(c["ident"][:, :], 0.0), "z0")
                pool.post(g.memset(empty[:, :, :], 0), "z1")
                g.memset(zero[:, :], 0.0)
                pool.post(g.memset(c["ones"][:, :], 1.0), "z2")
                pool.wait(g, 0, "z2")
                pool.post(g.affine_select(out=c["ident"][:, :], in_=c["ident"][:, :], compare_op=ALU.not_equal, fill=1.0,
                                          base=0, pattern=[[-1, P]], channel_multiplier=1), "ident")
                pool.post(g.affine_select(out=c["before"][:, :], in_=c["ones"][:, :], compare_op=ALU.is_gt, fill=0.0,
                                          base=0, pattern=[[1, N]], channel_multiplier=-1), "before")
                g.iota(c["iota"][:, :], [[1, E1]], base=0, channel_multiplier=0, allow_small_or_imprecise_dtypes=True)
                g.iota(c["token"][:, :], [[1, 1]], base=0, channel_multiplier=1)
                pool.post(g.iota(empty[:, :, 0], [[1, P]], base=TOKENS, channel_multiplier=0), "i")

            @block.sync
            def _(s):
                def w(dst, src):
                    s.dma_start(dst, src).then_inc(w_ready.sem, 16)
                    w.n += 1
                w.n = 0
                with nc.allow_non_contiguous_dma(reason="a few per-partition constants"):
                    w(c["gates"][:, 0:2], a["g_xattn"].partition_broadcast(P))
                    w(c["gates"][:, 2:4], a["g_ffn"].partition_broadcast(P))
                    w(c["cx_g"][:, :], a["L1_xattn_ln_x_g"].rearrange("(k p) -> p k", p=CK))
                    w(c["cx_b"][:, :], a["L1_xattn_ln_x_b"].rearrange("(k p) -> p k", p=CK))
                    w(c["lt_g"][:, :], a["L1_xattn_ln_l_g"].rearrange("(k p) -> p k", p=P))
                    w(c["lt_b"][:, :], a["L1_xattn_ln_l_b"].rearrange("(k p) -> p k", p=P))
                    for half in range(2):
                        for j, n in enumerate(("q", "k")):
                            w(c["qk_g"][half * DH:(half + 1) * DH, j:j + 1],
                              a[f"L1_xattn_{n}n_g"].rearrange("(p k) -> p k", k=1))
                for n, src, p in (("wq0", "L0_xattn_Wq", P), ("wk0", "L0_xattn_Wk", CK), ("wv0", "L0_xattn_Wv", CK),
                                  ("wo0", "L0_xattn_Wo", P), ("wr0", "L0_ffn_moe_router", P),
                                  ("wq1", "L1_xattn_WqT", P), ("wkv1", "L1_xattn_WkvT", CK), ("wlkv1", "L1_xattn_WlkvT", P),
                                  ("wo1", "L1_xattn_WoT", P), ("wr1", "L1_ffn_WgT", P)):
                    w(c[n][:, :, :], a[src].rearrange("(k p) n -> p k n", p=p))
                w(c["bo0"][:, :], a["L0_xattn_bo"].partition_broadcast(N))
                w(c["bo1"][:, :], a["L1_xattn_bo"].partition_broadcast(N))
                c["w_loads"] = w.n
                s.wait_ge(w_ready.sem, 16 * w.n)

            @block.vector
            def _(v):
                dve.post(v.memset(c["neghalf"][:, :], -0.5), "c0")
                v.wait_ge(w_ready.sem, 16 * c["w_loads"])
                dve.post(v.tensor_tensor(c["qk_s"][:, :], c["qk_g"][:, 0:1], c["qk_g"][:, 1:2], ALU.mult), "c1")
                dve.wait(v, 0, "c1")
                v.tensor_scalar(c["qk_s"][:, :], c["qk_s"][:, :], DH ** -0.5, None, ALU.mult)
                act.wait(v, 0, "tg")
                v.tensor_scalar(c["bo0"][:, :], c["bo0"][:, :], c["tg"][0:N, 0:1], None, ALU.mult)
                dve.post(v.tensor_scalar(c["bo1"][:, :], c["bo1"][:, :], c["tg"][0:N, 1:2], None, ALU.mult), "g")

            @block.scalar
            def _(s):
                pool.wait(s, 0, "i")
                for n in range(2):
                    t = dram[f"table{n}"]
                    blocks = t.shape[0] // P
                    full = t.rearrange("(b r) c -> b (r c)", r=P)
                    for at in range(0, blocks, P):
                        m = min(P, blocks - at)
                        s.dma_start(full[at:at + m], empty[0:m].rearrange("p r c -> p (r c)")).then_inc(st.sem, 16)
                        st.seen += 1
                    s.dma_start(dram[f"xn{n}"][TOKENS:TOKENS + SPARE], zero[:, :]).then_inc(st.sem, 16)
                    s.dma_start(dram[f"acc{n}"][TOKENS:TOKENS + SPARE], zero[:, :]).then_inc(st.sem, 16)
                    st.seen += 2
                s.wait_ge(w_ready.sem, 16 * c["w_loads"])
                act.post(s.activation(c["tg"][:, :], c["gates"][:, :], ACT.Tanh), "tg")
                s.wait_ge(st.sem, 16 * st.seen)


def attention(nc, maker, a, dram, c, layer):
    L0 = layer == 0
    heads = H0 if L0 else H1
    pairs = heads // 2
    keys = SP if L0 else K1
    chunks = [CH] * NCH if L0 else [CH] * NCH + [N]
    experts_n, topk = (E0, TOP0) if L0 else (E1, TOP1)
    tg_x, tg_f = c["tg"][0:N, layer:layer + 1], c["tg"][0:N, 2 + layer:3 + layer]
    wo, wr, bo = c[f"wo{layer}"], c[f"wr{layer}"], c[f"bo{layer}"]
    table, acc, xn_rows = dram[f"table{layer}"], dram[f"acc{layer}"], dram[f"xn{layer}"]
    ident, neghalf = c["ident"], c["neghalf"]
    L = str(layer)

    stack = ExitStack()
    with stack:
        sb, ps, lane = maker(stack)
        psS = ps("psS" + L, [P, 2, 512])
        psT = ps("psT" + L, [P, 2, 512])
        psO = ps("psO" + L, [P, 512])
        psJ = ps("psJ" + L, [P, 2, 512])
        psY = ps("psY" + L, [P, 512])

        x = sb("x" + L, [N, 2, D])
        xb = sb("xb" + L, [N, 2, D])
        st = sb("st" + L, [N, 6])
        mv = sb("mv" + L, [N, 2])
        rstd = sb("rstd" + L, [N, 2])
        xn = sb("xn_a" + L, [N, 2, D])
        xT = sb("xT" + L, [P, 2, N])
        qz = sb("qz" + L, [P, 2, heads, N])
        kT = sb("kT" + L, [P, 2, pairs, keys])
        vv = sb("vv" + L, [CH, 2, len(chunks), heads * DH])
        prob = sb("prob" + L, [N, 4, keys])
        nm = sb("nm" + L, [N, 4])
        rs = sb("rs" + L, [N, 4])
        rc = sb("rc" + L, [N, 4])
        pT = sb("pT" + L, [CH, 2, len(chunks), 2 * N])
        oT = sb("oT" + L, [P, pairs, N])
        x1 = sb("x1" + L, [N, 2, D])
        xm = sb("xm" + L, [N, 2, D])
        st1 = sb("st1" + L, [N, 6])
        mv1 = sb("mv1" + L, [N, 2])
        rstd1 = sb("rstd1" + L, [N, 2])
        xmT = sb("xmT" + L, [P, 2, N])
        sc = sb("sc" + L, [N, 3, E1])
        top_v = sb("top_v" + L, [N, 8])
        top_i = sb("top_i" + L, [N, 8], U32)
        top_f = sb("top_f" + L, [N, TOP1])
        hot = sb("hot" + L, [N, TOP1, E1])
        hit = sb("hit" + L, [N, TOP1, E1])
        chosen = sb("chosen" + L, [N, E1])
        slot_of = sb("slot_of" + L, [N, E1])
        pos_f = sb("pos_f" + L, [N, TOP1])
        tmp = sb("tmp" + L, [N, 8])
        pos = sb("pos" + L, [N, 2, TOP1], U32)
        slot = sb("slot" + L, [N, 2, TOP1, 2], I32)
        slot_w = slot[:, :, :, 1].bitcast(F32)
        if L0:
            cT = sb("cT" + L, [CK, 2, 2, SP])
        else:
            xl = sb("xl", [N, D])
            lT = xT
            ctx = sb("ctx", [CH, 2, NCH, C])
            cst = sb("cst", [CH, NCH, 6])
            cmv = sb("cmv", [CH, NCH, 2])
            crs = sb("crs", [CH, 2, NCH])
            cn = sb("cn", [CH, 2, NCH, C])
            cTn = sb("cTn", [CK, 2, SP])
            sq = sb("sq", [CH, 2, I1])
            ss = sb("ss", [CH, 5, H1])
            rk = sb("rk", [CH, 5, H1])
            kn = sb("kn", [CH, 2, I1])
            m8 = sb("m8", [N, 2, S], U8)
            mb = sb("mb", [N, 2, K1])
            gmax = sb("gmax", [N, 8])
            gtop = sb("gtop", [N, 8])
            gidx = sb("gidx", [N, 8], U32)
            gidf = sb("gidf", [N, TOPG])
            ghot = sb("ghot", [N, TOPG, GROUPS])
            gok = sb("gok", [N, GROUPS])

        ld_x = lane("ld_x" + L, ["x"], 16)
        ld_c = lane("ld_c" + L, ["c"] if L0 else ["c0", "c1", "m"], 16)
        st_x = lane("st_x" + L, ["x1", "xm"], 16)
        st_s = lane("st_s" + L, ["k%d" % k for k in range(topk)], 16)
        init = lane("init" + L, ["i"])
        evac_v = "act"
        if L0:
            uses = ["k0", "k1", "k2", "k3", "v0", "v1", "v2", "xt", "q"]
            owner = dict(k0="act", k1="act", k2="act", k3="act", v0="dve", v1="dve", v2="dve", xt="act", q="dve")
            P_dve = lane("P_dve" + L, ["stat", "mv", "xn", "v0", "v1", "v2", "q"])
            P_act = lane("P_act" + L, ["k0", "k1", "k2", "k3", "xt"])
            P_pool = lane("P_pool" + L, ["ve", "rstd", "xb"])
            P_pe = lane("P_pe" + L, uses)
        else:
            uses = ["lt", "ct0", "ct1", "q", "kv0", "qt", "kv1", "kt0", "kv2", "kt1", "kv3", "kt2", "kt3"]
            owner = {u: "dve" for u in uses} | dict(lt="act", ct0="act", ct1="act")
            P_dve = lane("P_dve" + L, [
                "stat", "mv", "xn", "stat2", "mv2", "xl", "cstat", "cmv", "cn",
                "ssq", "q", "ss0", "kv0", "qt", "ss1", "kv1", "kt0", "ss2", "kv2", "kt1", "ss3", "kv3", "kt2", "kt3"])
            P_act = lane("P_act" + L, ["lt", "ct0", "ct1", "sqq", "sq0", "v0", "sq1", "v1", "sq2", "v2", "sq3", "v3"])
            P_pool = lane("P_pool" + L, ["ve", "rstd", "ve2", "rstd2", "cve", "crs", "mb", "xb"] +
                          [f"{w}{j}" for j in "q0123" for w in ("ms", "rk")])
            P_pe = lane("P_pe" + L, uses)
        X_pe = lane("X_pe" + L, sum([[f"s{2 * p}", f"s{2 * p + 1}"] + ([f"o{p - 1}"] if p else []) +
                                     [f"t{2 * p}", f"t{2 * p + 1}"] for p in range(pairs)], []) + [f"o{pairs - 1}"])
        if L0:
            X_dve = lane("X_dve" + L, sum([[f"m{p}", f"r{p}", f"t{2 * p}", f"t{2 * p + 1}"] for p in range(pairs)], []))
        else:
            X_dve = lane("X_dve" + L, sum([[f"a{2 * p}", f"a{2 * p + 1}", f"m{p}", f"r{p}", f"t{2 * p}", f"t{2 * p + 1}"]
                                           for p in range(pairs)], []))
        X_act = lane("X_act" + L, sum([[f"e{2 * p}", f"e{2 * p + 1}"] + ([f"o{p - 1}"] if p else []) +
                                       ([f"t{2 * p}", f"t{2 * p + 1}"] if not L0 else [])
                                       for p in range(pairs)], []) + [f"o{pairs - 1}"])
        X_pool = lane("X_pool" + L, [f"n{h}" for h in range(heads)])
        Y_pe = lane("Y_pe" + L, ["wo", "xt", "lg", "rk"])
        router = (["lg", "top", "idx", "idf", "hot", "cho", "d", "w0", "w1", "w2", "w3"] if L0 else
                  ["s0", "s1", "gm", "gt", "gi", "gf", "gh", "go", "gk", "msk", "top", "idx", "idf", "hot", "cho",
                   "sum", "rcp", "w2", "w3"])
        Y_dve = lane("Y_dve" + L, ["x1", "stat", "mv", "xm"] + router + ["tok", "slot", "hit", "pos", "posi"])
        Y_act = lane("Y_act" + L, ["xt", "e"])
        Y_pool = lane("Y_pool" + L, ["ve", "rstd"])

        def bank(par, use):
            j = uses.index(use)
            before = (uses[j - 2], 0) if j >= 2 else (uses[j - 2 + len(uses)], 1)
            return psJ[:, (par * len(uses) + j) % 2, :], before

        def free_bank(eng, b, par, use):
            prev, back = bank(par, use)[1]
            (P_act if owner[prev] == "act" else P_dve).wait(eng, b - back, prev)
            if prev.startswith("kv"):
                P_act.wait(eng, b - back, "v" + prev[2:])

        def layer_norm(add, src, dst, stt, mvt, rst, dve, pool, names, ready, free=None):
            stat, mvn, ve, rn, done = names

            def d1(v, b):
                ready(v, b)
                dve.post(v.bn_stats(stt[:, :], src), stat)
                dve.wait(v, b, stat)
                settle(v, c)
                dve.post(v.bn_aggr(mvt[:, :], stt[:, :]), mvn)

            def g1(g, b):
                dve.wait(g, b, mvn)
                settle(g, c)
                pool.post(g.tensor_scalar(rst[:, 0:1], mvt[:, 1:2], LN_EPS, 1.0, ALU.add, ALU.mult), ve)
                pool.wait(g, b, ve)
                pool.post(g.tensor_tensor(rst[:, 1:2], rst[:, 0:1], neghalf[0:N, 0:1], ALU.pow), rn)

            def d2(v, b):
                pool.wait(v, b, rn)
                if free:
                    free(v, b)
                dve.post(v.tensor_scalar(dst, src, mvt[:, 0:1], rst[:, 1:2], ALU.subtract, ALU.mult), done)

            add("dve", d1), add("pool", g1), add("dve", d2)

        def p_bias(steps, off, par):
            def g0(g, b):
                ld_x.wait(g, b, "x")
                Y_dve.wait(g, b - 2, "x1")
                P_pool.post(g.tensor_tensor(xb[:, par, :], x[:, par, :], bo[:, :], ALU.add), "xb")
            steps.append(("pool", off, g0))

        def p_norm0(steps, off, par):
            def add(e, fn):
                steps.append((e, off, fn))

            layer_norm(add, x[:, par, :], xn[:, par, :], st, mv, rstd, P_dve, P_pool,
                       ("stat", "mv", "ve", "rstd", "xn"), lambda v, b: ld_x.wait(v, b, "x"))

        def p_k0(steps, off, par, m):
            use = f"k{m}"
            ph = bank(par, use)[0]

            def pe(t, b):
                ld_c.wait(t, b, "c")
                free_bank(t, b, par, use)
                for k in range(2):
                    mm = t.matmul(ph[:, 0:SP], c["wk0"][:, k, m * P:(m + 1) * P], cT[:, par, k, :], start=k == 0, stop=k == 1)
                P_pe.post(mm, use)

            def ac(s, b):
                P_pe.wait(s, b, use)
                P_act.post(s.activation(kT[:, par, m, :], ph[:, 0:SP], ACT.Copy), use)
            steps += [("pe", off, pe), ("act", off, ac)]

        def p_v0(steps, off, par, ch):
            use = f"v{ch}"
            ph = bank(par, use)[0]

            def pe(t, b):
                free_bank(t, b, par, use)
                for k in range(2):
                    mm = t.matmul(ph[0:CH, :], cT[:, par, k, ch * CH:(ch + 1) * CH], c["wv0"][:, k, :], start=k == 0, stop=k == 1)
                P_pe.post(mm, use)

            def dv(v, b):
                P_pe.wait(v, b, use)
                P_dve.post(v.tensor_copy(vv[:, par, ch, :], ph[0:CH, :]), use)
            steps += [("pe", off, pe), ("dve", off, dv)]

        def p_q0(steps, off, par):
            ph, pq = bank(par, "xt")[0], bank(par, "q")[0]

            def pe1(t, b):
                P_dve.wait(t, b, "xn")
                free_bank(t, b, par, "xt")
                for k in range(2):
                    mm = t.transpose(ph[:, k * N:(k + 1) * N], xn[:, par, k * P:(k + 1) * P], ident[0:N, 0:N])
                P_pe.post(mm, "xt")

            def ac(s, b):
                P_pe.wait(s, b, "xt")
                P_act.post(s.activation(xT[:, :, :], ph[:, 0:2 * N].rearrange("p (k n) -> p k n", k=2), ACT.Copy), "xt")

            def pe2(t, b):
                P_act.wait(t, b, "xt")
                free_bank(t, b, par, "q")
                for m in range(pairs):
                    for k in range(2):
                        mm = t.matmul(pq[:, m * N:(m + 1) * N], c["wq0"][:, k, m * P:(m + 1) * P], xT[:, k, :],
                                      start=k == 0, stop=k == 1)
                P_pe.post(mm, "q")

            def dv(v, b):
                P_pe.wait(v, b, "q")
                for half in range(2):
                    r = slice(half * DH, (half + 1) * DH)
                    ins = v.tensor_scalar(qz[r, par, half:heads:2, :], pq[r, 0:pairs * N].rearrange("p (m n) -> p m n", m=pairs),
                                          DH ** -0.5, None, ALU.mult)
                P_dve.post(ins, "q")
            steps += [("pe", off, pe1), ("act", off, ac), ("pe", off, pe2), ("dve", off, dv)]

        def p_norm1(steps, off, par):
            def add(e, fn):
                steps.append((e, off, fn))

            layer_norm(add, x[:, par, :], xn[:, par, :], st, mv, rstd, P_dve, P_pool,
                       ("stat", "mv", "ve", "rstd", "xn"), lambda v, b: ld_x.wait(v, b, "x"))
            layer_norm(add, xn[:, par, :], xl[:, :], st, mv, rstd, P_dve, P_pool,
                       ("stat2", "mv2", "ve2", "rstd2", "xl"), lambda v, b: P_dve.wait(v, b, "xn"),
                       lambda v, b: P_pe.wait(v, b - 1, "lt"))

            def d1(v, b):
                ld_c.wait(v, b, "m")
                for j in range(NCH):
                    ins = v.bn_stats(cst[:, j, :], ctx[:, par, j, :])
                P_dve.post(ins, "cstat")
                P_dve.wait(v, b, "cstat")
                settle(v, c)
                for j in range(NCH):
                    ins = v.bn_aggr(cmv[:, j, :], cst[:, j, :])
                P_dve.post(ins, "cmv")

            def g1(g, b):
                P_dve.wait(g, b, "cmv")
                settle(g, c)
                P_pool.post(g.tensor_scalar(crs[:, 0, :], cmv[:, :, 1], LN_EPS, 1.0, ALU.add, ALU.mult), "cve")
                P_pool.wait(g, b, "cve")
                P_pool.post(g.tensor_tensor(crs[:, 1, :], crs[:, 0, :], neghalf[0:CH, 0:NCH], ALU.pow), "crs")
                X_dve.wait(g, b - 2, f"a{heads - 1}")
                settle(g, c)
                P_pool.post(g.tensor_scalar(mb[:, par, 0:S], m8[:, par, :], -NEG, NEG, ALU.mult, ALU.add), "mb")

            def d2(v, b):
                P_pool.wait(v, b, "crs")
                P_pe.wait(v, b - 2, "ct1")
                for j in range(NCH):
                    ins = v.tensor_scalar(cn[:, par, j, :], ctx[:, par, j, :], cmv[:, j, 0:1], crs[:, 1, j:j + 1],
                                          ALU.subtract, ALU.mult)
                P_dve.post(ins, "cn")
            add("dve", d1), add("pool", g1), add("dve", d2)

        def p_t1(steps, off, par):
            def pe(t, b):
                P_dve.wait(t, b, "xl")
                free_bank(t, b, par, "lt")
                ph = bank(par, "lt")[0]
                for k in range(2):
                    mm = t.transpose(ph[:, k * N:(k + 1) * N], xl[:, k * P:(k + 1) * P], ident[0:N, 0:N])
                P_pe.post(mm, "lt")

            def ac(s, b):
                P_pe.wait(s, b, "lt")
                ph = bank(par, "lt")[0]
                for k in range(2):
                    ins = s.activation(lT[:, k, :], ph[:, k * N:(k + 1) * N], ACT.Identity,
                                       bias=c["lt_b"][:, k:k + 1], scale=c["lt_g"][:, k:k + 1])
                P_act.post(ins, "lt")
            steps += [("pe", off, pe), ("act", off, ac)]
            for k in range(2):
                def pe(t, b, k=k):
                    P_dve.wait(t, b, "cn")
                    free_bank(t, b, par, f"ct{k}")
                    ph = bank(par, f"ct{k}")[0]
                    for j in range(NCH):
                        mm = t.transpose(ph[0:CK, j * CH:(j + 1) * CH], cn[:, par, j, k * CK:(k + 1) * CK], ident[0:CH, 0:CH])
                    P_pe.post(mm, f"ct{k}")

                def ac(s, b, k=k):
                    P_pe.wait(s, b, f"ct{k}")
                    ph = bank(par, f"ct{k}")[0]
                    P_act.post(s.activation(cTn[:, k, :], ph[0:CK, 0:SP], ACT.Identity,
                                            bias=c["cx_b"][:, k:k + 1], scale=c["cx_g"][:, k:k + 1]), f"ct{k}")
                steps += [("pe", off, pe), ("act", off, ac)]

        def p_qkv1(steps, off, par, j):
            use = "q" if j == "q" else f"kv{j}"
            ph = bank(par, use)[0]
            rows = N if j in ("q", 3) else CH
            row = 4 if j == "q" else j
            nbuf = 0 if j == "q" else (j + 1) % 2

            def pe(t, b):
                free_bank(t, b, par, use)
                P_act.wait(t, b, "lt" if j in ("q", 3) else "ct1")
                for k in range(2):
                    if j == "q":
                        mm = t.matmul(ph[0:rows, 0:I1], lT[:, k, :], c["wq1"][:, k, :], start=k == 0, stop=k == 1)
                    elif j == 3:
                        mm = t.matmul(ph[0:rows, :], lT[:, k, :], c["wlkv1"][:, k, :], start=k == 0, stop=k == 1)
                    else:
                        mm = t.matmul(ph[0:rows, :], cTn[:, k, j * CH:(j + 1) * CH], c["wkv1"][:, k, :], start=k == 0, stop=k == 1)
                P_pe.post(mm, use)

            def ac(s, b):
                P_pe.wait(s, b, use)
                if j in (1, 2, 3):
                    P_dve.wait(s, b, {1: "ssq", 2: "ss0", 3: "ss1"}[j])
                P_act.post(s.activation(sq[0:rows, nbuf, :], ph[0:rows, 0:I1], ACT.Square), f"sq{j}")
                if j != "q":
                    P_act.post(s.activation(vv[0:rows, par, j, :], ph[0:rows, I1:2 * I1], ACT.Copy), f"v{j}")

            def d1(v, b):
                P_act.wait(v, b, f"sq{j}")
                P_dve.post(v.tensor_reduce(ss[0:rows, row, :], sq[0:rows, nbuf, :].rearrange("p (h d) -> p h d", h=H1),
                                           AX, ALU.add), f"ss{j}")

            def g1(g, b):
                P_dve.wait(g, b, f"ss{j}")
                settle(g, c)
                P_pool.post(g.tensor_scalar(rk[0:rows, row, :], ss[0:rows, row, :], 1.0 / DH, RMS_EPS ** 2,
                                            ALU.mult, ALU.max), f"ms{j}")
                P_pool.wait(g, b, f"ms{j}")
                P_pool.post(g.tensor_tensor(rk[0:rows, row, :], rk[0:rows, row, :], neghalf[0:rows, 0:H1], ALU.pow), f"rk{j}")

            def d2(v, b):
                P_pool.wait(v, b, f"rk{j}")
                if j != "q":
                    P_act.wait(v, b, f"v{j}")
                P_pe.wait(v, b if j != "q" and j >= 1 else b - 1, {"q": "kt3", 0: "kt2", 1: "qt", 2: "kt0", 3: "kt1"}[j])
                scale = rk[0:rows, row, :].unsqueeze(2).to_broadcast([rows, H1, DH])
                P_dve.post(v.tensor_tensor(kn[0:rows, nbuf, :].rearrange("p (h d) -> p h d", h=H1),
                                           ph[0:rows, 0:I1].rearrange("p (h d) -> p h d", h=H1), scale, ALU.mult), use)
            steps += [("pe", off, pe), ("act", off, ac), ("dve", off, d1), ("pool", off, g1), ("dve", off, d2)]

        def p_qkt1(steps, off, par, j):
            use = "qt" if j == "q" else f"kt{j}"
            ph = bank(par, use)[0]
            rows = N if j in ("q", 3) else CH
            nbuf = 0 if j == "q" else (j + 1) % 2

            def pe(t, b):
                P_dve.wait(t, b, "q" if j == "q" else f"kv{j}")
                free_bank(t, b, par, use)
                for k in range(2):
                    mm = t.transpose(ph[:, k * rows:(k + 1) * rows], kn[0:rows, nbuf, k * P:(k + 1) * P], ident[0:rows, 0:rows])
                P_pe.post(mm, use)

            def dv(v, b):
                P_pe.wait(v, b, use)
                src = ph[:, 0:2 * rows].rearrange("p (k n) -> p k n", k=2)
                if j == "q":
                    for half in range(2):
                        r = slice(half * DH, (half + 1) * DH)
                        ins = v.tensor_scalar(qz[r, par, half:heads:2, :], src[r], c["qk_s"][r, 0:1], None, ALU.mult)
                else:
                    ins = v.tensor_copy(kT[:, par, :, j * CH:j * CH + rows], src)
                P_dve.post(ins, use)
            steps += [("pe", off, pe), ("dve", off, dv)]

        def x_scores(steps, off, par, p):
            def pe(t, b, h):
                if p == 0 and h == 0:
                    if L0:
                        P_dve.wait(t, b, "q")
                    else:
                        P_dve.wait(t, b, "kt3")
                if L0:
                    P_act.wait(t, b, f"k{p}")
                hh = 2 * p + h
                if L0:
                    X_act.wait(t, b if p else b - 1, f"e{(hh - 2) % heads}")
                else:
                    X_dve.wait(t, b if p else b - 1, f"a{(hh - 2) % heads}")
                X_pe.post(t.matmul(psS[0:N, h, 0:keys], qz[:, par, hh, :], kT[:, par, p, :], start=True, stop=True), f"s{hh}")
            q2 = (2 * p) % 4

            def dv(v, b):
                if L0:
                    X_pe.wait(v, b, f"s{2 * p + 1}")
                    X_dve.post(v.tensor_reduce(nm[:, q2:q2 + 2], psS[0:N, :, 0:S], AX, ALU.max, negate=True), f"m{p}")
                    return
                if p == 0:
                    P_pool.wait(v, b, "mb")
                for h in range(2):
                    hh = 2 * p + h
                    X_pe.wait(v, b, f"s{hh}")
                    settle(v, c)
                    X_dve.post(v.tensor_tensor_reduce(prob[:, hh, :], psS[0:N, h, 0:keys], mb[:, par, :], 1.0, -3e38,
                                                      ALU.add, ALU.max, nm[:, hh:hh + 1]), f"a{hh}")
                X_dve.wait(v, b, f"a{2 * p + 1}")
                X_dve.post(v.tensor_scalar(nm[:, q2:q2 + 2], nm[:, q2:q2 + 2], -1.0, None, ALU.mult), f"m{p}")

            def ac(s, b, h):
                hh = 2 * p + h
                q = hh % 4
                X_dve.wait(s, b, f"m{p}")
                if L0:
                    X_pe.wait(s, b if hh >= 4 else b - 1, f"t{(hh - 4) % heads}")
                    src, dst = psS[0:N, h, 0:S], prob[:, q, 0:S]
                else:
                    src = dst = prob[:, q, :]
                X_act.post(s.activation(dst, src, ACT.Exp, bias=nm[:, q:q + 1], accum_out=rs[:, q:q + 1]), f"e{hh}")
            for h in range(2):
                steps.append(("pe", off, lambda t, b, h=h: pe(t, b, h)))
            steps.append(("dve", off, dv))
            for h in range(2):
                steps.append(("act", off, lambda s, b, h=h: ac(s, b, h)))

        def x_norm(steps, off, par, p):
            q2 = (2 * p) % 4

            def dv(v, b):
                X_act.wait(v, b, f"e{2 * p + 1}")
                X_dve.post(v.reciprocal(rc[:, q2:q2 + 2], rs[:, q2:q2 + 2]), f"r{p}")

            def po(g, b):
                X_dve.wait(g, b, f"r{p}")
                settle(g, c)
                for h in range(2):
                    q = q2 + h
                    X_pool.post(g.tensor_scalar(prob[:, q, :], prob[:, q, :], rc[:, q:q + 1], 1.0, ALU.mult, ALU.mult),
                                f"n{2 * p + h}")
            steps += [("dve", off, dv), ("pool", off, po)]

        def x_transpose(steps, off, par, p):
            for h in range(2):
                hh = 2 * p + h
                q = hh % 4

                def pe(t, b, h=h, hh=hh, q=q):
                    X_pool.wait(t, b, f"n{hh}")
                    X_dve.wait(t, b if p else b - 1, f"t{(hh - 2) % heads}")
                    if not L0:
                        X_act.wait(t, b if p else b - 1, f"t{(hh - 2) % heads}")
                    for j, rows in enumerate(chunks):
                        mm = t.transpose(psT[0:rows, h, j * N:(j + 1) * N], prob[:, q, j * CH:j * CH + rows], ident[0:N, 0:N])
                    X_pe.post(mm, f"t{hh}")

                def dv(v, b, h=h, hh=hh):
                    X_pe.wait(v, b, f"t{hh}")
                    X_dve.post(v.tensor_copy(pT[:, p % 2, 0:NCH, h * N:(h + 1) * N],
                                             psT[0:CH, h, 0:NCH * N].rearrange("p (j n) -> p j n", j=NCH)), f"t{hh}")

                def ac(s, b, h=h, hh=hh):
                    X_dve.wait(s, b, f"t{hh}")
                    X_act.post(s.activation(pT[0:N, p % 2, NCH, h * N:(h + 1) * N], psT[0:N, h, NCH * N:(NCH + 1) * N],
                                            ACT.Copy), f"t{hh}")
                steps += [("pe", off, pe), ("dve", off, dv)] + ([] if L0 else [("act", off, ac)])

        def x_values(steps, off, par, p):
            def pe(t, b):
                X_dve.wait(t, b, f"t{2 * p + 1}")
                if not L0:
                    X_act.wait(t, b, f"t{2 * p + 1}")
                if p == 0:
                    if L0:
                        P_dve.wait(t, b, "v2")
                    else:
                        P_act.wait(t, b, "v3")
                X_act.wait(t, b if p else b - 1, f"o{(p - 1) % pairs}")
                for j, rows in enumerate(chunks):
                    mm = t.matmul(psO[:, 0:2 * N], vv[0:rows, par, j, p * P:(p + 1) * P], pT[0:rows, p % 2, j, :],
                                  start=j == 0, stop=j == len(chunks) - 1)
                X_pe.post(mm, f"o{p}")

            def ac(s, b):
                X_pe.wait(s, b, f"o{p}")
                for half in range(2):
                    r = slice(half * DH, (half + 1) * DH)
                    ins = s.activation(oT[r, p, :], psO[r, half * N:(half + 1) * N], ACT.Copy)
                X_act.post(ins, f"o{p}")
            steps += [("pe", off, pe), ("act", off, ac)]

        def y_out(steps, off, par):
            def pe(t, b):
                X_act.wait(t, b, f"o{pairs - 1}")
                Y_dve.wait(t, b - 1, "slot")
                for p in range(pairs):
                    mm = t.matmul(psY[0:N, 0:D], oT[:, p, :], wo[:, p, :], start=p == 0, stop=p == pairs - 1)
                Y_pe.post(mm, "wo")

            def dv(v, b):
                Y_pe.wait(v, b, "wo")
                P_pool.wait(v, b, "xb")
                st_x.wait(v, b - 2, "xm")
                Y_dve.post(v.scalar_tensor_tensor(x1[:, par, :], psY[0:N, 0:D], tg_x, xb[:, par, :], ALU.mult, ALU.add), "x1")

            steps += [("pe", off, pe), ("dve", off, dv)]
            layer_norm(lambda e, fn: steps.append((e, off, fn)), x1[:, par, :], xm[:, par, :], st1, mv1, rstd1, Y_dve, Y_pool,
                       ("stat", "mv", "ve", "rstd", "xm"), lambda v, b: Y_dve.wait(v, b, "x1"))

            def store(s, b):
                st_x.wait(s, b - 1, "xm")
                Y_dve.wait(s, b, "x1")
                s.dma_start(acc[0:TOKENS].rearrange("(b n) d -> b n d", n=N)[b], x1[:, par, :]).then_inc(st_x.sem, 16)
                Y_dve.wait(s, b, "xm")
                s.dma_start(xn_rows[0:TOKENS].rearrange("(b n) d -> b n d", n=N)[b], xm[:, par, :]).then_inc(st_x.sem, 16)
            steps.append(("act", off, store))

        def y_transpose(steps, off, par):
            def pe(t, b):
                Y_dve.wait(t, b, "xm")
                for k in range(2):
                    mm = t.transpose(psY[:, k * N:(k + 1) * N], xm[:, par, k * P:(k + 1) * P], ident[0:N, 0:N])
                Y_pe.post(mm, "xt")

            def ac(s, b):
                Y_pe.wait(s, b, "xt")
                Y_act.post(s.activation(xmT[:, :, :], psY[:, 0:2 * N].rearrange("p (k n) -> p k n", k=2), ACT.Copy), "xt")
            steps += [("pe", off, pe), ("act", off, ac)]

        def y_route(steps, off, par):
            def pe(t, b):
                Y_act.wait(t, b, "xt")
                for k in range(2):
                    mm = t.matmul(psY[0:N, 0:experts_n], xmT[:, k, :], wr[:, k, :], start=k == 0, stop=k == 1)
                Y_pe.post(mm, "lg")

            def seq(v, b, ins, name):
                Y_dve.post(ins, name)
                Y_dve.wait(v, b, name)
                if name in ("lg", "top", "gm", "gt", "msk"):
                    settle(v, c)

            def one_hot(v, b, dst, idx_f, n, m, name):
                seq(v, b, v.tensor_tensor(dst, c["iota"][:, 0:m].unsqueeze(1).to_broadcast([N, n, m]),
                                          idx_f.unsqueeze(2).to_broadcast([N, n, m]), ALU.is_equal), name)

            w = slot_w[:, par, 0:topk]
            values = sc[:, 0, 0:experts_n]

            def pick(v, b, src):
                seq(v, b, v.max(top_v[:, :], src), "top")
                seq(v, b, v.max_index(top_i[:, :], top_v[:, :], src), "idx")
                seq(v, b, v.tensor_copy(top_f[:, 0:topk], top_i[:, 0:topk]), "idf")
                one_hot(v, b, hot[:, 0:topk, 0:experts_n], top_f[:, 0:topk], topk, experts_n, "hot")
                seq(v, b, v.tensor_reduce(chosen[:, 0:experts_n], hot[:, 0:topk, 0:experts_n].rearrange("p k e -> p e k"),
                                          AX, ALU.add), "cho")

            def dv0(v, b):
                Y_pe.wait(v, b, "lg")
                seq(v, b, v.tensor_copy(values, psY[0:N, 0:experts_n]), "lg")
                pick(v, b, values)
                seq(v, b, v.tensor_tensor(tmp[:, 0:1], top_v[:, 1:2], top_v[:, 0:1], ALU.subtract), "d")

            def ac0(s, b):
                Y_dve.wait(s, b, "d")
                Y_act.post(s.activation(tmp[:, 1:2], tmp[:, 0:1], ACT.Exp), "e")

            def weights0(v, b):
                Y_act.wait(v, b, "e")
                seq(v, b, v.tensor_scalar(tmp[:, 2:3], tmp[:, 1:2], 1.0, None, ALU.add), "w0")
                seq(v, b, v.reciprocal(tmp[:, 3:4], tmp[:, 2:3]), "w1")
                st_s.wait(v, b - 2, f"k{topk - 1}")
                seq(v, b, v.tensor_scalar(w[:, 0:1], tmp[:, 3:4], tg_f, None, ALU.mult), "w2")
                seq(v, b, v.tensor_scalar(w[:, 1:2], w[:, 0:1], tmp[:, 1:2], None, ALU.mult), "w3")

            def ac1(s, b):
                Y_pe.wait(s, b, "lg")
                Y_act.post(s.activation(sc[:, 1, :], psY[0:N, 0:E1], ACT.Exp, scale=-1.0), "e")

            def dv1(v, b):
                Y_act.wait(v, b, "e")
                seq(v, b, v.tensor_scalar(sc[:, 2, :], sc[:, 1, :], 1.0, None, ALU.add), "s0")
                seq(v, b, v.reciprocal(values, sc[:, 2, :]), "s1")
                grouped = values.rearrange("p (g e) -> p g e", g=GROUPS)
                seq(v, b, v.tensor_reduce(gmax[:, 0:GROUPS], grouped, AX, ALU.max), "gm")
                seq(v, b, v.max(gtop[:, :], gmax[:, :]), "gt")
                seq(v, b, v.max_index(gidx[:, :], gtop[:, :], gmax[:, :]), "gi")
                seq(v, b, v.tensor_copy(gidf[:, :], gidx[:, 0:TOPG]), "gf")
                one_hot(v, b, ghot[:, :, :], gidf[:, :], TOPG, GROUPS, "gh")
                seq(v, b, v.tensor_reduce(gok[:, :], ghot[:, :, :].rearrange("p k g -> p g k"), AX, ALU.add), "go")
                seq(v, b, v.tensor_scalar(gok[:, :], gok[:, :], 2.0, -2.0, ALU.mult, ALU.add), "gk")
                seq(v, b, v.tensor_tensor(sc[:, 1, :].rearrange("p (g e) -> p g e", g=GROUPS), grouped,
                                          gok[:, :].unsqueeze(2).to_broadcast([N, GROUPS, E1 // GROUPS]), ALU.add), "msk")
                pick(v, b, sc[:, 1, :])
                seq(v, b, v.tensor_reduce(tmp[:, 0:1], top_v[:, 0:topk], AX, ALU.add), "sum")
                seq(v, b, v.reciprocal(tmp[:, 1:2], tmp[:, 0:1]), "rcp")
                st_s.wait(v, b - 2, f"k{topk - 1}")
                seq(v, b, v.tensor_scalar(w, top_v[:, 0:topk], tmp[:, 1:2], ROUTE_SCALE, ALU.mult, ALU.mult), "w2")
                seq(v, b, v.tensor_scalar(w, w, tg_f, None, ALU.mult), "w3")
            steps.append(("pe", off, pe))
            if L0:
                steps += [("dve", off, dv0), ("act", off, ac0), ("dve", off, weights0)]
            else:
                steps += [("act", off, ac1), ("dve", off, dv1)]

        def y_dispatch(steps, off, par):
            def pe(t, b):
                Y_dve.wait(t, b, "cho")
                t.matmul(psY[0:N, 0:experts_n], c["before"][:, :], chosen[:, 0:experts_n], start=True, stop=True)
                Y_pe.post(t.matmul(psY[0:N, 2 * E1:2 * E1 + experts_n], c["ones"][:, :], chosen[:, 0:experts_n],
                                   start=True, stop=True, skip_group_check=True), "rk")

            def dv(v, b):
                base = c["base"][:, 0:experts_n]
                Y_pe.wait(v, b, "rk")
                v.tensor_tensor(slot_of[:, 0:experts_n], psY[0:N, 0:experts_n], base, ALU.add)
                Y_dve.post(v.tensor_scalar(slot[:, par, 0:topk, 0], c["token"][:, 0:1].to_broadcast([N, topk]), 0.0, None,
                                           ALU.add), "tok")
                Y_dve.wait(v, b, "tok")
                v.tensor_scalar(c["token"][:, :], c["token"][:, :], float(N), None, ALU.add)
                Y_dve.post(v.tensor_tensor(base, psY[0:N, 2 * E1:2 * E1 + experts_n], base, ALU.add), "slot")
                Y_dve.wait(v, b, "slot")
                Y_dve.post(v.tensor_tensor(hit[:, 0:topk, 0:experts_n], hot[:, 0:topk, 0:experts_n],
                                           slot_of[:, 0:experts_n].unsqueeze(1).to_broadcast([N, topk, experts_n]), ALU.mult), "hit")
                Y_dve.wait(v, b, "hit")
                Y_dve.post(v.tensor_reduce(pos_f[:, 0:topk], hit[:, 0:topk, 0:experts_n], AX, ALU.add), "pos")
                Y_dve.wait(v, b, "pos")
                Y_dve.post(v.tensor_copy(pos[:, par, 0:topk], pos_f[:, 0:topk]), "posi")

            def po(g, b):
                Y_dve.wait(g, b, "posi")
                st_s.wait(g, b - 1, f"k{topk - 1}")
                settle(g, c)
                for k in range(topk):
                    g.indirect_dma_start(table, bass.IndirectOffsetOnAxis(pos[:, par, k:k + 1], 0), slot[:, par, k, :], None)\
                        .then_inc(st_s.sem, 16)
            steps += [("pe", off, pe), ("dve", off, dv), ("pool", off, po)]

        def project(steps, off, par, part):
            if L0:
                {0: lambda: (p_k0(steps, off, par, 0), p_k0(steps, off, par, 1)),
                 1: lambda: (p_norm0(steps, off, par), p_bias(steps, off, par), p_k0(steps, off, par, 2), p_k0(steps, off, par, 3)),
                 2: lambda: (p_v0(steps, off, par, 0), p_v0(steps, off, par, 1)),
                 3: lambda: p_v0(steps, off, par, 2),
                 4: lambda: p_q0(steps, off, par)}[part]()
            else:
                {0: lambda: (p_bias(steps, off, par), p_t1(steps, off, par), p_qkv1(steps, off, par, "q"), p_qkv1(steps, off, par, 0)),
                 1: lambda: (p_qkt1(steps, off, par, "q"), p_qkv1(steps, off, par, 1), p_qkt1(steps, off, par, 0),
                             p_qkv1(steps, off, par, 2)),
                 2: lambda: (p_qkt1(steps, off, par, 1), p_qkv1(steps, off, par, 3)),
                 3: lambda: (p_qkt1(steps, off, par, 2), p_qkt1(steps, off, par, 3))}[part]()

        def prologue():
            steps = []
            if not L0:
                p_norm1(steps, 0, 0)
            for part in range(5 if L0 else 4):
                project(steps, 0, 0, part)
            if not L0:
                p_norm1(steps, 1, 1)
            return steps

        def iteration(i, par):
            par %= 2
            nxt, prv = i is None or i + 1 < B, i is None or i > 0
            nx2 = i is None or i + 2 < B
            steps = []
            for p in range(pairs):
                x_scores(steps, 0, par, p)
                if p == 0 and prv:
                    y_out(steps, -1, 1 - par)
                if p:
                    x_values(steps, 0, par, p - 1)
                if nxt:
                    project(steps, 1, 1 - par, p)
                x_norm(steps, 0, par, p)
                x_transpose(steps, 0, par, p)
                if L0 and p == 2 and prv:
                    y_transpose(steps, -1, 1 - par)
                if L0 and p == 3 and prv:
                    y_route(steps, -1, 1 - par)
                if not L0 and p == 0 and prv:
                    y_transpose(steps, -1, 1 - par)
                if not L0 and p == 1 and prv:
                    y_route(steps, -1, 1 - par)
            if nxt:
                project(steps, 1, 1 - par, pairs)
            x_values(steps, 0, par, pairs - 1)
            if not L0 and nxt:
                project(steps, 1, 1 - par, 3)
            if prv:
                y_dispatch(steps, -1, 1 - par)
            if not L0 and nx2:
                p_norm1(steps, 2, par)
            return steps

        def epilogue():
            steps = []
            for f in (y_out, y_transpose, y_route, y_dispatch):
                f(steps, -1, (B - 1) % 2)
            return steps

        def rounds(name, eng):
            run_rounds(name, eng, prologue(), iteration, epilogue(), B, 2, 3, 3)

        with nc.Block() as block:

            @block.sync
            def _(s):
                init.wait(s, 0, "i")

                def load(b, par):
                    P_pool.wait(s, b - 2, "xb")
                    P_dve.wait(s, b - 2, "xn")
                    ld_x.wait(s, b - 1, "x")
                    settle(s, c)
                    src = a["x"][b] if L0 else dram["acc0"][0:TOKENS].rearrange("(b n) d -> b n d", n=N)[b]
                    s.dma_start(x[:, par, :], src).then_inc(ld_x.sem, 16)
                    if L0:
                        P_pe.wait(s, b - 2, "v2")
                        ld_c.wait(s, b - 1, "c")
                        settle(s, c)
                        s.dma_start(cT[:, par, :, 0:S], a["ctxT"][b].rearrange("(k p) s -> p k s", p=CK)).then_inc(ld_c.sem, 16)
                    else:
                        P_dve.wait(s, b - 2, "cn")
                        settle(s, c)
                        P_pool.wait(s, b - 2, "mb")
                        ld_c.wait(s, b - 1, "m")
                        settle(s, c)
                        rows = a["ctx_768"][b]
                        s.dma_start(ctx[:, par, 0:2, :], rows[0:2 * CH].rearrange("(j p) c -> p j c", p=CH)).then_inc(ld_c.sem, 16)
                        s.dma_start(ctx[0:S - 2 * CH, par, 2, :], rows[2 * CH:S]).then_inc(ld_c.sem, 16)
                        s.dma_start(m8[:, par, :], a["mask"][b].partition_broadcast(N)).then_inc(ld_c.sem, 16)
                load(0, 0)
                load(1, 1)
                c[f"n_w{layer}"] = load_expert_weights(s, a, c, layer)
                with s.Fori(2, B - 1, 2) as b:
                    load(b, 0)
                    load(b + 1, 1)

            @block.scalar
            def _(s):
                init.wait(s, 0, "i")
                rounds("act", s)
                s.wait_ge(st_x.sem, B * 32)

            @block.vector
            def _(v):
                v.memset(qz[:, :, :, :], 0.0)
                v.memset(prob[:, :, :], 0.0)
                for e in range(experts_n):
                    v.memset(c["base"][:, e:e + 1], float(e * REGION))
                if L0:
                    v.memset(cT[:, :, :, :], 0.0)
                else:
                    v.memset(ctx[:, :, :, :], 0.0)
                    v.memset(mb[:, :, S:SP], NEG)
                    v.memset(mb[:, :, SP:K1], 0.0)
                    v.memset(gmax[:, :], -1.0)
                    v.tensor_scalar(c["token"][:, :], c["token"][:, :], float(-TOKENS), None, ALU.add)
                init.post(v.memset(vv[:, :, :, :], 0.0), "i")
                init.wait(v, 0, "i")
                rounds("dve", v)

            @block.tensor
            def _(t):
                init.wait(t, 0, "i")
                rounds("pe", t)

            @block.gpsimd
            def _(g):
                init.wait(g, 0, "i")
                rounds("pool", g)
                g.wait_ge(st_s.sem, B * topk * 16)

        for l in (P_dve, P_act, P_pool, P_pe, X_pe, X_dve, X_act, X_pool, Y_pe, Y_dve, Y_act, Y_pool):
            assert l.seen % len(l.events) == 0


def experts(nc, maker, a, dram, c, layer):
    L0 = layer == 0
    L = str(layer)
    E, topk, F = (E0, TOP0, F0) if L0 else (E1, TOP1, F1)
    NT = most_tiles(E, topk)
    table, acc, xn_rows = dram[f"table{layer}"], dram[f"acc{layer}"], dram[f"xn{layer}"]
    ident = c["ident"]
    w = c["expert_w"]
    w13 = w[:, 0:E * 4 * F].rearrange("p (e k f) -> p e k f", e=E, k=2)
    w2 = w[:, E * 4 * F:E * 4 * F + E * (F // P) * D].rearrange("p (e k d) -> p e k d", e=E, k=F // P)
    KF = F // P
    LOOK = 2
    NTX = NT + LOOK + 1
    stack = ExitStack()
    with stack:
        sb, ps, lane = maker(stack)
        psX = ps("psX" + L, [P, 512])
        psG = ps("psG" + L, [P, 2, 512])
        psU = ps("psU" + L, [P, 2, 512])
        psH = ps("psH" + L, [P, 512])
        psD = ps("psD" + L, [P, 2, 512])
        slots = sb("slots" + L, [P, 4, 2], I32)
        slot_w = slots[:, :, 1].bitcast(F32)
        xg = sb("xg" + L, [P, 4, D])
        xT = sb("xgT" + L, [P, 2, 2, P])
        gate = sb("gate" + L, [P, 2, F])
        hid = sb("hid" + L, [P, 2, F])
        hT = sb("hT" + L, [P, 2, KF, P])
        y = sb("y" + L, [P, 2, D])
        f = sb("tilef" + L, [1, 4, E])
        fi = sb("tilei" + L, [1, 2, E], I32)
        ge = sb("tilege" + L, [1, NTX, E])
        jj = sb("tilej" + L, [1, NTX])
        tf = sb("tilet" + L, [1, 3, NTX])
        tile_e = sb("tile_e" + L, [1, NTX], I32)
        tile_r = sb("tile_r" + L, [1, NTX], I32)
        if not L0:
            bias = sb("bias1", [P, E, 3, F])
            pre = sb("pre1", [P, 2, 2 * F])
            yb = sb("yb1", [P, 2, D])

        setup_d = lane("tile_d" + L, ["n", "i", "sh", "f", "cum", "ge", "e", "tb", "tbs", "tr", "tr2", "row", "done"])
        setup_p = lane("tile_p" + L, ["j"])
        cum = lane("tile_c" + L, ["e"])
        ld_s = lane("ld_s" + L, ["s"], 16)
        ga = lane("ga" + L, ["g"], 16)
        sc = lane("sc" + L, ["s"], 16)
        ld_b = lane("ld_b" + L, ["b"], 16)
        pe_tx, pe_g, pe_u, pe_th, pe_o = (lane(f"pe_{n}{L}", [n]) for n in ("tx", "g", "u", "th", "o"))
        act_xt, act_g, act_h = (lane(f"act_{n}{L}", [n]) for n in ("xt", "g", "h"))
        dve_h = lane("dve_h" + L, ["h"] if L0 else ["pre", "h"])
        dve_y = lane("dve_y" + L, ["y"] if L0 else ["yb", "y"])

        def gather(steps, off, r):
            def po(g, j):
                ld_s.wait(g, j, "s")
                pe_tx.wait(g, j - 4, "tx")
                ga.wait(g, j - 1, "g")
                settle(g, c)
                g.indirect_dma_start(xg[:, r, :], None, xn_rows, bass.IndirectOffsetOnAxis(slots[:, r, 0:1].bitcast(U32), 0))\
                    .then_inc(ga.sem, 16)
            steps.append(("pool", off, po))

        def tx(steps, off, r):
            def t1(t, j):
                ga.wait(t, j, "g")
                act_xt.wait(t, j - 1, "xt")
                for k in range(2):
                    mm = t.transpose(psX[:, k * P:(k + 1) * P], xg[:, r, k * P:(k + 1) * P], ident[:, :])
                pe_tx.post(mm, "tx")

            def a1(s, j):
                pe_tx.wait(s, j, "tx")
                pe_g.wait(s, j - 2, "g") if not L0 else pe_u.wait(s, j - 2, "u")
                act_xt.post(s.activation(xT[:, r % 2, :, :], psX[:, 0:2 * P].rearrange("p (k n) -> p k n", k=2), ACT.Copy), "xt")
            steps += [("pe", off, t1), ("act", off, a1)]

        def expert_of(t, j):
            return t.value_load(tile_e[0:1, bass.ds(j, 1)], min_val=0, max_val=E - 1)

        def up(steps, off, r, part):
            pst, lan = ((psG, pe_g), (psU, pe_u))[part]

            def t1(t, j):
                act_xt.wait(t, j, "xt")
                if L0:
                    (act_g if part == 0 else dve_h).wait(t, j - 2, "g" if part == 0 else "h")
                else:
                    dve_h.wait(t, j - 2, "pre")
                settle(t, c)
                e = expert_of(t, j)
                for k in range(2):
                    mm = t.matmul(pst[:, r % 2, :], xT[:, r % 2, k, :], w13[:, bass.ds(e, 1), k, part * 512:(part + 1) * 512],
                                  start=k == 0, stop=k == 1)
                lan.post(mm, "gu"[part])
            steps.append(("pe", off, t1))
            if L0 and part == 0:
                def a1(s, j):
                    pe_g.wait(s, j, "g")
                    dve_h.wait(s, j - 2, "h")
                    act_g.post(s.activation(gate[:, r % 2, :], psG[:, r % 2, :], ACT.Silu), "g")
                steps.append(("act", off, a1))
            elif L0:
                def d1(v, j):
                    pe_u.wait(v, j, "u")
                    act_g.wait(v, j, "g")
                    pe_th.wait(v, j - 2, "th")
                    dve_h.post(v.tensor_tensor(hid[:, r % 2, :], psU[:, r % 2, :], gate[:, r % 2, :], ALU.mult), "h")
                steps.append(("dve", off, d1))
            else:
                def d0(v, j):
                    pe_g.wait(v, j, "g")
                    settle(v, c)
                    e = v.value_load(tile_e[0:1, bass.ds(j, 1)], min_val=0, max_val=E - 1)
                    dve_h.post(v.tensor_tensor(pre[:, r % 2, :], psG[:, r % 2, :],
                                               bias[:, bass.ds(e, 1), 0:2, :].rearrange("p e k f -> p (e k f)"), ALU.add), "pre")

                def a1(s, j):
                    dve_h.wait(s, j, "pre")
                    act_g.post(s.activation(gate[:, r % 2, :], pre[:, r % 2, 0:F], ACT.Silu), "g")

                def d1(v, j):
                    act_g.wait(v, j, "g")
                    pe_th.wait(v, j - 2, "th")
                    dve_h.post(v.tensor_tensor(hid[:, r % 2, :], pre[:, r % 2, F:2 * F], gate[:, r % 2, :], ALU.mult), "h")
                steps += [("dve", off, d0), ("act", off, a1), ("dve", off, d1)]

        def th(steps, off, r):
            def t1(t, j):
                dve_h.wait(t, j, "h")
                act_h.wait(t, j - 1, "h")
                for k in range(KF):
                    mm = t.transpose(psH[:, k * P:(k + 1) * P], hid[:, r % 2, k * P:(k + 1) * P], ident[:, :])
                pe_th.post(mm, "th")

            def a1(s, j):
                pe_th.wait(s, j, "th")
                pe_o.wait(s, j - 2, "o")
                act_h.post(s.activation(hT[:, r % 2, :, :], psH[:, 0:F].rearrange("p (k n) -> p k n", k=KF), ACT.Copy), "h")
            steps += [("pe", off, t1), ("act", off, a1)]

        def down(steps, off, r):
            def t1(t, j):
                act_h.wait(t, j, "h")
                dve_y.wait(t, j - 2, "y" if L0 else "yb")
                settle(t, c)
                e = expert_of(t, j)
                for k in range(KF):
                    mm = t.matmul(psD[:, r % 2, 0:D], hT[:, r % 2, k, :], w2[:, bass.ds(e, 1), k, :], start=k == 0, stop=k == KF - 1)
                pe_o.post(mm, "o")

            def d1(v, j):
                pe_o.wait(v, j, "o")
                src = psD[:, r % 2, 0:D]
                if not L0:
                    settle(v, c)
                    e = v.value_load(tile_e[0:1, bass.ds(j, 1)], min_val=0, max_val=E - 1)
                    dve_y.post(v.tensor_tensor(yb[:, r % 2, :], src, bias[:, bass.ds(e, 1), 2, :].rearrange("p e f -> p (e f)"),
                                               ALU.add), "yb")
                    dve_y.wait(v, j, "yb")
                    src = yb[:, r % 2, :]
                sc.wait(v, j - 2, "s")
                dve_y.post(v.tensor_scalar(y[:, r % 2, :], src, slot_w[:, r:r + 1], None, ALU.mult), "y")

            def po(g, j):
                dve_y.wait(g, j, "y")
                sc.wait(g, j - 1, "s")
                settle(g, c)
                g.indirect_dma_start(acc, bass.IndirectOffsetOnAxis(slots[:, r, 0:1].bitcast(U32), 0), y[:, r % 2, :], None,
                                     compute_op=ALU.add).then_inc(sc.sem, 16)
            steps += [("pe", off, t1), ("dve", off, d1), ("pool", off, po)]

        def prologue():
            steps = []
            gather(steps, 0, 0)
            gather(steps, 1, 1)
            tx(steps, 0, 0)
            return steps

        def iteration(i, r):
            prv = i is None or i > 0
            steps = []
            gather(steps, 2, (r + 2) % 4)
            up(steps, 0, r % 4, 0)
            if prv:
                th(steps, -1, (r - 1) % 4)
            if L0:
                up(steps, 0, r % 4, 1)
            tx(steps, 1, (r + 1) % 4)
            if prv:
                down(steps, -1, (r - 1) % 4)
            return steps

        def epilogue():
            steps = []
            r = (NT - 1) % 4
            th(steps, -1, r)
            down(steps, -1, r)
            return steps

        head = 3 + (NT - 3) % 4

        def rounds(name, eng):
            run_rounds(name, eng, prologue(), iteration, epilogue(), NT, 4, head, 0)

        with nc.Block() as block:

            @block.gpsimd
            def _(g):
                setup_p.post(g.iota(jj[:, :], [[1, NTX]], base=0, channel_multiplier=0, allow_small_or_imprecise_dtypes=True), "j")
                rounds("pool", g)
                g.wait_ge(sc.sem, 16 * NT)
                g.wait_ge(ga.sem, 16 * (NT + LOOK))

            @block.vector
            def _(v):
                def seq(ins, name):
                    setup_d.post(ins, name)
                    setup_d.wait(v, 0, name)
                base = c["base"][0:1, 0:E]
                for e in range(E):
                    ins = v.tensor_scalar(f[:, 0, e:e + 1], base[:, e:e + 1], float(P - 1 - e * REGION), None, ALU.add)
                seq(ins, "n")
                seq(v.tensor_copy(fi[:, 0, :], f[:, 0, :]), "i")
                seq(v.tensor_scalar(fi[:, 1, :], fi[:, 0, :], 7, None, ALU.arith_shift_right), "sh")
                seq(v.tensor_copy(f[:, 1, :], fi[:, 1, :]), "f")
                seq(v.tensor_copy(f[:, 2, 0:1], f[:, 1, 0:1]), "cum")
                for e in range(1, E):
                    v.tensor_tensor(f[:, 2, e:e + 1], f[:, 2, e - 1:e], f[:, 1, e:e + 1], ALU.add).then_inc(cum.sem, 1)
                    v.wait_ge(cum.sem, e)
                setup_p.wait(v, 0, "j")
                seq(v.tensor_tensor(ge[:, :, :], jj[:, :].unsqueeze(2).to_broadcast([1, NTX, E]),
                                    f[:, 2, :].unsqueeze(1).to_broadcast([1, NTX, E]), ALU.is_ge), "ge")
                seq(v.tensor_reduce(tf[:, 0, :], ge[:, :, :], AX, ALU.add), "e")
                seq(v.tensor_tensor(ge[:, :, :], ge[:, :, :], f[:, 1, :].unsqueeze(1).to_broadcast([1, NTX, E]), ALU.mult), "tb")
                seq(v.tensor_reduce(tf[:, 1, :], ge[:, :, :], AX, ALU.add), "tbs")
                seq(v.tensor_tensor(tf[:, 2, :], jj[:, :], tf[:, 1, :], ALU.subtract), "tr")
                seq(v.tensor_scalar(tf[:, 2, :], tf[:, 2, :], float(P), None, ALU.mult), "tr2")
                seq(v.scalar_tensor_tensor(tf[:, 1, :], tf[:, 0, :], float(REGION), tf[:, 2, :], ALU.mult, ALU.add), "row")
                v.tensor_copy(tile_r[:, :], tf[:, 1, :])
                seq(v.tensor_scalar(tile_e[:, :], tf[:, 0, :], float(E - 1), None, ALU.min), "done")
                if not L0:
                    v.wait_ge(ld_b.sem, 16 * 3)
                rounds("dve", v)

            @block.sync
            def _(s):
                if not L0:
                    for k, n in enumerate(("b1", "b3", "b2")):
                        s.dma_start(bias[:, :, k, :], a[f"L1_ffn_{n}"].partition_broadcast(P)).then_inc(ld_b.sem, 16)
                setup_d.wait(s, 0, "done")

                def load(j, r):
                    sc.wait(s, j - 4, "s")
                    ld_s.wait(s, j - 1, "s")
                    settle(s, c)
                    row = s.value_load(tile_r[0:1, bass.ds(j, 1)], min_val=0, max_val=table.shape[0] - P)
                    s.dma_start(slots[:, r, :], table[bass.ds(row, P), :]).then_inc(ld_s.sem, 16)
                total = NT + LOOK
                first = 4 + total % 4
                for j in range(first):
                    load(j, j % 4)
                with s.Fori(first, total - 3, 4) as j:
                    for k in range(4):
                        load(j + k, (first + k) % 4)

            @block.scalar
            def _(s):
                rounds("act", s)

            @block.tensor
            def _(t):
                t.wait_ge(c[f"x{layer}_ready"].sem, 16 * c[f"n_w{layer}"])
                setup_d.wait(t, 0, "done")
                rounds("pe", t)


_SAME = ["x", "ctx_768", "g_xattn", "g_ffn", "L0_xattn_Wq", "L0_xattn_Wk", "L0_xattn_Wv", "L0_xattn_Wo", "L0_xattn_bo",
         "L0_ffn_moe_router", "L0_ffn_moe_w13", "L0_ffn_moe_w2", "L1_xattn_ln_x_g", "L1_xattn_ln_x_b",
         "L1_xattn_ln_l_g", "L1_xattn_ln_l_b", "L1_xattn_qn_g", "L1_xattn_kn_g", "L1_xattn_bo",
         "L1_ffn_b1", "L1_ffn_b2", "L1_ffn_b3"]


def kernel(**inputs):
    import numpy as _np
    import concourse.bacc as _bacc
    from concourse import mybir as _mybir
    from concourse.bass_utils import run_bass_kernel_spmd as _run

    i = {k: _np.asarray(v) for k, v in inputs.items()}
    laid = {n: i[n] for n in _SAME}
    laid["ctxT"] = i["ctx_768"].transpose(0, 2, 1)
    laid["mask"] = i["mask_BxS2_bk0"]
    for n in ("L1_xattn_Wq", "L1_xattn_Wkv", "L1_xattn_Wlkv", "L1_xattn_Wo", "L1_ffn_Wg"):
        laid[n + "T"] = i[n].T
    for n in ("L1_ffn_W1", "L1_ffn_W2", "L1_ffn_W3"):
        laid[n + "T"] = i[n].transpose(0, 2, 1)
    laid = {n: _np.ascontiguousarray(v) for n, v in laid.items()}

    nc = _bacc.Bacc("TRN2", target_bir_lowering=False, num_devices=1)
    args = {n: nc.dram_tensor(f"in_{n}", v.shape, _mybir.dt.from_np(v.dtype), kind="ExternalInput").ap()
            for n, v in laid.items()}
    out = nc.dram_tensor("out", (TOKENS + SPARE, D), F32, kind="ExternalOutput").ap()
    build(nc, args, out)
    r = _run(nc, [{f"in_{n}": v for n, v in laid.items()}], core_ids=[0])
    return r.results[0]["out"][0:TOKENS].reshape(B, N, D)
```

```python
from contextlib import ExitStack

import numpy as np

import concourse.bass as bass
from concourse import mybir

F32 = mybir.dt.float32
I32 = mybir.dt.int32
U32 = mybir.dt.uint32
U8 = mybir.dt.uint8
ALU = mybir.AluOpType
ACT = mybir.ActivationFunctionType
AX = mybir.AxisListType.X

B, N, D = 32, 100, 256
S, C = 361, 192
TOKENS = B * N
P = 128
SPARE = P
CH = 121
NCH = 3
SP = CH * NCH
CK = 96
H0, H1, DH = 8, 4, 64
I0, I1 = H0 * DH, H1 * DH
K1 = CH + SP
REGION = TOKENS
E0, TOP0, F0 = 8, 2, 512
E1, TOP1, F1 = 16, 4, 256
GROUPS, TOPG = 4, 2
ROUTE_SCALE = 2.5
LN_EPS = 1e-5
RMS_EPS = 1e-8
NEG = -1e30


def most_tiles(experts, top):
    return (TOKENS * top + experts * (P - 1)) // P


class Lane:

    def __init__(self, sem, events, step=1):
        self.sem, self.events, self.step = sem, list(events), step
        self.seen = 0
        assert len(set(self.events)) == len(self.events)

    def post(self, ins, event):
        assert self.events[self.seen % len(self.events)] == event, (self.sem, event, self.seen)
        self.seen += 1
        ins.then_inc(self.sem, self.step)

    def wait(self, eng, rnd, event):
        k = (self.events.index(event) + 1) * self.step
        value = rnd * (len(self.events) * self.step) + k
        if isinstance(value, int) and value <= 0:
            return
        eng.wait_ge(self.sem, value)


class Group:

    def __init__(self, lanes):
        self.lanes = lanes
        self.of = {e: l for l in lanes for e in l.events}

    def post(self, ins, event):
        self.of[event].post(ins, event)

    def wait(self, eng, rnd, event):
        self.of[event].wait(eng, rnd, event)


def settle(eng, c):
    eng.sem_inc(c["settled"], 1)


def emit(steps, name, eng, base):
    for engine, off, fn in steps:
        if engine == name:
            fn(eng, base + off)


def run_rounds(name, eng, prologue, iteration, epilogue, rounds, unroll, head, tail):
    emit(prologue, name, eng, 0)
    for i in range(head):
        emit(iteration(i, i), name, eng, i)
    assert (rounds - head - tail) % unroll == 0
    bodies = [iteration(None, head + j) for j in range(unroll)]
    if any(e == name for body in bodies for e, _, _ in body):
        with eng.Fori(head, rounds - tail - unroll + 1, unroll) as i:
            for j, body in enumerate(bodies):
                emit(body, name, eng, i + j)
    for i in range(rounds - tail, rounds):
        emit(iteration(i, i), name, eng, i)
    emit(epilogue, name, eng, rounds)


def build(nc, a, out):
    top = ExitStack()
    dram = {}
    for n, e, t in ((0, E0, most_tiles(E0, TOP0)), (1, E1, most_tiles(E1, TOP1))):
        rows = e * REGION + (t + 3) * P
        dram[f"table{n}"] = nc.dram_tensor(f"table{n}", (rows, 2), I32, kind="Internal").ap()
        dram[f"xn{n}"] = nc.dram_tensor(f"xn{n}", (TOKENS + SPARE, D), F32, kind="Internal").ap()
    dram["acc0"] = nc.dram_tensor("acc0", (TOKENS + SPARE, D), F32, kind="Internal").ap()
    dram["acc1"] = out

    def maker(stack):
        def sb(name, shape, dt=F32):
            return stack.enter_context(nc.sbuf_tensor(name, list(shape), dt))

        def ps(name, shape):
            return stack.enter_context(nc.psum_tensor(name, list(shape), F32))

        def lane(name, events, step=1):
            return Lane(stack.enter_context(nc.semaphore(name)), events, step)

        return sb, ps, lane

    with top:
        sb, ps, lane = maker(top)
        c = dict(
            settled=top.enter_context(nc.semaphore("settled")),
            ident=sb("ident", [P, P]), before=sb("before", [N, N]), ones=sb("ones", [N, N]),
            iota=sb("iota", [N, E1]), neghalf=sb("neghalf", [P, 4]),
            gates=sb("gates", [P, 4]), tg=sb("tg", [P, 4]),
            token=sb("token", [N, 1], I32), base=sb("base", [N, E1]),
            expert_w=sb("expert_w", [P, 3 * E0 * 2 * F0]),
            wq0=sb("wq0", [P, 2, I0]), wk0=sb("wk0", [CK, 2, I0]), wv0=sb("wv0", [CK, 2, I0]),
            wo0=sb("wo0", [P, 4, D]), wr0=sb("wr0", [P, 2, E0]), bo0=sb("bo0", [N, D]),
            wq1=sb("wq1", [P, 2, I1]), wkv1=sb("wkv1", [CK, 2, 2 * I1]), wlkv1=sb("wlkv1", [P, 2, 2 * I1]),
            wo1=sb("wo1", [P, 2, D]), wr1=sb("wr1", [P, 2, E1]), bo1=sb("bo1", [N, D]),
            cx_g=sb("cx_g", [CK, 2]), cx_b=sb("cx_b", [CK, 2]), lt_g=sb("lt_g", [P, 2]), lt_b=sb("lt_b", [P, 2]),
            qk_g=sb("qk_g", [P, 2]), qk_s=sb("qk_s", [P, 1]),
            w_ready=lane("w_ready", ["all"], 16), x0_ready=lane("experts0_w", ["w"], 16),
            x1_ready=lane("experts1_w", ["w"], 16),
        )
        setup(nc, maker, a, dram, c)
        attention(nc, maker, a, dram, c, 0)
        experts(nc, maker, a, dram, c, 0)
        attention(nc, maker, a, dram, c, 1)
        experts(nc, maker, a, dram, c, 1)


def load_expert_weights(eng, a, c, n):
    w = c["expert_w"]
    if n == 0:
        w13 = w[:, 0:E0 * 2 * 2 * F0].rearrange("p (e k f) -> p e k f", e=E0, k=2)
        w2 = w[:, E0 * 4 * F0:E0 * 4 * F0 + E0 * 4 * D].rearrange("p (e k d) -> p e k d", e=E0, k=4)
        for e in range(E0):
            eng.dma_start(w13[:, e], a["L0_ffn_moe_w13"][e].rearrange("(k p) f -> p k f", p=P)).then_inc(c["x0_ready"].sem, 16)
            eng.dma_start(w2[:, e], a["L0_ffn_moe_w2"][e].rearrange("(k p) d -> p k d", p=P)).then_inc(c["x0_ready"].sem, 16)
        return 2 * E0
    w13 = w[:, 0:E1 * 2 * 2 * F1].rearrange("p (e k f) -> p e k f", e=E1, k=2)
    w2 = w[:, E1 * 4 * F1:E1 * 4 * F1 + E1 * 2 * D].rearrange("p (e k d) -> p e k d", e=E1, k=2)
    for e in range(E1):
        eng.dma_start(w13[:, e, :, 0:F1], a["L1_ffn_W1T"][e].rearrange("(k p) f -> p k f", p=P)).then_inc(c["x1_ready"].sem, 16)
        eng.dma_start(w13[:, e, :, F1:2 * F1], a["L1_ffn_W3T"][e].rearrange("(k p) f -> p k f", p=P)).then_inc(c["x1_ready"].sem, 16)
        eng.dma_start(w2[:, e], a["L1_ffn_W2T"][e].rearrange("(k p) d -> p k d", p=P)).then_inc(c["x1_ready"].sem, 16)
    return 3 * E1


def setup(nc, maker, a, dram, c):
    stack = ExitStack()
    with stack:
        sb, ps, lane = maker(stack)
        empty = sb("empty_slots", [P, P, 2], I32)
        zero = sb("zero_rows", [P, D])
        pool = lane("setup_pool", ["z0", "z1", "z2", "ident", "before", "i"])
        dve = lane("setup_dve", ["c0", "c1", "g"])
        act = lane("setup_act", ["tg"])
        st = lane("setup_stores", ["s"], 16)
        w_ready = c["w_ready"]
        with nc.Block() as block:

            @block.gpsimd
            def _(g):
                pool.post(g.memset(c["ident"][:, :], 0.0), "z0")
                pool.post(g.memset(empty[:, :, :], 0), "z1")
                g.memset(zero[:, :], 0.0)
                pool.post(g.memset(c["ones"][:, :], 1.0), "z2")
                pool.wait(g, 0, "z2")
                pool.post(g.affine_select(out=c["ident"][:, :], in_=c["ident"][:, :], compare_op=ALU.not_equal, fill=1.0,
                                          base=0, pattern=[[-1, P]], channel_multiplier=1), "ident")
                pool.post(g.affine_select(out=c["before"][:, :], in_=c["ones"][:, :], compare_op=ALU.is_gt, fill=0.0,
                                          base=0, pattern=[[1, N]], channel_multiplier=-1), "before")
                g.iota(c["iota"][:, :], [[1, E1]], base=0, channel_multiplier=0, allow_small_or_imprecise_dtypes=True)
                g.iota(c["token"][:, :], [[1, 1]], base=0, channel_multiplier=1)
                pool.post(g.iota(empty[:, :, 0], [[1, P]], base=TOKENS, channel_multiplier=0), "i")

            @block.sync
            def _(s):
                def w(dst, src):
                    s.dma_start(dst, src).then_inc(w_ready.sem, 16)
                    w.n += 1
                w.n = 0
                with nc.allow_non_contiguous_dma(reason="a few per-partition constants"):
                    w(c["gates"][:, 0:2], a["g_xattn"].partition_broadcast(P))
                    w(c["gates"][:, 2:4], a["g_ffn"].partition_broadcast(P))
                    w(c["cx_g"][:, :], a["L1_xattn_ln_x_g"].rearrange("(k p) -> p k", p=CK))
                    w(c["cx_b"][:, :], a["L1_xattn_ln_x_b"].rearrange("(k p) -> p k", p=CK))
                    w(c["lt_g"][:, :], a["L1_xattn_ln_l_g"].rearrange("(k p) -> p k", p=P))
                    w(c["lt_b"][:, :], a["L1_xattn_ln_l_b"].rearrange("(k p) -> p k", p=P))
                    for half in range(2):
                        for j, n in enumerate(("q", "k")):
                            w(c["qk_g"][half * DH:(half + 1) * DH, j:j + 1],
                              a[f"L1_xattn_{n}n_g"].rearrange("(p k) -> p k", k=1))
                for n, src, p in (("wq0", "L0_xattn_Wq", P), ("wk0", "L0_xattn_Wk", CK), ("wv0", "L0_xattn_Wv", CK),
                                  ("wo0", "L0_xattn_Wo", P), ("wr0", "L0_ffn_moe_router", P),
                                  ("wq1", "L1_xattn_WqT", P), ("wkv1", "L1_xattn_WkvT", CK), ("wlkv1", "L1_xattn_WlkvT", P),
                                  ("wo1", "L1_xattn_WoT", P), ("wr1", "L1_ffn_WgT", P)):
                    w(c[n][:, :, :], a[src].rearrange("(k p) n -> p k n", p=p))
                w(c["bo0"][:, :], a["L0_xattn_bo"].partition_broadcast(N))
                w(c["bo1"][:, :], a["L1_xattn_bo"].partition_broadcast(N))
                c["w_loads"] = w.n
                s.wait_ge(w_ready.sem, 16 * w.n)

            @block.vector
            def _(v):
                dve.post(v.memset(c["neghalf"][:, :], -0.5), "c0")
                v.wait_ge(w_ready.sem, 16 * c["w_loads"])
                dve.post(v.tensor_tensor(c["qk_s"][:, :], c["qk_g"][:, 0:1], c["qk_g"][:, 1:2], ALU.mult), "c1")
                dve.wait(v, 0, "c1")
                v.tensor_scalar(c["qk_s"][:, :], c["qk_s"][:, :], DH ** -0.5, None, ALU.mult)
                act.wait(v, 0, "tg")
                v.tensor_scalar(c["bo0"][:, :], c["bo0"][:, :], c["tg"][0:N, 0:1], None, ALU.mult)
                dve.post(v.tensor_scalar(c["bo1"][:, :], c["bo1"][:, :], c["tg"][0:N, 1:2], None, ALU.mult), "g")

            @block.scalar
            def _(s):
                pool.wait(s, 0, "i")
                for n in range(2):
                    t = dram[f"table{n}"]
                    blocks = t.shape[0] // P
                    full = t.rearrange("(b r) c -> b (r c)", r=P)
                    for at in range(0, blocks, P):
                        m = min(P, blocks - at)
                        s.dma_start(full[at:at + m], empty[0:m].rearrange("p r c -> p (r c)")).then_inc(st.sem, 16)
                        st.seen += 1
                    s.dma_start(dram[f"xn{n}"][TOKENS:TOKENS + SPARE], zero[:, :]).then_inc(st.sem, 16)
                    s.dma_start(dram[f"acc{n}"][TOKENS:TOKENS + SPARE], zero[:, :]).then_inc(st.sem, 16)
                    st.seen += 2
                s.wait_ge(w_ready.sem, 16 * c["w_loads"])
                act.post(s.activation(c["tg"][:, :], c["gates"][:, :], ACT.Tanh), "tg")
                s.wait_ge(st.sem, 16 * st.seen)


def attention(nc, maker, a, dram, c, layer):
    L0 = layer == 0
    heads = H0 if L0 else H1
    pairs = heads // 2
    keys = SP if L0 else K1
    nch = NCH if L0 else NCH + 1
    experts_n, topk = (E0, TOP0) if L0 else (E1, TOP1)
    tg_x, tg_f = c["tg"][0:N, layer:layer + 1], c["tg"][0:N, 2 + layer:3 + layer]
    wo, wr, bo = c[f"wo{layer}"], c[f"wr{layer}"], c[f"bo{layer}"]
    table, acc, xn_rows = dram[f"table{layer}"], dram[f"acc{layer}"], dram[f"xn{layer}"]
    ident, neghalf = c["ident"], c["neghalf"]
    L = str(layer)

    stack = ExitStack()
    with stack:
        sb, ps, lane = maker(stack)
        psS = ps("psS" + L, [P, 2, 512])
        psT = ps("psT" + L, [P, 2, 512])
        psO = ps("psO" + L, [P, 512])
        psJ = ps("psJ" + L, [P, 2, 512])
        psY = ps("psY" + L, [P, 512])

        x = sb("x" + L, [N, 2, D])
        xb = sb("xb" + L, [N, 2, D])
        st = sb("st" + L, [N, 6])
        mv = sb("mv" + L, [N, 2])
        rstd = sb("rstd" + L, [N, 2])
        xn = sb("xn_a" + L, [N, 2, D])
        xT = sb("xT" + L, [P, 2, N])
        qz = sb("qz" + L, [P, 2, heads, N])
        kT = sb("kT" + L, [P, 2, pairs, keys])
        if L0:
            vv = sb("vv0", [CH, 2, NCH, I0])
        else:
            kv = sb("kv", [CH, 2, NCH + 2, 2 * I1])
            vv = kv[:, :, 1:, I1:2 * I1]
        prob = sb("prob" + L, [N, 4, keys])
        nm = sb("nm" + L, [N, 4])
        rs = sb("rs" + L, [N, 4])
        rc = sb("rc" + L, [N, 4])
        pT = sb("pT" + L, [CH, 2, 2, nch, N])
        oT = sb("oT" + L, [P, pairs, N])
        x1 = sb("x1" + L, [N, 2, D])
        xm = sb("xm" + L, [N, 2, D])
        st1 = sb("st1" + L, [N, 6])
        mv1 = sb("mv1" + L, [N, 2])
        rstd1 = sb("rstd1" + L, [N, 2])
        xmT = sb("xmT" + L, [P, 2, N])
        sc = sb("sc" + L, [N, 3, E1])
        top_v = sb("top_v" + L, [N, 8])
        top_i = sb("top_i" + L, [N, 8], U32)
        top_f = sb("top_f" + L, [N, TOP1])
        hot = sb("hot" + L, [N, TOP1, E1])
        hit = sb("hit" + L, [N, TOP1, E1])
        chosen = sb("chosen" + L, [N, E1])
        slot_of = sb("slot_of" + L, [N, E1])
        pos_f = sb("pos_f" + L, [N, TOP1])
        tmp = sb("tmp" + L, [N, 8])
        pos = sb("pos" + L, [N, 2, TOP1], U32)
        slot = sb("slot" + L, [N, 2, TOP1, 2], I32)
        slot_w = slot[:, :, :, 1].bitcast(F32)
        if L0:
            cT = sb("cT" + L, [CK, 2, 2, SP])
        else:
            cn = ctx = sb("ctx", [CH, 2, NCH, C])
            xl = sb("xl", [N, 2, D])
            lT = xT
            cst = sb("cst", [CH, NCH, 6])
            cmv = sb("cmv", [CH, NCH, 2])
            crs = sb("crs", [CH, 2, NCH])
            cTn = sb("cTn", [CK, 2, SP])
            sq = sb("sq", [CH, NCH + 2, I1])
            ss = sb("ss", [CH, NCH + 2, H1])
            rk = sb("rk", [CH, NCH + 2, H1])
            m8 = sb("m8", [N, 2, S], U8)
            mb = sb("mb", [N, 2, K1])
            gmax = sb("gmax", [N, 8])
            gtop = sb("gtop", [N, 8])
            gidx = sb("gidx", [N, 8], U32)
            gidf = sb("gidf", [N, TOPG])
            ghot = sb("ghot", [N, TOPG, GROUPS])
            gok = sb("gok", [N, GROUPS])

        ld_x = lane("ld_x" + L, ["x"], 16)
        ld_c = lane("ld_c" + L, ["c"] if L0 else ["c0", "c1", "m"], 16)
        st_x = lane("st_x" + L, ["x1", "xm"], 16)
        st_s = lane("st_s" + L, ["k%d" % k for k in range(topk)], 16)
        init = lane("init" + L, ["i"])

        def group(name, *stages):
            return Group([lane(f"{name}_{k}{L}", events) for k, events in enumerate(stages)])

        each_pair, each_head = range(pairs), range(heads)
        if L0:
            now = []
            N_dve, N_pool = lane("N_dve0", ["stat", "mv", "xn"]), lane("N_pool0", ["ve", "rstd"])
            uses = ["xt", "k0", "k1", "q", "k2", "k3", "v0", "v1", "v2"]
            owner = dict(k0="act", k1="act", k2="act", k3="act", v0="dve", v1="dve", v2="dve", xt="act", q="dve")
            P_pool = lane("P_pool0", ["xb"])
        else:
            N_dve = lane("N_dve1", ["stat", "mv", "xn", "stat2", "mv2", "xl", "cstat", "cmv", "cn"])
            N_pool = lane("N_pool1", ["ve", "rstd", "ve2", "rstd2", "cve", "crs", "mb"])
            uses = ["lt", "ct0", "ct1", "qt", "kt0", "kt1", "q", "kv0", "kv1", "kv2", "kv3"]
            now = ["qt", "kt0", "kt1"]
            owner = {u: "act" for u in uses}
            P_pool = lane("P_pool1", ["msA", "rkA", "msB", "rkB", "xb"])
            P_dve = lane("P_dve1", ["ssA", "knA", "ssB", "knB"])
            P_pe = group("P_pe", [u for u in uses if u not in now], now)
            P_act = group("P_act", ["lt", "ct0", "ct1", "q", "kv0", "kv1", "sqA", "kv2", "kv3", "sqB"], now)
        if L0:
            P_pe = lane("P_pe0", uses)
            P_dve = lane("P_dve0", [u for u in uses if owner[u] == "dve"])
            P_act = lane("P_act0", [u for u in uses if owner[u] == "act"])
        X_pe = group("X_pe", [f"s{h}" for h in each_head], [f"t{p}" for p in each_pair], [f"o{p}" for p in each_pair])
        X_dve = group("X_dve", sum([([] if L0 else [f"a{2 * p}", f"a{2 * p + 1}"]) + [f"m{p}"] for p in each_pair], []),
                      [f"r{p}" for p in each_pair], *([[f"t{p}" for p in each_pair]] if L0 else []))
        X_act = group("X_act", [f"e{h}" for h in each_head], [f"o{p}" for p in each_pair],
                      *([] if L0 else [[f"t{p}" for p in each_pair]]))
        X_t = X_dve if L0 else X_act
        X_pool = lane("X_pool" + L, [f"n{h}" for h in each_head])
        Y_pe = lane("Y_pe" + L, ["wo", "xt", "lg", "rk"])
        router = (["lg", "top", "idx", "idf", "hot", "cho", "d", "w0", "w1", "w2", "w3"] if L0 else
                  ["s0", "s1", "gm", "gt", "gi", "gf", "gh", "go", "gk", "msk", "top", "idx", "idf", "hot", "cho",
                   "sum", "rcp", "w2", "w3"])
        Y_dve = lane("Y_dve" + L, ["x1", "stat", "mv", "xm"] + router + ["tok", "slot", "hit", "pos", "posi"])
        Y_act = lane("Y_act" + L, ["xt", "e"])
        Y_pool = lane("Y_pool" + L, ["ve", "rstd"])

        def bank(par, use):
            return psJ[:, ((par + (use in now)) * len(uses) + uses.index(use)) % 2, :]

        def free_bank(eng, b, par, use):
            at, shift = uses.index(use), 0
            while True:
                at -= 2
                if at < 0:
                    at, shift = at + len(uses), shift - 1
                prev = uses[at]
                back = b + shift + (use in now) - (prev in now)
                if not isinstance(back, int) or 0 <= back < B:
                    break
                if back < -1:
                    return
            (P_act if owner[prev] == "act" else P_dve).wait(eng, back, prev)

        def layer_norm(add, src, dst, stt, mvt, rst, dve, pool, names, ready, free=None):
            stat, mvn, ve, rn, done = names

            def d1(v, b):
                ready(v, b)
                dve.post(v.bn_stats(stt[:, :], src), stat)
                dve.wait(v, b, stat)
                settle(v, c)
                dve.post(v.bn_aggr(mvt[:, :], stt[:, :]), mvn)

            def g1(g, b):
                dve.wait(g, b, mvn)
                settle(g, c)
                pool.post(g.tensor_scalar(rst[:, 0:1], mvt[:, 1:2], LN_EPS, 1.0, ALU.add, ALU.mult), ve)
                pool.wait(g, b, ve)
                pool.post(g.tensor_tensor(rst[:, 1:2], rst[:, 0:1], neghalf[0:N, 0:1], ALU.pow), rn)

            def d2(v, b):
                pool.wait(v, b, rn)
                if free:
                    free(v, b)
                dve.post(v.tensor_scalar(dst, src, mvt[:, 0:1], rst[:, 1:2], ALU.subtract, ALU.mult), done)

            add("dve", d1), add("pool", g1), add("dve", d2)

        def p_bias(steps, off, par):
            def g0(g, b):
                ld_x.wait(g, b, "x")
                Y_dve.wait(g, b - 2, "x1")
                P_pool.post(g.tensor_tensor(xb[:, par, :], x[:, par, :], bo[:, :], ALU.add), "xb")
            steps.append(("pool", off, g0))

        def p_norm0(steps, off, par):
            def add(e, fn):
                steps.append((e, off, fn))

            layer_norm(add, x[:, par, :], xn[:, par, :], st, mv, rstd, N_dve, N_pool,
                       ("stat", "mv", "ve", "rstd", "xn"), lambda v, b: ld_x.wait(v, b, "x"))

        def p_k0(steps, off, par, m):
            use = f"k{m}"
            ph = bank(par, use)

            def pe(t, b):
                ld_c.wait(t, b, "c")
                free_bank(t, b, par, use)
                for k in range(2):
                    mm = t.matmul(ph[:, 0:SP], c["wk0"][:, k, m * P:(m + 1) * P], cT[:, par, k, :], start=k == 0, stop=k == 1)
                P_pe.post(mm, use)

            def ac(s, b):
                P_pe.wait(s, b, use)
                P_act.post(s.activation(kT[:, par, m, :], ph[:, 0:SP], ACT.Copy), use)
            steps += [("pe", off, pe), ("act", off, ac)]

        def p_v0(steps, off, par, ch):
            use = f"v{ch}"
            ph = bank(par, use)

            def pe(t, b):
                free_bank(t, b, par, use)
                for k in range(2):
                    mm = t.matmul(ph[0:CH, :], cT[:, par, k, ch * CH:(ch + 1) * CH], c["wv0"][:, k, :], start=k == 0, stop=k == 1)
                P_pe.post(mm, use)

            def dv(v, b):
                P_pe.wait(v, b, use)
                P_dve.post(v.tensor_copy(vv[:, par, ch, :], ph[0:CH, :]), use)
            steps += [("pe", off, pe), ("dve", off, dv)]

        def p_xt0(steps, off, par):
            ph = bank(par, "xt")

            def pe1(t, b):
                N_dve.wait(t, b, "xn")
                free_bank(t, b, par, "xt")
                for k in range(2):
                    mm = t.transpose(ph[:, k * N:(k + 1) * N], xn[:, par, k * P:(k + 1) * P], ident[0:N, 0:N])
                P_pe.post(mm, "xt")

            def ac(s, b):
                P_pe.wait(s, b, "xt")
                P_act.post(s.activation(xT[:, :, :], ph[:, 0:2 * N].rearrange("p (k n) -> p k n", k=2), ACT.Copy), "xt")

            steps += [("pe", off, pe1), ("act", off, ac)]

        def p_q0(steps, off, par):
            pq = bank(par, "q")

            def pe2(t, b):
                P_act.wait(t, b, "xt")
                free_bank(t, b, par, "q")
                for m in range(pairs):
                    for k in range(2):
                        mm = t.matmul(pq[:, m * N:(m + 1) * N], c["wq0"][:, k, m * P:(m + 1) * P], xT[:, k, :],
                                      start=k == 0, stop=k == 1)
                P_pe.post(mm, "q")

            def dv(v, b):
                P_pe.wait(v, b, "q")
                for half in range(2):
                    r = slice(half * DH, (half + 1) * DH)
                    ins = v.tensor_scalar(qz[r, par, half:heads:2, :], pq[r, 0:pairs * N].rearrange("p (m n) -> p m n", m=pairs),
                                          DH ** -0.5, None, ALU.mult)
                P_dve.post(ins, "q")
            steps += [("pe", off, pe2), ("dve", off, dv)]

        def p_norm1(steps, off, par):
            def add(e, fn):
                steps.append((e, off, fn))

            layer_norm(add, x[:, par, :], xn[:, par, :], st, mv, rstd, N_dve, N_pool,
                       ("stat", "mv", "ve", "rstd", "xn"), lambda v, b: ld_x.wait(v, b, "x"))
            layer_norm(add, xn[:, par, :], xl[:, par, :], st, mv, rstd, N_dve, N_pool,
                       ("stat2", "mv2", "ve2", "rstd2", "xl"), lambda v, b: N_dve.wait(v, b, "xn"))

            def d1(v, b):
                ld_c.wait(v, b, "m")
                for j in range(NCH):
                    ins = v.bn_stats(cst[:, j, :], ctx[:, par, j, :])
                N_dve.post(ins, "cstat")
                N_dve.wait(v, b, "cstat")
                settle(v, c)
                for j in range(NCH):
                    ins = v.bn_aggr(cmv[:, j, :], cst[:, j, :])
                N_dve.post(ins, "cmv")

            def g1(g, b):
                N_dve.wait(g, b, "cmv")
                settle(g, c)
                N_pool.post(g.tensor_scalar(crs[:, 0, :], cmv[:, :, 1], LN_EPS, 1.0, ALU.add, ALU.mult), "cve")
                N_pool.wait(g, b, "cve")
                N_pool.post(g.tensor_tensor(crs[:, 1, :], crs[:, 0, :], neghalf[0:CH, 0:NCH], ALU.pow), "crs")
                X_dve.wait(g, b - 2, f"a{heads - 1}")
                settle(g, c)
                N_pool.post(g.tensor_scalar(mb[:, par, CH:CH + S], m8[:, par, :], -NEG, NEG, ALU.mult, ALU.add), "mb")

            def d2(v, b):
                N_pool.wait(v, b, "crs")
                for j in range(NCH):
                    ins = v.tensor_scalar(cn[:, par, j, :], ctx[:, par, j, :], cmv[:, j, 0:1], crs[:, 1, j:j + 1],
                                          ALU.subtract, ALU.mult)
                N_dve.post(ins, "cn")
            add("dve", d1), add("pool", g1), add("dve", d2)

        def p_t1(steps, off, par):
            def pe(t, b):
                N_dve.wait(t, b, "xl")
                free_bank(t, b, par, "lt")
                ph = bank(par, "lt")
                for k in range(2):
                    mm = t.transpose(ph[:, k * N:(k + 1) * N], xl[:, par, k * P:(k + 1) * P], ident[0:N, 0:N])
                P_pe.post(mm, "lt")

            def ac(s, b):
                P_pe.wait(s, b, "lt")
                ph = bank(par, "lt")
                for k in range(2):
                    ins = s.activation(lT[:, k, :], ph[:, k * N:(k + 1) * N], ACT.Identity,
                                       bias=c["lt_b"][:, k:k + 1], scale=c["lt_g"][:, k:k + 1])
                P_act.post(ins, "lt")
            steps += [("pe", off, pe), ("act", off, ac)]
            for k in range(2):
                def pe(t, b, k=k):
                    N_dve.wait(t, b, "cn")
                    free_bank(t, b, par, f"ct{k}")
                    ph = bank(par, f"ct{k}")
                    for j in range(NCH):
                        mm = t.transpose(ph[0:CK, j * CH:(j + 1) * CH], cn[:, par, j, k * CK:(k + 1) * CK], ident[0:CH, 0:CH])
                    P_pe.post(mm, f"ct{k}")

                def ac(s, b, k=k):
                    P_pe.wait(s, b, f"ct{k}")
                    ph = bank(par, f"ct{k}")
                    P_act.post(s.activation(cTn[:, k, :], ph[0:CK, 0:SP], ACT.Identity,
                                            bias=c["cx_b"][:, k:k + 1], scale=c["cx_g"][:, k:k + 1]), f"ct{k}")
                steps += [("pe", off, pe), ("act", off, ac)]

        def p_qkv1(steps, off, par, j):
            use = f"kv{j - 1}" if j else "q"
            ph = bank(par, use)
            latents = j < 2
            rows, cols = N if latents else CH, 2 * I1 if j else I1
            wt = c["wq1"] if j == 0 else c["wlkv1"] if latents else c["wkv1"]

            def pe(t, b):
                free_bank(t, b, par, use)
                P_act.wait(t, b, "lt" if latents else "ct1")
                for k in range(2):
                    lhs = lT[:, k, :] if latents else cTn[:, k, (j - 2) * CH:(j - 1) * CH]
                    mm = t.matmul(ph[0:rows, 0:cols], lhs, wt[:, k, :], start=k == 0, stop=k == 1)
                P_pe.post(mm, use)

            def ac(s, b):
                P_pe.wait(s, b, use)
                P_act.post(s.activation(kv[0:rows, par, j, 0:cols], ph[0:rows, 0:cols], ACT.Copy), use)
            steps += [("pe", off, pe), ("act", off, ac)]

        def p_rms(steps, off, par, part):
            r, n, last = (slice(0, 3), 3, "kv1") if part == "A" else (slice(3, 5), 2, "kv3")
            qk = kv[:, par, r, 0:I1]

            def ac(s, b):
                P_act.wait(s, b, last)
                P_dve.wait(s, b - 1, "ss" + part)
                P_act.post(s.activation(sq[:, r, :], qk, ACT.Square), "sq" + part)

            def d1(v, b):
                P_act.wait(v, b, "sq" + part)
                P_dve.post(v.tensor_reduce(ss[:, r, :], sq[:, r, :].rearrange("p j (h d) -> p j h d", h=H1), AX, ALU.add),
                           "ss" + part)

            def g1(g, b):
                P_dve.wait(g, b, "ss" + part)
                settle(g, c)
                P_pool.post(g.tensor_scalar(rk[:, r, :], ss[:, r, :], 1.0 / DH, RMS_EPS ** 2, ALU.mult, ALU.max), "ms" + part)
                P_pool.wait(g, b, "ms" + part)
                P_pool.post(g.tensor_tensor(rk[:, r, :], rk[:, r, :], neghalf[0:CH, 0:1].unsqueeze(2).to_broadcast([CH, n, H1]),
                                            ALU.pow), "rk" + part)

            def d2(v, b):
                P_pool.wait(v, b, "rk" + part)
                rows = qk.rearrange("p j (h d) -> p j h d", h=H1)
                scale = rk[:, r, :].unsqueeze(3).to_broadcast([CH, n, H1, DH])
                P_dve.post(v.tensor_tensor(rows, rows, scale, ALU.mult), "kn" + part)
            steps += [("act", off, ac), ("dve", off, d1), ("pool", off, g1), ("dve", off, d2)]

        def p_qkt1(steps, off, par):
            def peq(t, b):
                P_dve.wait(t, b, "knA")
                free_bank(t, b, par, "qt")
                ph = bank(par, "qt")
                for k in range(2):
                    mm = t.transpose(ph[:, k * N:(k + 1) * N], kv[0:N, par, 0, k * P:(k + 1) * P], ident[0:N, 0:N])
                P_pe.post(mm, "qt")

            def acq(s, b):
                P_pe.wait(s, b, "qt")
                src = bank(par, "qt")[:, 0:2 * N].rearrange("p (k n) -> p k n", k=2)
                for half in range(2):
                    r = slice(half * DH, (half + 1) * DH)
                    ins = s.activation(qz[r, par, half:heads:2, :], src[r], ACT.Copy, scale=c["qk_s"][r, 0:1])
                P_act.post(ins, "qt")
            steps += [("pe", off, peq), ("act", off, acq)]
            for k in range(2):
                def pe(t, b, k=k):
                    P_dve.wait(t, b, "knB")
                    free_bank(t, b, par, f"kt{k}")
                    ph = bank(par, f"kt{k}")
                    for j in range(nch):
                        mm = t.transpose(ph[:, j * CH:(j + 1) * CH], kv[:, par, 1 + j, k * P:(k + 1) * P], ident[0:CH, 0:CH])
                    P_pe.post(mm, f"kt{k}")

                def ac(s, b, k=k):
                    P_pe.wait(s, b, f"kt{k}")
                    P_act.post(s.activation(kT[:, par, k, :], bank(par, f"kt{k}")[:, 0:keys], ACT.Copy), f"kt{k}")
                steps += [("pe", off, pe), ("act", off, ac)]

        def x_scores(steps, off, par, p):
            def pe(t, b, h):
                if p == 0 and h == 0:
                    if L0:
                        P_dve.wait(t, b, "q")
                    else:
                        P_act.wait(t, b, "qt")
                if not L0 and h == 0:
                    P_act.wait(t, b, f"kt{p}")
                if L0:
                    P_act.wait(t, b, f"k{p}")
                hh = 2 * p + h
                if L0:
                    X_act.wait(t, b if p else b - 1, f"e{(hh - 2) % heads}")
                else:
                    X_dve.wait(t, b if p else b - 1, f"a{(hh - 2) % heads}")
                X_pe.post(t.matmul(psS[0:N, h, 0:keys], qz[:, par, hh, :], kT[:, par, p, :], start=True, stop=True), f"s{hh}")
            q2 = (2 * p) % 4

            def dv(v, b):
                if L0:
                    X_pe.wait(v, b, f"s{2 * p + 1}")
                    X_dve.post(v.tensor_reduce(nm[:, q2:q2 + 2], psS[0:N, :, 0:S], AX, ALU.max, negate=True), f"m{p}")
                    return
                if p == 0:
                    N_pool.wait(v, b, "mb")
                for h in range(2):
                    hh = 2 * p + h
                    X_pe.wait(v, b, f"s{hh}")
                    settle(v, c)
                    X_dve.post(v.tensor_tensor_reduce(prob[:, hh, :], psS[0:N, h, 0:keys], mb[:, par, :], 1.0, -3e38,
                                                      ALU.add, ALU.max, nm[:, hh:hh + 1]), f"a{hh}")
                X_dve.wait(v, b, f"a{2 * p + 1}")
                X_dve.post(v.tensor_scalar(nm[:, q2:q2 + 2], nm[:, q2:q2 + 2], -1.0, None, ALU.mult), f"m{p}")

            def ac(s, b, h):
                hh = 2 * p + h
                q = hh % 4
                X_dve.wait(s, b, f"m{p}")
                if L0:
                    X_pe.wait(s, b if hh >= 4 else b - 1, f"t{(hh - 4) % heads // 2}")
                    src, dst = psS[0:N, h, 0:S], prob[:, q, 0:S]
                else:
                    src = dst = prob[:, q, :]
                X_act.post(s.activation(dst, src, ACT.Exp, bias=nm[:, q:q + 1], accum_out=rs[:, q:q + 1]), f"e{hh}")
            for h in range(2):
                steps.append(("pe", off, lambda t, b, h=h: pe(t, b, h)))
            steps.append(("dve", off, dv))
            for h in range(2):
                steps.append(("act", off, lambda s, b, h=h: ac(s, b, h)))

        def x_norm(steps, off, par, p):
            q2 = (2 * p) % 4

            def dv(v, b):
                X_act.wait(v, b, f"e{2 * p + 1}")
                X_dve.post(v.reciprocal(rc[:, q2:q2 + 2], rs[:, q2:q2 + 2]), f"r{p}")

            def po(g, b):
                X_dve.wait(g, b, f"r{p}")
                settle(g, c)
                for h in range(2):
                    q = q2 + h
                    X_pool.post(g.tensor_scalar(prob[:, q, :], prob[:, q, :], rc[:, q:q + 1], 1.0, ALU.mult, ALU.mult),
                                f"n{2 * p + h}")
            steps += [("dve", off, dv), ("pool", off, po)]

        def x_transpose(steps, off, par, p):
            def pe(t, b):
                for h in range(2):
                    X_pool.wait(t, b, f"n{2 * p + h}")
                    if h == 0:
                        X_t.wait(t, b if p else b - 1, f"t{(p - 1) % pairs}")
                    for j in range(nch):
                        mm = t.transpose(psT[0:CH, h, j * N:(j + 1) * N], prob[:, (2 * p + h) % 4, j * CH:(j + 1) * CH],
                                         ident[0:N, 0:N])
                X_pe.post(mm, f"t{p}")

            def out(e, b):
                X_pe.wait(e, b, f"t{p}")
                dst, src = pT[:, p % 2, :, :, :], psT[0:CH, :, 0:nch * N].rearrange("p h (j n) -> p h j n", j=nch)
                X_t.post(e.tensor_copy(dst, src) if L0 else e.activation(dst, src, ACT.Copy), f"t{p}")
            steps += [("pe", off, pe), ("dve" if L0 else "act", off, out)]

        def x_values(steps, off, par, p):
            def pe(t, b):
                X_t.wait(t, b, f"t{p}")
                if p == 0:
                    if L0:
                        P_dve.wait(t, b, "v2")
                    else:
                        P_act.wait(t, b, "kv3")
                X_act.wait(t, b if p else b - 1, f"o{(p - 1) % pairs}")
                for j in range(nch):
                    mm = t.matmul(psO[:, 0:2 * N], vv[:, par, j, p * P:(p + 1) * P], pT[:, p % 2, :, j, :],
                                  start=j == 0, stop=j == nch - 1)
                X_pe.post(mm, f"o{p}")

            def ac(s, b):
                X_pe.wait(s, b, f"o{p}")
                for half in range(2):
                    r = slice(half * DH, (half + 1) * DH)
                    ins = s.activation(oT[r, p, :], psO[r, half * N:(half + 1) * N], ACT.Copy)
                X_act.post(ins, f"o{p}")
            steps += [("pe", off, pe), ("act", off, ac)]

        def y_out(steps, off, par):
            def pe(t, b):
                X_act.wait(t, b, f"o{pairs - 1}")
                Y_dve.wait(t, b - 1, "slot")
                for p in range(pairs):
                    mm = t.matmul(psY[0:N, 0:D], oT[:, p, :], wo[:, p, :], start=p == 0, stop=p == pairs - 1)
                Y_pe.post(mm, "wo")

            def dv(v, b):
                Y_pe.wait(v, b, "wo")
                P_pool.wait(v, b, "xb")
                st_x.wait(v, b - 2, "xm")
                Y_dve.post(v.scalar_tensor_tensor(x1[:, par, :], psY[0:N, 0:D], tg_x, xb[:, par, :], ALU.mult, ALU.add), "x1")

            steps += [("pe", off, pe), ("dve", off, dv)]
            layer_norm(lambda e, fn: steps.append((e, off, fn)), x1[:, par, :], xm[:, par, :], st1, mv1, rstd1, Y_dve, Y_pool,
                       ("stat", "mv", "ve", "rstd", "xm"), lambda v, b: Y_dve.wait(v, b, "x1"))

        def y_store(steps, off, par):
            def store(s, b):
                st_x.wait(s, b - 1, "xm")
                Y_dve.wait(s, b, "x1")
                settle(s, c)
                s.dma_start(acc[0:TOKENS].rearrange("(b n) d -> b n d", n=N)[b], x1[:, par, :]).then_inc(st_x.sem, 16)
                Y_dve.wait(s, b, "xm")
                settle(s, c)
                s.dma_start(xn_rows[0:TOKENS].rearrange("(b n) d -> b n d", n=N)[b], xm[:, par, :]).then_inc(st_x.sem, 16)
            steps.append(("sp", off, store))

        def y_transpose(steps, off, par):
            def pe(t, b):
                Y_dve.wait(t, b, "xm")
                for k in range(2):
                    mm = t.transpose(psY[:, k * N:(k + 1) * N], xm[:, par, k * P:(k + 1) * P], ident[0:N, 0:N])
                Y_pe.post(mm, "xt")

            def ac(s, b):
                Y_pe.wait(s, b, "xt")
                Y_act.post(s.activation(xmT[:, :, :], psY[:, 0:2 * N].rearrange("p (k n) -> p k n", k=2), ACT.Copy), "xt")
            steps += [("pe", off, pe), ("act", off, ac)]

        def y_route(steps, off, par):
            def pe(t, b):
                Y_act.wait(t, b, "xt")
                for k in range(2):
                    mm = t.matmul(psY[0:N, 0:experts_n], xmT[:, k, :], wr[:, k, :], start=k == 0, stop=k == 1)
                Y_pe.post(mm, "lg")

            def seq(v, b, ins, name):
                Y_dve.post(ins, name)
                Y_dve.wait(v, b, name)
                if name in ("lg", "top", "gm", "gt", "msk"):
                    settle(v, c)

            def one_hot(v, b, dst, idx_f, n, m, name):
                seq(v, b, v.tensor_tensor(dst, c["iota"][:, 0:m].unsqueeze(1).to_broadcast([N, n, m]),
                                          idx_f.unsqueeze(2).to_broadcast([N, n, m]), ALU.is_equal), name)

            w = slot_w[:, par, 0:topk]
            values = sc[:, 0, 0:experts_n]

            def pick(v, b, src):
                seq(v, b, v.max(top_v[:, :], src), "top")
                seq(v, b, v.max_index(top_i[:, :], top_v[:, :], src), "idx")
                seq(v, b, v.tensor_copy(top_f[:, 0:topk], top_i[:, 0:topk]), "idf")
                one_hot(v, b, hot[:, 0:topk, 0:experts_n], top_f[:, 0:topk], topk, experts_n, "hot")
                seq(v, b, v.tensor_reduce(chosen[:, 0:experts_n], hot[:, 0:topk, 0:experts_n].rearrange("p k e -> p e k"),
                                          AX, ALU.add), "cho")

            def dv0(v, b):
                Y_pe.wait(v, b, "lg")
                seq(v, b, v.tensor_copy(values, psY[0:N, 0:experts_n]), "lg")
                pick(v, b, values)
                seq(v, b, v.tensor_tensor(tmp[:, 0:1], top_v[:, 1:2], top_v[:, 0:1], ALU.subtract), "d")

            def ac0(s, b):
                Y_dve.wait(s, b, "d")
                Y_act.post(s.activation(tmp[:, 1:2], tmp[:, 0:1], ACT.Exp), "e")

            def weights0(v, b):
                Y_act.wait(v, b, "e")
                seq(v, b, v.tensor_scalar(tmp[:, 2:3], tmp[:, 1:2], 1.0, None, ALU.add), "w0")
                seq(v, b, v.reciprocal(tmp[:, 3:4], tmp[:, 2:3]), "w1")
                st_s.wait(v, b - 2, f"k{topk - 1}")
                seq(v, b, v.tensor_scalar(w[:, 0:1], tmp[:, 3:4], tg_f, None, ALU.mult), "w2")
                seq(v, b, v.tensor_scalar(w[:, 1:2], w[:, 0:1], tmp[:, 1:2], None, ALU.mult), "w3")

            def ac1(s, b):
                Y_pe.wait(s, b, "lg")
                Y_act.post(s.activation(sc[:, 1, :], psY[0:N, 0:E1], ACT.Exp, scale=-1.0), "e")

            def dv1(v, b):
                Y_act.wait(v, b, "e")
                seq(v, b, v.tensor_scalar(sc[:, 2, :], sc[:, 1, :], 1.0, None, ALU.add), "s0")
                seq(v, b, v.reciprocal(values, sc[:, 2, :]), "s1")
                grouped = values.rearrange("p (g e) -> p g e", g=GROUPS)
                seq(v, b, v.tensor_reduce(gmax[:, 0:GROUPS], grouped, AX, ALU.max), "gm")
                seq(v, b, v.max(gtop[:, :], gmax[:, :]), "gt")
                seq(v, b, v.max_index(gidx[:, :], gtop[:, :], gmax[:, :]), "gi")
                seq(v, b, v.tensor_copy(gidf[:, :], gidx[:, 0:TOPG]), "gf")
                one_hot(v, b, ghot[:, :, :], gidf[:, :], TOPG, GROUPS, "gh")
                seq(v, b, v.tensor_reduce(gok[:, :], ghot[:, :, :].rearrange("p k g -> p g k"), AX, ALU.add), "go")
                seq(v, b, v.tensor_scalar(gok[:, :], gok[:, :], 2.0, -2.0, ALU.mult, ALU.add), "gk")
                seq(v, b, v.tensor_tensor(sc[:, 1, :].rearrange("p (g e) -> p g e", g=GROUPS), grouped,
                                          gok[:, :].unsqueeze(2).to_broadcast([N, GROUPS, E1 // GROUPS]), ALU.add), "msk")
                pick(v, b, sc[:, 1, :])
                seq(v, b, v.tensor_reduce(tmp[:, 0:1], top_v[:, 0:topk], AX, ALU.add), "sum")
                seq(v, b, v.reciprocal(tmp[:, 1:2], tmp[:, 0:1]), "rcp")
                st_s.wait(v, b - 2, f"k{topk - 1}")
                seq(v, b, v.tensor_scalar(w, top_v[:, 0:topk], tmp[:, 1:2], ROUTE_SCALE, ALU.mult, ALU.mult), "w2")
                seq(v, b, v.tensor_scalar(w, w, tg_f, None, ALU.mult), "w3")
            steps.append(("pe", off, pe))
            if L0:
                steps += [("dve", off, dv0), ("act", off, ac0), ("dve", off, weights0)]
            else:
                steps += [("act", off, ac1), ("dve", off, dv1)]

        def y_dispatch(steps, off, par):
            def pe(t, b):
                Y_dve.wait(t, b, "cho")
                t.matmul(psY[0:N, 0:experts_n], c["before"][:, :], chosen[:, 0:experts_n], start=True, stop=True)
                Y_pe.post(t.matmul(psY[0:N, 2 * E1:2 * E1 + experts_n], c["ones"][:, :], chosen[:, 0:experts_n],
                                   start=True, stop=True, skip_group_check=True), "rk")

            def dv(v, b):
                base = c["base"][:, 0:experts_n]
                Y_pe.wait(v, b, "rk")
                v.tensor_tensor(slot_of[:, 0:experts_n], psY[0:N, 0:experts_n], base, ALU.add)
                Y_dve.post(v.tensor_scalar(slot[:, par, 0:topk, 0], c["token"][:, 0:1].to_broadcast([N, topk]), 0.0, None,
                                           ALU.add), "tok")
                Y_dve.wait(v, b, "tok")
                v.tensor_scalar(c["token"][:, :], c["token"][:, :], float(N), None, ALU.add)
                Y_dve.post(v.tensor_tensor(base, psY[0:N, 2 * E1:2 * E1 + experts_n], base, ALU.add), "slot")
                Y_dve.wait(v, b, "slot")
                Y_dve.post(v.tensor_tensor(hit[:, 0:topk, 0:experts_n], hot[:, 0:topk, 0:experts_n],
                                           slot_of[:, 0:experts_n].unsqueeze(1).to_broadcast([N, topk, experts_n]), ALU.mult), "hit")
                Y_dve.wait(v, b, "hit")
                Y_dve.post(v.tensor_reduce(pos_f[:, 0:topk], hit[:, 0:topk, 0:experts_n], AX, ALU.add), "pos")
                Y_dve.wait(v, b, "pos")
                Y_dve.post(v.tensor_copy(pos[:, par, 0:topk], pos_f[:, 0:topk]), "posi")

            def po(g, b):
                Y_dve.wait(g, b, "posi")
                st_s.wait(g, b - 1, f"k{topk - 1}")
                settle(g, c)
                for k in range(topk):
                    g.indirect_dma_start(table, bass.IndirectOffsetOnAxis(pos[:, par, k:k + 1], 0), slot[:, par, k, :], None)\
                        .then_inc(st_s.sem, 16)
            steps += [("pe", off, pe), ("dve", off, dv), ("pool", off, po)]

        def load_x(steps, off, par):
            def sp(s, b):
                P_pool.wait(s, b - 2, "xb")
                N_dve.wait(s, b - 2, "xn")
                ld_x.wait(s, b - 1, "x")
                settle(s, c)
                src = a["x"][b] if L0 else dram["acc0"][0:TOKENS].rearrange("(b n) d -> b n d", n=N)[b]
                s.dma_start(x[:, par, :], src).then_inc(ld_x.sem, 16)
            steps.append(("sp", off, sp))

        def load_c(steps, off, par):
            def sp(s, b):
                if L0:
                    P_pe.wait(s, b - 2, "v2")
                    ld_c.wait(s, b - 1, "c")
                    settle(s, c)
                    s.dma_start(cT[:, par, :, 0:S], a["ctxT"][b].rearrange("(k p) s -> p k s", p=CK)).then_inc(ld_c.sem, 16)
                    return
                P_pe.wait(s, b - 2, "ct1")
                settle(s, c)
                N_pool.wait(s, b - 2, "mb")
                ld_c.wait(s, b - 1, "m")
                settle(s, c)
                rows = a["ctx_768"][b]
                s.dma_start(ctx[:, par, 0:2, :], rows[0:2 * CH].rearrange("(j p) c -> p j c", p=CH)).then_inc(ld_c.sem, 16)
                s.dma_start(ctx[0:S - 2 * CH, par, 2, :], rows[2 * CH:S]).then_inc(ld_c.sem, 16)
                s.dma_start(m8[:, par, :], a["mask"][b].partition_broadcast(N)).then_inc(ld_c.sem, 16)
            steps.append(("sp", off, sp))

        def project(steps, off, par, part):
            for f, *args in ([[(p_xt0,), (p_k0, 0), (p_k0, 1)], [(p_q0,)], [(p_bias,), (p_k0, 2), (p_k0, 3), (p_v0, 0)],
                              [(p_v0, 1), (p_v0, 2)]] if L0 else
                             [[(p_t1,), (p_qkv1, 0), (p_qkv1, 1), (p_qkv1, 2), (p_rms, "A"), (p_qkv1, 3), (p_qkv1, 4),
                               (p_rms, "B"), (p_bias,)]])[part]:
                f(steps, off, par, *args)
        p_norm = p_norm0 if L0 else p_norm1

        def prologue():
            steps = []
            for b in range(3):
                load_x(steps, b, b % 2)
                load_c(steps, b, b % 2)
            p_norm(steps, 0, 0)
            for part in range(pairs if L0 else 1):
                project(steps, 0, 0, part)
            if L0:
                x_scores(steps, 0, 0, 0)
            p_norm(steps, 1, 1)
            return steps

        def iteration(i, par):
            par %= 2
            nxt, nx2, nx3 = (i is None or i + k < B for k in (1, 2, 3))
            prv = i is None or i > 0
            steps = []

            def last(fn):
                if prv:
                    fn(steps, -1, 1 - par)

            def scores(p):
                if p < pairs:
                    x_scores(steps, 0, par, p)
                elif nxt:
                    x_scores(steps, 1, 1 - par, 0)

            def values(p):
                if p >= 0:
                    x_values(steps, 0, par, p)
                elif prv:
                    x_values(steps, -1, 1 - par, pairs - 1)

            if nx3:
                load_x(steps, 3, 1 - par)
            if L0:
                for p in range(pairs):
                    x_norm(steps, 0, par, p)
                    if nxt:
                        project(steps, 1, 1 - par, p)
                    if p == 1:
                        last(y_out)
                    if p == 3:
                        last(y_transpose)
                    scores(p + 1)
                    if p == 3:
                        last(y_route)
                    values(p - 1)
                    x_transpose(steps, 0, par, p)
                    if p == 2 and nx2:
                        p_norm(steps, 2, par)
                last(y_dispatch)
            else:
                def made(ok, fn, off, half, *args):
                    got = []
                    if ok:
                        fn(got, off, half, *args)
                    return {e: [x for x in got if x[0] == e] for e in ("pe", "dve", "act", "pool")}
                s0, s1 = (made(True, x_scores, 0, par, p) for p in range(2))
                n0, n1 = (made(True, x_norm, 0, par, p) for p in range(2))
                t0, t1 = (made(True, x_transpose, 0, par, p) for p in range(2))
                v0, v1 = made(True, x_values, 0, par, 0), made(prv, x_values, -1, 1 - par, 1)
                tr = made(nxt, p_t1, 1, 1 - par)
                q, kv0, kv1, kv2, kv3 = (made(nxt, p_qkv1, 1, 1 - par, j) for j in range(nch + 1))
                ra, rb = (made(nxt, p_rms, 1, 1 - par, part) for part in "AB")
                xbias, kt = made(nxt, p_bias, 1, 1 - par), made(True, p_qkt1, 0, par)
                norm = made(nx2, p_norm, 2, par)
                yo, yt, yr, yd = (made(prv, fn, -1, 1 - par) for fn in (y_out, y_transpose, y_route, y_dispatch))

                for stage in (v1, tr, kt, yo, s0, q, kv0, s1, yt, kv1, yr, t0, kv2, kv3, v0, t1, yd):
                    steps += stage["pe"]
                for stage in (v1, tr, kt, q, s0, kv0, yt, s1, kv1, yr, ra, t0, kv2, kv3, rb, v0, t1):
                    steps += stage["act"]
                nd, rad, rbd, yod = norm["dve"], ra["dve"], rb["dve"], yo["dve"]
                for part in (yod[:2], s0["dve"], yod[2:], n0["dve"], nd[:1], s1["dve"], nd[1:3], n1["dve"], rad[:1],
                             yr["dve"], rad[1:], nd[3:5], rbd[:1], nd[5:], rbd[1:], yd["dve"]):
                    steps += part
                ng = norm["pool"]
                for part in (yo["pool"], n0["pool"], ng[:1], n1["pool"], ng[1:2], ra["pool"], ng[2:], rb["pool"],
                             xbias["pool"], yd["pool"]):
                    steps += part
            last(y_store)
            if nx3:
                load_c(steps, 3, 1 - par)
            if i == B - 3:
                steps.append(("sp", 0, lambda s, b: c.update({f"n_w{layer}": load_expert_weights(s, a, c, layer)})))
            return steps

        def epilogue():
            steps = []
            last = (B - 1) % 2
            x_values(steps, -1, last, pairs - 1)
            for f in (y_out, y_store, y_transpose, y_route, y_dispatch):
                f(steps, -1, last)
            return steps

        def rounds(name, eng):
            run_rounds(name, eng, prologue(), iteration, epilogue(), B, 2, 3, 3)

        with nc.Block() as block:

            @block.sync
            def _(s):
                init.wait(s, 0, "i")
                rounds("sp", s)
                s.wait_ge(st_x.sem, B * 32)

            @block.scalar
            def _(s):
                init.wait(s, 0, "i")
                rounds("act", s)

            @block.vector
            def _(v):
                v.memset(qz[:, :, :, :], 0.0)
                v.memset(prob[:, :, :], 0.0)
                for e in range(experts_n):
                    v.memset(c["base"][:, e:e + 1], float(e * REGION))
                if L0:
                    v.memset(cT[:, :, :, :], 0.0)
                else:
                    v.memset(ctx[:, :, :, :], 0.0)
                    v.memset(mb[:, :, 0:N], 0.0)
                    v.memset(mb[:, :, N:CH], NEG)
                    v.memset(mb[:, :, CH + S:K1], NEG)
                    v.memset(gmax[:, :], -1.0)
                    v.tensor_scalar(c["token"][:, :], c["token"][:, :], float(-TOKENS), None, ALU.add)
                init.post(v.memset((vv if L0 else kv)[:, :, :, :], 0.0), "i")
                init.wait(v, 0, "i")
                rounds("dve", v)

            @block.tensor
            def _(t):
                init.wait(t, 0, "i")
                rounds("pe", t)

            @block.gpsimd
            def _(g):
                init.wait(g, 0, "i")
                rounds("pool", g)
                g.wait_ge(st_s.sem, B * topk * 16)

        for g in (N_dve, N_pool, P_dve, P_act, P_pool, P_pe, X_pool, Y_pe, Y_dve, Y_act, Y_pool, X_pe, X_dve, X_act):
            for l in g.lanes if isinstance(g, Group) else [g]:
                assert l.seen % len(l.events) == 0, l.events


def experts(nc, maker, a, dram, c, layer):
    L0 = layer == 0
    L = str(layer)
    E, topk, F = (E0, TOP0, F0) if L0 else (E1, TOP1, F1)
    NT = most_tiles(E, topk)
    table, acc, xn_rows = dram[f"table{layer}"], dram[f"acc{layer}"], dram[f"xn{layer}"]
    ident = c["ident"]
    w = c["expert_w"]
    w13 = w[:, 0:E * 4 * F].rearrange("p (e k f) -> p e k f", e=E, k=2)
    w2 = w[:, E * 4 * F:E * 4 * F + E * (F // P) * D].rearrange("p (e k d) -> p e k d", e=E, k=F // P)
    KF = F // P
    LOOK = 2
    NTX = NT + LOOK + 1
    RING = 8
    stack = ExitStack()
    with stack:
        sb, ps, lane = maker(stack)
        psX = ps("psX" + L, [P, 512])
        psG = ps("psG" + L, [P, 2, 512])
        psU = ps("psU" + L, [P, 2, 512])
        psH = ps("psH" + L, [P, 512])
        psD = ps("psD" + L, [P, 2, 512])
        slots = sb("slots" + L, [P, RING, 2], I32)
        slot_w = slots[:, :, 1].bitcast(F32)
        xg = sb("xg" + L, [P, 4, D])
        xT = sb("xgT" + L, [P, 2, 2, P])
        gate = sb("gate" + L, [P, 2, F])
        hid = sb("hid" + L, [P, 2, F])
        hT = sb("hT" + L, [P, 2, KF, P])
        y = sb("y" + L, [P, 2, D])
        f = sb("tilef" + L, [1, 4, E])
        fi = sb("tilei" + L, [1, 2, E], I32)
        ge = sb("tilege" + L, [1, NTX, E])
        jj = sb("tilej" + L, [1, NTX])
        tf = sb("tilet" + L, [1, 3, NTX])
        tile_e = sb("tile_e" + L, [1, NTX], I32)
        tile_r = sb("tile_r" + L, [1, NTX], I32)
        if not L0:
            bias = sb("bias1", [P, E, 3, F])
            pre = sb("pre1", [P, 2, 2 * F])
            yb = sb("yb1", [P, 2, D])

        setup_d = lane("tile_d" + L, ["n", "i", "sh", "f", "cum", "ge", "e", "tb", "tbs", "tr", "tr2", "row", "done"])
        setup_p = lane("tile_p" + L, ["j"])
        cum = lane("tile_c" + L, ["e"])
        ld_s = [lane(f"ld_s{q}_{L}", ["s"], 16).sem for q in range(4)]
        ga = lane("ga" + L, ["g"], 16)
        sc = lane("sc" + L, ["s"], 16)
        ld_b = lane("ld_b" + L, ["b"], 16)
        pe_tx, pe_g, pe_u, pe_th, pe_o = (lane(f"pe_{n}{L}", [n]) for n in ("tx", "g", "u", "th", "o"))
        act_xt, act_g, act_h = (lane(f"act_{n}{L}", [n]) for n in ("xt", "g", "h"))
        dve_h = lane("dve_h" + L, ["h"] if L0 else ["pre", "h"])
        dve_y = lane("dve_y" + L, ["y"] if L0 else ["yb", "y"])

        def slots_loaded(eng, j, r):
            eng.wait_ge(ld_s[r % 4], (j - r % 4) * 4 + 16)

        def gather(steps, off, r):
            def po(g, j):
                slots_loaded(g, j, r)
                pe_tx.wait(g, j - 4, "tx")
                ga.wait(g, j - 1, "g")
                settle(g, c)
                g.indirect_dma_start(xg[:, r % 4, :], None, xn_rows, bass.IndirectOffsetOnAxis(slots[:, r, 0:1].bitcast(U32), 0))\
                    .then_inc(ga.sem, 16)
            steps.append(("pool", off, po))

        def tx(steps, off, r):
            def t1(t, j):
                ga.wait(t, j, "g")
                act_xt.wait(t, j - 1, "xt")
                for k in range(2):
                    mm = t.transpose(psX[:, k * P:(k + 1) * P], xg[:, r % 4, k * P:(k + 1) * P], ident[:, :])
                pe_tx.post(mm, "tx")

            def a1(s, j):
                pe_tx.wait(s, j, "tx")
                pe_g.wait(s, j - 2, "g") if not L0 else pe_u.wait(s, j - 2, "u")
                act_xt.post(s.activation(xT[:, r % 2, :, :], psX[:, 0:2 * P].rearrange("p (k n) -> p k n", k=2), ACT.Copy), "xt")
            steps += [("pe", off, t1), ("act", off, a1)]

        def expert_of(t, j):
            return t.value_load(tile_e[0:1, bass.ds(j, 1)], min_val=0, max_val=E - 1)

        def up(steps, off, r, part):
            pst, lan = ((psG, pe_g), (psU, pe_u))[part]

            def t1(t, j):
                act_xt.wait(t, j, "xt")
                if L0:
                    (act_g if part == 0 else dve_h).wait(t, j - 2, "g" if part == 0 else "h")
                else:
                    dve_h.wait(t, j - 2, "pre")
                settle(t, c)
                e = expert_of(t, j)
                for k in range(2):
                    mm = t.matmul(pst[:, r % 2, :], xT[:, r % 2, k, :], w13[:, bass.ds(e, 1), k, part * 512:(part + 1) * 512],
                                  start=k == 0, stop=k == 1)
                lan.post(mm, "gu"[part])
            steps.append(("pe", off, t1))
            if L0 and part == 0:
                def a1(s, j):
                    pe_g.wait(s, j, "g")
                    dve_h.wait(s, j - 2, "h")
                    act_g.post(s.activation(gate[:, r % 2, :], psG[:, r % 2, :], ACT.Silu), "g")
                steps.append(("act", off, a1))
            elif L0:
                def d1(v, j):
                    pe_u.wait(v, j, "u")
                    act_g.wait(v, j, "g")
                    pe_th.wait(v, j - 2, "th")
                    dve_h.post(v.tensor_tensor(hid[:, r % 2, :], psU[:, r % 2, :], gate[:, r % 2, :], ALU.mult), "h")
                steps.append(("dve", off, d1))
            else:
                def d0(v, j):
                    pe_g.wait(v, j, "g")
                    settle(v, c)
                    e = v.value_load(tile_e[0:1, bass.ds(j, 1)], min_val=0, max_val=E - 1)
                    dve_h.post(v.tensor_tensor(pre[:, r % 2, :], psG[:, r % 2, :],
                                               bias[:, bass.ds(e, 1), 0:2, :].rearrange("p e k f -> p (e k f)"), ALU.add), "pre")

                def a1(s, j):
                    dve_h.wait(s, j, "pre")
                    act_g.post(s.activation(gate[:, r % 2, :], pre[:, r % 2, 0:F], ACT.Silu), "g")

                def d1(v, j):
                    act_g.wait(v, j, "g")
                    pe_th.wait(v, j - 2, "th")
                    dve_h.post(v.tensor_tensor(hid[:, r % 2, :], pre[:, r % 2, F:2 * F], gate[:, r % 2, :], ALU.mult), "h")
                steps += [("dve", off, d0), ("act", off, a1), ("dve", off, d1)]

        def th(steps, off, r):
            def t1(t, j):
                dve_h.wait(t, j, "h")
                act_h.wait(t, j - 1, "h")
                for k in range(KF):
                    mm = t.transpose(psH[:, k * P:(k + 1) * P], hid[:, r % 2, k * P:(k + 1) * P], ident[:, :])
                pe_th.post(mm, "th")

            def a1(s, j):
                pe_th.wait(s, j, "th")
                pe_o.wait(s, j - 2, "o")
                act_h.post(s.activation(hT[:, r % 2, :, :], psH[:, 0:F].rearrange("p (k n) -> p k n", k=KF), ACT.Copy), "h")
            steps += [("pe", off, t1), ("act", off, a1)]

        def down(steps, off, r):
            def t1(t, j):
                act_h.wait(t, j, "h")
                dve_y.wait(t, j - 2, "y" if L0 else "yb")
                settle(t, c)
                e = expert_of(t, j)
                for k in range(KF):
                    mm = t.matmul(psD[:, r % 2, 0:D], hT[:, r % 2, k, :], w2[:, bass.ds(e, 1), k, :], start=k == 0, stop=k == KF - 1)
                pe_o.post(mm, "o")

            def d1(v, j):
                pe_o.wait(v, j, "o")
                src = psD[:, r % 2, 0:D]
                if not L0:
                    settle(v, c)
                    e = v.value_load(tile_e[0:1, bass.ds(j, 1)], min_val=0, max_val=E - 1)
                    dve_y.post(v.tensor_tensor(yb[:, r % 2, :], src, bias[:, bass.ds(e, 1), 2, :].rearrange("p e f -> p (e f)"),
                                               ALU.add), "yb")
                    dve_y.wait(v, j, "yb")
                    src = yb[:, r % 2, :]
                sc.wait(v, j - 2, "s")
                dve_y.post(v.tensor_scalar(y[:, r % 2, :], src, slot_w[:, r:r + 1], None, ALU.mult), "y")

            def po(g, j):
                dve_y.wait(g, j, "y")
                sc.wait(g, j - 1, "s")
                settle(g, c)
                g.indirect_dma_start(acc, bass.IndirectOffsetOnAxis(slots[:, r, 0:1].bitcast(U32), 0), y[:, r % 2, :], None,
                                     compute_op=ALU.add).then_inc(sc.sem, 16)
            steps += [("pe", off, t1), ("dve", off, d1), ("pool", off, po)]

        def prologue():
            steps = []
            gather(steps, 0, 0)
            gather(steps, 1, 1)
            tx(steps, 0, 0)
            return steps

        def iteration(i, r):
            def made(ok, fn, off, *args):
                got = []
                if ok:
                    fn(got, off, (r + off) % RING, *args)
                return {e: [x for x in got if x[0] == e] for e in ("pe", "dve", "act", "pool")}
            ga, x = made(True, gather, 2), made(True, tx, 1)
            u0, u1 = made(True, up, 0, 0), made(L0, up, 0, 1)
            h, d = made(i is None or i > 0, th, -1), made(i is None or i > 1, down, -2)
            pe = (u0, d, x, u1, h) if L0 else (u0, x, d, h)
            act = (x, u0, h)
            steps = [st for part in pe for st in part["pe"]] + [st for part in act for st in part["act"]]
            steps += [st for part in (u0, u1, d) for st in part["dve"]] + ga["pool"] + d["pool"]
            return steps

        def epilogue():
            steps = []
            down(steps, -2, (NT - 2) % RING)
            th(steps, -1, (NT - 1) % RING)
            down(steps, -1, (NT - 1) % RING)
            return steps

        head = 4 + (NT - 4) % RING

        def rounds(name, eng):
            run_rounds(name, eng, prologue(), iteration, epilogue(), NT, RING, head, 0)

        with nc.Block() as block:

            @block.gpsimd
            def _(g):
                setup_p.post(g.iota(jj[:, :], [[1, NTX]], base=0, channel_multiplier=0, allow_small_or_imprecise_dtypes=True), "j")
                rounds("pool", g)
                g.wait_ge(sc.sem, 16 * NT)
                g.wait_ge(ga.sem, 16 * (NT + LOOK))

            @block.vector
            def _(v):
                def seq(ins, name):
                    setup_d.post(ins, name)
                    setup_d.wait(v, 0, name)
                base = c["base"][0:1, 0:E]
                for e in range(E):
                    ins = v.tensor_scalar(f[:, 0, e:e + 1], base[:, e:e + 1], float(P - 1 - e * REGION), None, ALU.add)
                seq(ins, "n")
                seq(v.tensor_copy(fi[:, 0, :], f[:, 0, :]), "i")
                seq(v.tensor_scalar(fi[:, 1, :], fi[:, 0, :], 7, None, ALU.arith_shift_right), "sh")
                seq(v.tensor_copy(f[:, 1, :], fi[:, 1, :]), "f")
                seq(v.tensor_copy(f[:, 2, 0:1], f[:, 1, 0:1]), "cum")
                for e in range(1, E):
                    v.tensor_tensor(f[:, 2, e:e + 1], f[:, 2, e - 1:e], f[:, 1, e:e + 1], ALU.add).then_inc(cum.sem, 1)
                    v.wait_ge(cum.sem, e)
                setup_p.wait(v, 0, "j")
                seq(v.tensor_tensor(ge[:, :, :], jj[:, :].unsqueeze(2).to_broadcast([1, NTX, E]),
                                    f[:, 2, :].unsqueeze(1).to_broadcast([1, NTX, E]), ALU.is_ge), "ge")
                seq(v.tensor_reduce(tf[:, 0, :], ge[:, :, :], AX, ALU.add), "e")
                seq(v.tensor_tensor(ge[:, :, :], ge[:, :, :], f[:, 1, :].unsqueeze(1).to_broadcast([1, NTX, E]), ALU.mult), "tb")
                seq(v.tensor_reduce(tf[:, 1, :], ge[:, :, :], AX, ALU.add), "tbs")
                seq(v.tensor_tensor(tf[:, 2, :], jj[:, :], tf[:, 1, :], ALU.subtract), "tr")
                seq(v.tensor_scalar(tf[:, 2, :], tf[:, 2, :], float(P), None, ALU.mult), "tr2")
                seq(v.scalar_tensor_tensor(tf[:, 1, :], tf[:, 0, :], float(REGION), tf[:, 2, :], ALU.mult, ALU.add), "row")
                v.tensor_copy(tile_r[:, :], tf[:, 1, :])
                seq(v.tensor_scalar(tile_e[:, :], tf[:, 0, :], float(E - 1), None, ALU.min), "done")
                if not L0:
                    v.wait_ge(ld_b.sem, 16 * 3)
                rounds("dve", v)

            @block.sync
            def _(s):
                if not L0:
                    for k, n in enumerate(("b1", "b3", "b2")):
                        s.dma_start(bias[:, :, k, :], a[f"L1_ffn_{n}"].partition_broadcast(P)).then_inc(ld_b.sem, 16)
                setup_d.wait(s, 0, "done")

                def load(j, r):
                    sc.wait(s, j - RING, "s")
                    settle(s, c)
                    if not isinstance(j, int) or j >= 4:
                        slots_loaded(s, j - 4, r)
                    settle(s, c)
                    row = s.value_load(tile_r[0:1, bass.ds(j, 1)], min_val=0, max_val=table.shape[0] - P)
                    s.dma_start(slots[:, r, :], table[bass.ds(row, P), :]).then_inc(ld_s[r % 4], 16)
                total = NT + LOOK
                first = RING + total % RING
                for j in range(first):
                    load(j, j % RING)
                with s.Fori(first, total - RING + 1, RING) as j:
                    for k in range(RING):
                        load(j + k, (first + k) % RING)

            @block.scalar
            def _(s):
                rounds("act", s)

            @block.tensor
            def _(t):
                t.wait_ge(c[f"x{layer}_ready"].sem, 16 * c[f"n_w{layer}"])
                setup_d.wait(t, 0, "done")
                rounds("pe", t)


_SAME = ["x", "ctx_768", "g_xattn", "g_ffn", "L0_xattn_Wq", "L0_xattn_Wk", "L0_xattn_Wv", "L0_xattn_Wo", "L0_xattn_bo",
         "L0_ffn_moe_router", "L0_ffn_moe_w13", "L0_ffn_moe_w2", "L1_xattn_ln_x_g", "L1_xattn_ln_x_b",
         "L1_xattn_ln_l_g", "L1_xattn_ln_l_b", "L1_xattn_qn_g", "L1_xattn_kn_g", "L1_xattn_bo",
         "L1_ffn_b1", "L1_ffn_b2", "L1_ffn_b3"]


def kernel(**inputs):
    import numpy as _np
    import concourse.bacc as _bacc
    from concourse import mybir as _mybir
    from concourse.bass_utils import run_bass_kernel_spmd as _run

    i = {k: _np.asarray(v) for k, v in inputs.items()}
    laid = {n: i[n] for n in _SAME}
    laid["ctxT"] = i["ctx_768"].transpose(0, 2, 1)
    laid["mask"] = i["mask_BxS2_bk0"]
    for n in ("L1_xattn_Wq", "L1_xattn_Wkv", "L1_xattn_Wlkv", "L1_xattn_Wo", "L1_ffn_Wg"):
        laid[n + "T"] = i[n].T
    for n in ("L1_ffn_W1", "L1_ffn_W2", "L1_ffn_W3"):
        laid[n + "T"] = i[n].transpose(0, 2, 1)
    laid = {n: _np.ascontiguousarray(v) for n, v in laid.items()}

    nc = _bacc.Bacc("TRN2", target_bir_lowering=False, num_devices=1)
    args = {n: nc.dram_tensor(f"in_{n}", v.shape, _mybir.dt.from_np(v.dtype), kind="ExternalInput").ap()
            for n, v in laid.items()}
    out = nc.dram_tensor("out", (TOKENS + SPARE, D), F32, kind="ExternalOutput").ap()
    build(nc, args, out)
    r = _run(nc, [{f"in_{n}": v for n, v in laid.items()}], core_ids=[0])
    return r.results[0]["out"][0:TOKENS].reshape(B, N, D)
```

```python
from contextlib import ExitStack

import numpy as np

import concourse.bass as bass
from concourse import mybir

F32 = mybir.dt.float32
F32R = mybir.dt.float32r
I32 = mybir.dt.int32
U32 = mybir.dt.uint32
U8 = mybir.dt.uint8
ALU = mybir.AluOpType
ACT = mybir.ActivationFunctionType
AX = mybir.AxisListType.X

B, N, D = 32, 100, 256
S, C = 361, 192
TOKENS = B * N
P = 128
SPARE = P
CH = 121
NCH = 3
SP = CH * NCH
CK = 96
H0, H1, DH = 8, 4, 64
I0, I1 = H0 * DH, H1 * DH
K1 = CH + SP
REGION = TOKENS
E0, TOP0, F0 = 8, 2, 512
E1, TOP1, F1 = 16, 4, 256
GROUPS, TOPG = 4, 2
ROUTE_SCALE = 2.5
LN_EPS = 1e-5
RMS_EPS = 1e-8
NEG = -1e30


def most_tiles(experts, top):
    return (TOKENS * top + experts * (P - 1)) // P


class Lane:

    def __init__(self, sem, events, step=1):
        self.sem, self.events, self.step = sem, list(events), step
        self.seen = 0
        assert len(set(self.events)) == len(self.events)

    def post(self, ins, event):
        assert self.events[self.seen % len(self.events)] == event, (self.sem, event, self.seen)
        self.seen += 1
        ins.then_inc(self.sem, self.step)

    def wait(self, eng, rnd, event):
        k = (self.events.index(event) + 1) * self.step
        value = rnd * (len(self.events) * self.step) + k
        if isinstance(value, int) and value <= 0:
            return
        eng.wait_ge(self.sem, value)


class Group:

    def __init__(self, lanes):
        self.lanes = lanes
        self.of = {e: l for l in lanes for e in l.events}

    def post(self, ins, event):
        self.of[event].post(ins, event)

    def wait(self, eng, rnd, event):
        self.of[event].wait(eng, rnd, event)


def settle(eng, c):
    eng.sem_inc(c["settled"], 1)


def emit(steps, name, eng, base):
    for engine, off, fn in steps:
        if engine == name:
            fn(eng, base + off)


def run_rounds(name, eng, prologue, iteration, epilogue, rounds, unroll, head, tail):
    emit(prologue, name, eng, 0)
    for i in range(head):
        emit(iteration(i, i), name, eng, i)
    assert (rounds - head - tail) % unroll == 0
    bodies = [iteration(None, head + j) for j in range(unroll)]
    if any(e == name for body in bodies for e, _, _ in body):
        with eng.Fori(head, rounds - tail - unroll + 1, unroll) as i:
            for j, body in enumerate(bodies):
                emit(body, name, eng, i + j)
    for i in range(rounds - tail, rounds):
        emit(iteration(i, i), name, eng, i)
    emit(epilogue, name, eng, rounds)


def build(nc, a, out):
    top = ExitStack()
    dram = {}
    for n, e, t in ((0, E0, most_tiles(E0, TOP0)), (1, E1, most_tiles(E1, TOP1))):
        rows = e * REGION + (t + 3) * P
        dram[f"table{n}"] = nc.dram_tensor(f"table{n}", (rows, 2), I32, kind="Internal").ap()
        dram[f"xn{n}"] = nc.dram_tensor(f"xn{n}", (TOKENS + SPARE, D), F32, kind="Internal").ap()
    dram["acc0"] = nc.dram_tensor("acc0", (TOKENS + SPARE, D), F32, kind="Internal").ap()
    dram["acc1"] = out

    def maker(stack):
        def sb(name, shape, dt=F32):
            return stack.enter_context(nc.sbuf_tensor(name, list(shape), dt))

        def ps(name, shape):
            return stack.enter_context(nc.psum_tensor(name, list(shape), F32))

        def lane(name, events, step=1):
            return Lane(stack.enter_context(nc.semaphore(name)), events, step)

        return sb, ps, lane

    with top:
        sb, ps, lane = maker(top)
        c = dict(
            settled=top.enter_context(nc.semaphore("settled")),
            ident=sb("ident", [P, P]), before=sb("before", [N, N]), ones=sb("ones", [N, P]),
            iota=sb("iota", [N, E1]), neghalf=sb("neghalf", [P, 4]),
            gates=sb("gates", [P, 4]), tg=sb("tg", [P, 4]),
            token=sb("token", [N, 1], I32), base=sb("base", [P, E1]),
            region=sb("region", [P, E1]), upto=sb("upto", [P, E1, E1]), tile=sb("tile", [P, 1]),
            expert_w=sb("expert_w", [P, 3 * E0 * 2 * F0]),
            wq0=sb("wq0", [P, 2, I0]), wk0=sb("wk0", [CK, 2, I0]),
            wo0=sb("wo0", [P, 4, D]), wr0=sb("wr0", [P, 2, E0]), bo0=sb("bo0", [N, D]),
            wq1=sb("wq1", [P, 2, I1]), wkv1=sb("wkv1", [CK, 2, 2 * I1]), wlkv1=sb("wlkv1", [P, 2, 2 * I1]),
            wo1=sb("wo1", [P, 2, D]), wr1=sb("wr1", [P, 2, E1]), bo1=sb("bo1", [N, D]),
            cx_g=sb("cx_g", [CK, 2]), cx_b=sb("cx_b", [CK, 2]), lt_g=sb("lt_g", [P, 2]), lt_b=sb("lt_b", [P, 2]),
            qk_g=sb("qk_g", [P, 2]), qk_s=sb("qk_s", [P, 1]),
            w_ready=lane("w_ready", ["all"], 16), x0_ready=lane("experts0_w", ["w"], 16),
            x1_ready=lane("experts1_w", ["w"], 16),
        )
        c["wv0"] = c["expert_w"][0:CK, 0:2 * I0].rearrange("p (k n) -> p k n", k=2)
        setup(nc, maker, a, dram, c)
        attention(nc, maker, a, dram, c, 0)
        experts(nc, maker, a, dram, c, 0)
        attention(nc, maker, a, dram, c, 1)
        experts(nc, maker, a, dram, c, 1)


def load_expert_weights(eng, a, c, n):
    w = c["expert_w"]
    if n == 0:
        w13 = w[:, 0:E0 * 2 * 2 * F0].rearrange("p (e k f) -> p e k f", e=E0, k=2)
        w2 = w[:, E0 * 4 * F0:E0 * 4 * F0 + E0 * 4 * D].rearrange("p (e k d) -> p e k d", e=E0, k=4)
        for e in range(E0):
            eng.dma_start(w13[:, e], a["L0_ffn_moe_w13"][e].rearrange("(k p) f -> p k f", p=P)).then_inc(c["x0_ready"].sem, 16)
            eng.dma_start(w2[:, e], a["L0_ffn_moe_w2"][e].rearrange("(k p) d -> p k d", p=P)).then_inc(c["x0_ready"].sem, 16)
        return 2 * E0
    w13 = w[:, 0:E1 * 2 * 2 * F1].rearrange("p (e k f) -> p e k f", e=E1, k=2)
    w2 = w[:, E1 * 4 * F1:E1 * 4 * F1 + E1 * 2 * D].rearrange("p (e k d) -> p e k d", e=E1, k=2)
    for e in range(E1):
        eng.dma_start(w13[:, e, :, 0:F1], a["L1_ffn_W1T"][e].rearrange("(k p) f -> p k f", p=P)).then_inc(c["x1_ready"].sem, 16)
        eng.dma_start(w13[:, e, :, F1:2 * F1], a["L1_ffn_W3T"][e].rearrange("(k p) f -> p k f", p=P)).then_inc(c["x1_ready"].sem, 16)
        eng.dma_start(w2[:, e], a["L1_ffn_W2T"][e].rearrange("(k p) d -> p k d", p=P)).then_inc(c["x1_ready"].sem, 16)
    return 3 * E1


def setup(nc, maker, a, dram, c):
    stack = ExitStack()
    with stack:
        sb, ps, lane = maker(stack)
        empty = sb("empty_slots", [P, P, 2], I32)
        zero = sb("zero_rows", [P, D])
        pool = lane("setup_pool", ["z0", "z1", "z2", "ident", "before", "i"])
        dve = lane("setup_dve", ["c0", "c1", "g"])
        act = lane("setup_act", ["tg"])
        st = lane("setup_stores", ["s"], 16)
        w_ready = c["w_ready"]
        with nc.Block() as block:

            @block.gpsimd
            def _(g):
                pool.post(g.memset(c["ident"][:, :], 0.0), "z0")
                pool.post(g.memset(empty[:, :, :], 0), "z1")
                g.memset(zero[:, :], 0.0)
                g.memset(c["upto"][:, :, :], 1.0)
                pool.post(g.memset(c["ones"][:, :], 1.0), "z2")
                pool.wait(g, 0, "z2")
                pool.post(g.affine_select(out=c["ident"][:, :], in_=c["ident"][:, :], compare_op=ALU.not_equal, fill=1.0,
                                          base=0, pattern=[[-1, P]], channel_multiplier=1), "ident")
                pool.post(g.affine_select(out=c["before"][:, :], in_=c["ones"][:, 0:N], compare_op=ALU.is_gt, fill=0.0,
                                          base=0, pattern=[[1, N]], channel_multiplier=-1), "before")
                g.affine_select(out=c["upto"][:, :, :], in_=c["upto"][:, :, :], compare_op=ALU.is_ge, fill=0.0,
                                base=0, pattern=[[1, E1], [-1, E1]], channel_multiplier=0)
                g.iota(c["region"][:, :], [[REGION, E1]], base=1 - P, channel_multiplier=0, allow_small_or_imprecise_dtypes=True)
                g.iota(c["tile"][:, :], [[1, 1]], base=0, channel_multiplier=1, allow_small_or_imprecise_dtypes=True)
                g.iota(c["iota"][:, :], [[1, E1]], base=0, channel_multiplier=0, allow_small_or_imprecise_dtypes=True)
                g.iota(c["token"][:, :], [[1, 1]], base=0, channel_multiplier=1)
                pool.post(g.iota(empty[:, :, 0], [[1, P]], base=TOKENS, channel_multiplier=0), "i")

            @block.sync
            def _(s):
                def w(dst, src):
                    s.dma_start(dst, src).then_inc(w_ready.sem, 16)
                    w.n += 1
                w.n = 0
                with nc.allow_non_contiguous_dma(reason="a few per-partition constants"):
                    w(c["gates"][:, 0:2], a["g_xattn"].partition_broadcast(P))
                    w(c["gates"][:, 2:4], a["g_ffn"].partition_broadcast(P))
                    w(c["cx_g"][:, :], a["L1_xattn_ln_x_g"].rearrange("(k p) -> p k", p=CK))
                    w(c["cx_b"][:, :], a["L1_xattn_ln_x_b"].rearrange("(k p) -> p k", p=CK))
                    w(c["lt_g"][:, :], a["L1_xattn_ln_l_g"].rearrange("(k p) -> p k", p=P))
                    w(c["lt_b"][:, :], a["L1_xattn_ln_l_b"].rearrange("(k p) -> p k", p=P))
                    for half in range(2):
                        for j, n in enumerate(("q", "k")):
                            w(c["qk_g"][half * DH:(half + 1) * DH, j:j + 1],
                              a[f"L1_xattn_{n}n_g"].rearrange("(p k) -> p k", k=1))
                for n, src, p in (("wq0", "L0_xattn_Wq", P), ("wk0", "L0_xattn_Wk", CK), ("wv0", "L0_xattn_Wv", CK),
                                  ("wo0", "L0_xattn_Wo", P), ("wr0", "L0_ffn_moe_router", P),
                                  ("wq1", "L1_xattn_WqT", P), ("wkv1", "L1_xattn_WkvT", CK), ("wlkv1", "L1_xattn_WlkvT", P),
                                  ("wo1", "L1_xattn_WoT", P), ("wr1", "L1_ffn_WgT", P)):
                    w(c[n][:, :, :], a[src].rearrange("(k p) n -> p k n", p=p))
                w(c["bo0"][:, :], a["L0_xattn_bo"].partition_broadcast(N))
                w(c["bo1"][:, :], a["L1_xattn_bo"].partition_broadcast(N))
                c["w_loads"] = w.n
                s.wait_ge(w_ready.sem, 16 * w.n)

            @block.vector
            def _(v):
                dve.post(v.memset(c["neghalf"][:, :], -0.5), "c0")
                v.wait_ge(w_ready.sem, 16 * c["w_loads"])
                dve.post(v.tensor_tensor(c["qk_s"][:, :], c["qk_g"][:, 0:1], c["qk_g"][:, 1:2], ALU.mult), "c1")
                dve.wait(v, 0, "c1")
                v.tensor_scalar(c["qk_s"][:, :], c["qk_s"][:, :], DH ** -0.5, None, ALU.mult)
                act.wait(v, 0, "tg")
                v.tensor_scalar(c["bo0"][:, :], c["bo0"][:, :], c["tg"][0:N, 0:1], None, ALU.mult)
                dve.post(v.tensor_scalar(c["bo1"][:, :], c["bo1"][:, :], c["tg"][0:N, 1:2], None, ALU.mult), "g")

            @block.scalar
            def _(s):
                pool.wait(s, 0, "i")
                for n in range(2):
                    t = dram[f"table{n}"]
                    blocks = t.shape[0] // P
                    full = t.rearrange("(b r) c -> b (r c)", r=P)
                    for at in range(0, blocks, P):
                        m = min(P, blocks - at)
                        s.dma_start(full[at:at + m], empty[0:m].rearrange("p r c -> p (r c)")).then_inc(st.sem, 16)
                        st.seen += 1
                    s.dma_start(dram[f"xn{n}"][TOKENS:TOKENS + SPARE], zero[:, :]).then_inc(st.sem, 16)
                    s.dma_start(dram[f"acc{n}"][TOKENS:TOKENS + SPARE], zero[:, :]).then_inc(st.sem, 16)
                    st.seen += 2
                s.wait_ge(w_ready.sem, 16 * c["w_loads"])
                act.post(s.activation(c["tg"][:, :], c["gates"][:, :], ACT.Tanh), "tg")
                s.wait_ge(st.sem, 16 * st.seen)


def attention(nc, maker, a, dram, c, layer):
    L0 = layer == 0
    heads = H0 if L0 else H1
    pairs = heads // 2
    keys = SP if L0 else K1
    nch = NCH if L0 else NCH + 1
    experts_n, topk = (E0, TOP0) if L0 else (E1, TOP1)
    tg_x, tg_f = c["tg"][0:N, layer:layer + 1], c["tg"][0:N, 2 + layer:3 + layer]
    wo, wr, bo = c[f"wo{layer}"], c[f"wr{layer}"], c[f"bo{layer}"]
    table, acc, xn_rows = dram[f"table{layer}"], dram[f"acc{layer}"], dram[f"xn{layer}"]
    ident, neghalf = c["ident"], c["neghalf"]
    L = str(layer)

    stack = ExitStack()
    with stack:
        sb, ps, lane = maker(stack)
        psS = ps("psS" + L, [P, 2, 512])
        psT = ps("psT" + L, [P, 2, 512])
        psO = ps("psO" + L, [P, 512])
        psJ = ps("psJ" + L, [P, 2, 512])
        psY = ps("psY" + L, [P, 512])

        x = sb("x" + L, [N, 2, D])
        xb = sb("xb" + L, [N, 2, D])
        st = sb("st" + L, [N, 6])
        mv = sb("mv" + L, [N, 2])
        rstd = sb("rstd" + L, [N, 2])
        xn = sb("xn_a" + L, [N, 2, D])
        xT = sb("xT" + L, [P, 2, N])
        qz = sb("qz" + L, [P, 2, heads, N])
        kT = sb("kT" + L, [P, 2, pairs, keys])
        if L0:
            vv = sb("vv0", [CH, 2, NCH, I0])
        else:
            kv = sb("kv", [CH, 2, NCH + 2, 2 * I1])
            vv = kv[:, :, 1:, I1:2 * I1]
        prob = sb("prob" + L, [N, 4, keys])
        nm = sb("nm" + L, [N, 4])
        rs = sb("rs" + L, [N, 4])
        rc = sb("rc" + L, [N, 4])
        pT = sb("pT" + L, [CH, 2, 2, nch, N])
        oT = sb("oT" + L, [P, pairs, N])
        x1 = sb("x1" + L, [N, 2, D])
        xm = sb("xm" + L, [N, 2, D])
        st1 = sb("st1" + L, [N, 6])
        mv1 = sb("mv1" + L, [N, 2])
        rstd1 = sb("rstd1" + L, [N, 2])
        xmT = sb("xmT" + L, [P, 2, N])
        sc = sb("sc" + L, [N, 3, E1])
        top_v = sb("top_v" + L, [N, 8])
        top_i = sb("top_i" + L, [N, 8], U32)
        top_f = sb("top_f" + L, [N, TOP1])
        hot = sb("hot" + L, [N, TOP1, E1])
        hit = sb("hit" + L, [N, TOP1, E1])
        chosen = sb("chosen" + L, [N, E1])
        slot_of = sb("slot_of" + L, [N, E1])
        pos_f = sb("pos_f" + L, [N, TOP1])
        tmp = sb("tmp" + L, [N, 8])
        pos = sb("pos" + L, [N, 2, TOP1], U32)
        slot = sb("slot" + L, [N, 2, TOP1, 2], I32)
        slot_w = slot[:, :, :, 1].bitcast(F32)
        if L0:
            cT = sb("cT" + L, [CK, 2, 2, SP])
            c_hl = sb("c_hl", [CK, 2, 2, SP], F32R)
            wv_hl = sb("wv_hl", [CK, 2, 2, I0], F32R)
        else:
            cn = ctx = sb("ctx", [CH, 2, NCH, C])
            xl = sb("xl", [N, 2, D])
            lT = xT
            cst = sb("cst", [CH, NCH, 6])
            cmv = sb("cmv", [CH, NCH, 2])
            crs = sb("crs", [CH, 2, NCH])
            cTn = sb("cTn", [CK, 2, SP])
            sq = sb("sq", [CH, NCH + 2, I1])
            ss = sb("ss", [CH, NCH + 2, H1])
            rk = sb("rk", [CH, NCH + 2, H1])
            m8 = sb("m8", [N, 2, S], U8)
            mb = sb("mb", [N, 2, K1])
            gmax = sb("gmax", [N, 8])
            gtop = sb("gtop", [N, 8])
            gidx = sb("gidx", [N, 8], U32)
            gidf = sb("gidf", [N, TOPG])
            ghot = sb("ghot", [N, TOPG, GROUPS])
            gok = sb("gok", [N, GROUPS])

        ld_x = lane("ld_x" + L, ["x"], 16)
        ld_c = lane("ld_c" + L, ["c"] if L0 else ["c0", "c1", "m"], 16)
        st_x = lane("st_x" + L, ["x1", "xm"], 16)
        st_s = lane("st_s" + L, ["k%d" % k for k in range(topk)], 16)
        init = lane("init" + L, ["i"])

        def group(name, *stages):
            return Group([lane(f"{name}_{k}{L}", events) for k, events in enumerate(stages)])

        each_pair, each_head = range(pairs), range(heads)
        if L0:
            now = []
            C_act, C_dve = lane("C_act0", ["high"]), lane("C_dve0", ["low"])
            W_dve = lane("W_dve0", ["high", "low"])
            N_dve, N_pool = lane("N_dve0", ["stat", "mv", "xn"]), lane("N_pool0", ["ve", "rstd"])
            uses = ["xt", "k0", "k1", "q", "k2", "k3", "v0", "v1", "v2"]
            owner = dict(k0="act", k1="act", k2="act", k3="act", v0="dve", v1="dve", v2="dve", xt="act", q="dve")
            P_pool = lane("P_pool0", ["xb"])
        else:
            N_dve = lane("N_dve1", ["cstat", "cmv", "cn", "stat", "mv", "xn", "stat2", "mv2", "xl"])
            N_pool = lane("N_pool1", ["cve", "crs", "ve", "rstd", "ve2", "rstd2", "mb"])
            uses = ["lt", "ct0", "ct1", "qt", "kt0", "kt1", "q", "kv0", "kv1", "kv2", "kv3"]
            now = ["qt", "kt0", "kt1"]
            owner = {u: "act" for u in uses}
            P_pool = lane("P_pool1", ["msA", "rkA", "msB", "rkB", "xb"])
            P_dve = group("P_dve", ["ssA", "ssB"], ["knA", "knB"])
            P_pe = group("P_pe", [u for u in uses if u not in now], now)
            P_act = group("P_act", ["lt", "ct0", "ct1", "q", "kv0", "kv1", "sqA", "kv2", "kv3", "sqB"], now)
        if L0:
            P_pe = lane("P_pe0", uses)
            P_dve = lane("P_dve0", [u for u in uses if owner[u] == "dve"])
            P_act = lane("P_act0", [u for u in uses if owner[u] == "act"])
        X_pe = group("X_pe", [f"s{h}" for h in each_head], [f"t{p}" for p in each_pair], [f"o{p}" for p in each_pair])
        X_dve = group("X_dve", sum([([] if L0 else [f"a{2 * p}", f"a{2 * p + 1}"]) + [f"m{p}"] for p in each_pair], []),
                      [f"r{p}" for p in each_pair], *([[f"t{p}" for p in each_pair]] if L0 else []))
        X_act = group("X_act", [f"e{h}" for h in each_head], [f"o{p}" for p in each_pair],
                      *([] if L0 else [[f"t{p}" for p in each_pair]]))
        X_t = X_dve if L0 else X_act
        X_pool = lane("X_pool" + L, [f"n{h}" for h in each_head])
        Y_pe = group("Y_pe", ["wo", "xt", "lg"], ["rk"])
        router = (["lg", "top", "idx", "idf", "hot", "cho", "d", "w0", "w1", "w2", "w3"] if L0 else
                  ["s0", "s1", "gm", "gt", "gi", "gf", "gh", "go", "gk", "msk", "top", "idx", "idf", "hot", "cho",
                   "sum", "rcp", "w2", "w3"])
        Y_dve = group("Y_dve", ["x1", "stat", "mv", "xm"] + router, ["tok", "slot", "hit", "pos", "posi"])
        Y_act = lane("Y_act" + L, ["xt", "e"])
        Y_pool = lane("Y_pool" + L, ["ve", "rstd"])

        def bank(par, use):
            return psJ[:, ((par + (use in now)) * len(uses) + uses.index(use)) % 2, :]

        def free_bank(eng, b, par, use):
            at, shift = uses.index(use), 0
            while True:
                at -= 2
                if at < 0:
                    at, shift = at + len(uses), shift - 1
                prev = uses[at]
                back = b + shift + (use in now) - (prev in now)
                if not isinstance(back, int) or 0 <= back < B:
                    break
                if back < -1:
                    return
            (P_act if owner[prev] == "act" else P_dve).wait(eng, back, prev)

        def layer_norm(add, src, dst, stt, mvt, rst, dve, pool, names, ready, free=None):
            stat, mvn, ve, rn, done = names

            def d1(v, b):
                ready(v, b)
                dve.post(v.bn_stats(stt[:, :], src), stat)
                dve.wait(v, b, stat)
                settle(v, c)
                dve.post(v.bn_aggr(mvt[:, :], stt[:, :]), mvn)

            def g1(g, b):
                dve.wait(g, b, mvn)
                settle(g, c)
                pool.post(g.tensor_scalar(rst[:, 0:1], mvt[:, 1:2], LN_EPS, 1.0, ALU.add, ALU.mult), ve)
                pool.wait(g, b, ve)
                pool.post(g.tensor_tensor(rst[:, 1:2], rst[:, 0:1], neghalf[0:N, 0:1], ALU.pow), rn)

            def d2(v, b):
                pool.wait(v, b, rn)
                if free:
                    free(v, b)
                dve.post(v.tensor_scalar(dst, src, mvt[:, 0:1], rst[:, 1:2], ALU.subtract, ALU.mult), done)

            add("dve", d1), add("pool", g1), add("dve", d2)

        def p_bias(steps, off, par):
            def g0(g, b):
                ld_x.wait(g, b, "x")
                Y_dve.wait(g, b - 2, "x1")
                P_pool.post(g.tensor_tensor(xb[:, par, :], x[:, par, :], bo[:, :], ALU.add), "xb")
            steps.append(("pool", off, g0))

        def p_norm0(steps, off, par):
            def add(e, fn):
                steps.append((e, off, fn))

            layer_norm(add, x[:, par, :], xn[:, par, :], st, mv, rstd, N_dve, N_pool,
                       ("stat", "mv", "ve", "rstd", "xn"), lambda v, b: ld_x.wait(v, b, "x"))

        TERMS = ((0, 0), (0, 1), (1, 0))

        def p_split0(steps, off, par):
            def ac(s, b):
                ld_c.wait(s, b, "c")
                P_pe.wait(s, b - 1, "v2")
                C_act.post(s.activation(c_hl[:, 0], cT[:, par], ACT.Copy), "high")

            def dv(v, b):
                C_act.wait(v, b, "high")
                C_dve.post(v.tensor_tensor(c_hl[:, 1], cT[:, par], c_hl[:, 0].bitcast(F32), ALU.subtract), "low")
            steps += [("act", off, ac), ("dve", off, dv)]

        def p_k0(steps, off, par, m):
            use = f"k{m}"
            ph = bank(par, use)

            def pe(t, b):
                ld_c.wait(t, b, "c")
                free_bank(t, b, par, use)
                for k in range(2):
                    mm = t.matmul(ph[:, 0:SP], c["wk0"][:, k, m * P:(m + 1) * P], cT[:, par, k, :], start=k == 0, stop=k == 1)
                P_pe.post(mm, use)

            def ac(s, b):
                P_pe.wait(s, b, use)
                P_act.post(s.activation(kT[:, par, m, :], ph[:, 0:SP], ACT.Copy), use)
            steps += [("pe", off, pe), ("act", off, ac)]

        def p_v0(steps, off, par, ch):
            use = f"v{ch}"
            ph = bank(par, use)

            def pe(t, b):
                C_dve.wait(t, b, "low")
                free_bank(t, b, par, use)
                for n, (k, (x_, y_)) in enumerate((k, term) for k in range(2) for term in TERMS):
                    mm = t.matmul(ph[0:CH, :], c_hl[:, x_, k, ch * CH:(ch + 1) * CH], wv_hl[:, y_, k, :], start=n == 0, stop=n == 5)
                P_pe.post(mm, use)

            def dv(v, b):
                P_pe.wait(v, b, use)
                P_dve.post(v.tensor_copy(vv[:, par, ch, :], ph[0:CH, :]), use)
            steps += [("pe", off, pe), ("dve", off, dv)]

        def p_xt0(steps, off, par):
            ph = bank(par, "xt")

            def pe1(t, b):
                N_dve.wait(t, b, "xn")
                free_bank(t, b, par, "xt")
                for k in range(2):
                    mm = t.transpose(ph[:, k * N:(k + 1) * N], xn[:, par, k * P:(k + 1) * P], ident[0:N, 0:N])
                P_pe.post(mm, "xt")

            def ac(s, b):
                P_pe.wait(s, b, "xt")
                P_act.post(s.activation(xT[:, :, :], ph[:, 0:2 * N].rearrange("p (k n) -> p k n", k=2), ACT.Copy), "xt")

            steps += [("pe", off, pe1), ("act", off, ac)]

        def p_q0(steps, off, par):
            pq = bank(par, "q")

            def pe2(t, b):
                P_act.wait(t, b, "xt")
                free_bank(t, b, par, "q")
                for m in range(pairs):
                    for k in range(2):
                        mm = t.matmul(pq[:, m * N:(m + 1) * N], c["wq0"][:, k, m * P:(m + 1) * P], xT[:, k, :],
                                      start=k == 0, stop=k == 1)
                P_pe.post(mm, "q")

            def dv(v, b):
                P_pe.wait(v, b, "q")
                for half in range(2):
                    r = slice(half * DH, (half + 1) * DH)
                    ins = v.tensor_scalar(qz[r, par, half:heads:2, :], pq[r, 0:pairs * N].rearrange("p (m n) -> p m n", m=pairs),
                                          DH ** -0.5, None, ALU.mult)
                P_dve.post(ins, "q")
            steps += [("pe", off, pe2), ("dve", off, dv)]

        def p_norm1(steps, off, par):
            def add(e, fn):
                steps.append((e, off, fn))

            def d0(v, b):
                ld_c.wait(v, b, "m")
                for j in range(NCH):
                    ins = v.bn_stats(cst[:, j, :], ctx[:, par, j, :])
                N_dve.post(ins, "cstat")

            def d1(v, b):
                N_dve.wait(v, b, "cstat")
                settle(v, c)
                for j in range(NCH):
                    ins = v.bn_aggr(cmv[:, j, :], cst[:, j, :])
                N_dve.post(ins, "cmv")

            def g1(g, b):
                N_dve.wait(g, b, "cmv")
                settle(g, c)
                N_pool.post(g.tensor_scalar(crs[:, 0, :], cmv[:, :, 1], LN_EPS, 1.0, ALU.add, ALU.mult), "cve")
                N_pool.wait(g, b, "cve")
                N_pool.post(g.tensor_tensor(crs[:, 1, :], crs[:, 0, :], neghalf[0:CH, 0:NCH], ALU.pow), "crs")

            def g2(g, b):
                X_dve.wait(g, b - 2, f"a{heads - 1}")
                settle(g, c)
                N_pool.post(g.tensor_scalar(mb[:, par, CH:CH + S], m8[:, par, :], -NEG, NEG, ALU.mult, ALU.add), "mb")

            def d2(v, b):
                N_pool.wait(v, b, "crs")
                for j in range(NCH):
                    ins = v.tensor_scalar(cn[:, par, j, :], ctx[:, par, j, :], cmv[:, j, 0:1], crs[:, 1, j:j + 1],
                                          ALU.subtract, ALU.mult)
                N_dve.post(ins, "cn")
            add("dve", d0), add("dve", d1), add("pool", g1), add("dve", d2)
            layer_norm(add, x[:, par, :], xn[:, par, :], st, mv, rstd, N_dve, N_pool,
                       ("stat", "mv", "ve", "rstd", "xn"), lambda v, b: ld_x.wait(v, b, "x"))
            layer_norm(add, xn[:, par, :], xl[:, par, :], st, mv, rstd, N_dve, N_pool,
                       ("stat2", "mv2", "ve2", "rstd2", "xl"), lambda v, b: N_dve.wait(v, b, "xn"))
            add("pool", g2)

        def p_t1(steps, off, par):
            def pe(t, b):
                N_dve.wait(t, b, "xl")
                free_bank(t, b, par, "lt")
                ph = bank(par, "lt")
                for k in range(2):
                    mm = t.transpose(ph[:, k * N:(k + 1) * N], xl[:, par, k * P:(k + 1) * P], ident[0:N, 0:N])
                P_pe.post(mm, "lt")

            def ac(s, b):
                P_pe.wait(s, b, "lt")
                ph = bank(par, "lt")
                for k in range(2):
                    ins = s.activation(lT[:, k, :], ph[:, k * N:(k + 1) * N], ACT.Identity,
                                       bias=c["lt_b"][:, k:k + 1], scale=c["lt_g"][:, k:k + 1])
                P_act.post(ins, "lt")
            steps += [("pe", off, pe), ("act", off, ac)]
            for k in range(2):
                def pe(t, b, k=k):
                    N_dve.wait(t, b, "cn")
                    free_bank(t, b, par, f"ct{k}")
                    ph = bank(par, f"ct{k}")
                    for j in range(NCH):
                        mm = t.transpose(ph[0:CK, j * CH:(j + 1) * CH], cn[:, par, j, k * CK:(k + 1) * CK], ident[0:CH, 0:CH])
                    P_pe.post(mm, f"ct{k}")

                def ac(s, b, k=k):
                    P_pe.wait(s, b, f"ct{k}")
                    ph = bank(par, f"ct{k}")
                    P_act.post(s.activation(cTn[:, k, :], ph[0:CK, 0:SP], ACT.Identity,
                                            bias=c["cx_b"][:, k:k + 1], scale=c["cx_g"][:, k:k + 1]), f"ct{k}")
                steps += [("pe", off, pe), ("act", off, ac)]

        def p_qkv1(steps, off, par, j):
            use = f"kv{j - 1}" if j else "q"
            ph = bank(par, use)
            latents = j < 2
            rows, cols = N if latents else CH, 2 * I1 if j else I1
            wt = c["wq1"] if j == 0 else c["wlkv1"] if latents else c["wkv1"]

            def pe(t, b):
                free_bank(t, b, par, use)
                P_act.wait(t, b, "lt" if latents else "ct1")
                for k in range(2):
                    lhs = lT[:, k, :] if latents else cTn[:, k, (j - 2) * CH:(j - 1) * CH]
                    mm = t.matmul(ph[0:rows, 0:cols], lhs, wt[:, k, :], start=k == 0, stop=k == 1)
                P_pe.post(mm, use)

            def ac(s, b):
                P_pe.wait(s, b, use)
                P_act.post(s.activation(kv[0:rows, par, j, 0:cols], ph[0:rows, 0:cols], ACT.Copy), use)
            steps += [("pe", off, pe), ("act", off, ac)]

        def p_rms(steps, off, par, part):
            r, n, last = (slice(0, 3), 3, "kv1") if part == "A" else (slice(3, 5), 2, "kv3")
            qk = kv[:, par, r, 0:I1]

            def ac(s, b):
                P_act.wait(s, b, last)
                P_dve.wait(s, b - 1, "ss" + part)
                P_act.post(s.activation(sq[:, r, :], qk, ACT.Square), "sq" + part)

            def d1(v, b):
                P_act.wait(v, b, "sq" + part)
                P_dve.post(v.tensor_reduce(ss[:, r, :], sq[:, r, :].rearrange("p j (h d) -> p j h d", h=H1), AX, ALU.add),
                           "ss" + part)

            def g1(g, b):
                P_dve.wait(g, b, "ss" + part)
                settle(g, c)
                P_pool.post(g.tensor_scalar(rk[:, r, :], ss[:, r, :], 1.0 / DH, RMS_EPS ** 2, ALU.mult, ALU.max), "ms" + part)
                P_pool.wait(g, b, "ms" + part)
                P_pool.post(g.tensor_tensor(rk[:, r, :], rk[:, r, :], neghalf[0:CH, 0:1].unsqueeze(2).to_broadcast([CH, n, H1]),
                                            ALU.pow), "rk" + part)

            def d2(v, b):
                P_pool.wait(v, b, "rk" + part)
                rows = qk.rearrange("p j (h d) -> p j h d", h=H1)
                scale = rk[:, r, :].unsqueeze(3).to_broadcast([CH, n, H1, DH])
                P_dve.post(v.tensor_tensor(rows, rows, scale, ALU.mult), "kn" + part)
            steps += [("act", off, ac), ("dve", off, d1), ("pool", off, g1), ("dve", off, d2)]

        def p_qkt1(steps, off, par):
            def peq(t, b):
                P_dve.wait(t, b, "knA")
                free_bank(t, b, par, "qt")
                ph = bank(par, "qt")
                for k in range(2):
                    mm = t.transpose(ph[:, k * N:(k + 1) * N], kv[0:N, par, 0, k * P:(k + 1) * P], ident[0:N, 0:N])
                P_pe.post(mm, "qt")

            def acq(s, b):
                P_pe.wait(s, b, "qt")
                src = bank(par, "qt")[:, 0:2 * N].rearrange("p (k n) -> p k n", k=2)
                for half in range(2):
                    r = slice(half * DH, (half + 1) * DH)
                    ins = s.activation(qz[r, par, half:heads:2, :], src[r], ACT.Copy, scale=c["qk_s"][r, 0:1])
                P_act.post(ins, "qt")
            steps += [("pe", off, peq), ("act", off, acq)]
            for k in range(2):
                def pe(t, b, k=k):
                    P_dve.wait(t, b, "knB")
                    free_bank(t, b, par, f"kt{k}")
                    ph = bank(par, f"kt{k}")
                    for j in range(nch):
                        mm = t.transpose(ph[:, j * CH:(j + 1) * CH], kv[:, par, 1 + j, k * P:(k + 1) * P], ident[0:CH, 0:CH])
                    P_pe.post(mm, f"kt{k}")

                def ac(s, b, k=k):
                    P_pe.wait(s, b, f"kt{k}")
                    P_act.post(s.activation(kT[:, par, k, :], bank(par, f"kt{k}")[:, 0:keys], ACT.Copy), f"kt{k}")
                steps += [("pe", off, pe), ("act", off, ac)]

        def x_scores(steps, off, par, p):
            def pe(t, b, h):
                if p == 0 and h == 0:
                    if L0:
                        P_dve.wait(t, b, "q")
                    else:
                        P_act.wait(t, b, "qt")
                if not L0 and h == 0:
                    P_act.wait(t, b, f"kt{p}")
                if L0:
                    P_act.wait(t, b, f"k{p}")
                hh = 2 * p + h
                if L0:
                    X_act.wait(t, b if p else b - 1, f"e{(hh - 2) % heads}")
                else:
                    X_dve.wait(t, b if p else b - 1, f"a{(hh - 2) % heads}")
                X_pe.post(t.matmul(psS[0:N, h, 0:keys], qz[:, par, hh, :], kT[:, par, p, :], start=True, stop=True), f"s{hh}")
            q2 = (2 * p) % 4

            def dv(v, b):
                if L0:
                    X_pe.wait(v, b, f"s{2 * p + 1}")
                    X_dve.post(v.tensor_reduce(nm[:, q2:q2 + 2], psS[0:N, :, 0:S], AX, ALU.max, negate=True), f"m{p}")
                    return
                if p == 0:
                    N_pool.wait(v, b, "mb")
                for h in range(2):
                    hh = 2 * p + h
                    X_pe.wait(v, b, f"s{hh}")
                    settle(v, c)
                    X_dve.post(v.tensor_tensor_reduce(prob[:, hh, :], psS[0:N, h, 0:keys], mb[:, par, :], 1.0, -3e38,
                                                      ALU.add, ALU.max, nm[:, hh:hh + 1]), f"a{hh}")
                X_dve.wait(v, b, f"a{2 * p + 1}")
                X_dve.post(v.tensor_scalar(nm[:, q2:q2 + 2], nm[:, q2:q2 + 2], -1.0, None, ALU.mult), f"m{p}")

            def ac(s, b, h):
                hh = 2 * p + h
                q = hh % 4
                X_dve.wait(s, b, f"m{p}")
                if L0:
                    X_pe.wait(s, b if hh >= 4 else b - 1, f"t{(hh - 4) % heads // 2}")
                    src, dst = psS[0:N, h, 0:S], prob[:, q, 0:S]
                else:
                    src = dst = prob[:, q, :]
                X_act.post(s.activation(dst, src, ACT.Exp, bias=nm[:, q:q + 1], accum_out=rs[:, q:q + 1]), f"e{hh}")
            for h in range(2):
                steps.append(("pe", off, lambda t, b, h=h: pe(t, b, h)))
            steps.append(("dve", off, dv))
            for h in range(2):
                steps.append(("act", off, lambda s, b, h=h: ac(s, b, h)))

        def x_norm(steps, off, par, p):
            q2 = (2 * p) % 4

            def dv(v, b):
                X_act.wait(v, b, f"e{2 * p + 1}")
                X_dve.post(v.reciprocal(rc[:, q2:q2 + 2], rs[:, q2:q2 + 2]), f"r{p}")

            def po(g, b):
                X_dve.wait(g, b, f"r{p}")
                settle(g, c)
                for h in range(2):
                    q = q2 + h
                    X_pool.post(g.tensor_scalar(prob[:, q, :], prob[:, q, :], rc[:, q:q + 1], 1.0, ALU.mult, ALU.mult),
                                f"n{2 * p + h}")
            steps += [("dve", off, dv), ("pool", off, po)]

        def x_transpose(steps, off, par, p):
            def pe(t, b):
                for h in range(2):
                    X_pool.wait(t, b, f"n{2 * p + h}")
                    if h == 0:
                        X_t.wait(t, b if p else b - 1, f"t{(p - 1) % pairs}")
                    for j in range(nch):
                        mm = t.transpose(psT[0:CH, h, j * N:(j + 1) * N], prob[:, (2 * p + h) % 4, j * CH:(j + 1) * CH],
                                         ident[0:N, 0:N])
                X_pe.post(mm, f"t{p}")

            def out(e, b):
                X_pe.wait(e, b, f"t{p}")
                dst, src = pT[:, p % 2, :, :, :], psT[0:CH, :, 0:nch * N].rearrange("p h (j n) -> p h j n", j=nch)
                X_t.post(e.tensor_copy(dst, src) if L0 else e.activation(dst, src, ACT.Copy), f"t{p}")
            steps += [("pe", off, pe), ("dve" if L0 else "act", off, out)]

        def x_values(steps, off, par, p):
            def pe(t, b):
                X_t.wait(t, b, f"t{p}")
                if p == 0:
                    if L0:
                        P_dve.wait(t, b, "v2")
                    else:
                        P_act.wait(t, b, "kv3")
                X_act.wait(t, b if p else b - 1, f"o{(p - 1) % pairs}")
                for j in range(nch):
                    mm = t.matmul(psO[:, 0:2 * N], vv[:, par, j, p * P:(p + 1) * P], pT[:, p % 2, :, j, :],
                                  start=j == 0, stop=j == nch - 1)
                X_pe.post(mm, f"o{p}")

            def ac(s, b):
                X_pe.wait(s, b, f"o{p}")
                for half in range(2):
                    r = slice(half * DH, (half + 1) * DH)
                    ins = s.activation(oT[r, p, :], psO[r, half * N:(half + 1) * N], ACT.Copy)
                X_act.post(ins, f"o{p}")
            steps += [("pe", off, pe), ("act", off, ac)]

        def y_out(steps, off, par):
            def pe(t, b):
                X_act.wait(t, b, f"o{pairs - 1}")
                if L0:
                    Y_dve.wait(t, b - 1, "slot")
                else:
                    Y_act.wait(t, b - 1, "e")
                for p in range(pairs):
                    mm = t.matmul(psY[0:N, 0:D], oT[:, p, :], wo[:, p, :], start=p == 0, stop=p == pairs - 1)
                Y_pe.post(mm, "wo")

            def dv(v, b):
                Y_pe.wait(v, b, "wo")
                P_pool.wait(v, b, "xb")
                st_x.wait(v, b - 2, "xm")
                Y_dve.post(v.scalar_tensor_tensor(x1[:, par, :], psY[0:N, 0:D], tg_x, xb[:, par, :], ALU.mult, ALU.add), "x1")

            steps += [("pe", off, pe), ("dve", off, dv)]
            layer_norm(lambda e, fn: steps.append((e, off, fn)), x1[:, par, :], xm[:, par, :], st1, mv1, rstd1, Y_dve, Y_pool,
                       ("stat", "mv", "ve", "rstd", "xm"), lambda v, b: Y_dve.wait(v, b, "x1"))

        def y_store(steps, off, par):
            def store(s, b):
                st_x.wait(s, b - 1, "xm")
                Y_dve.wait(s, b, "x1")
                settle(s, c)
                s.dma_start(acc[0:TOKENS].rearrange("(b n) d -> b n d", n=N)[b], x1[:, par, :]).then_inc(st_x.sem, 16)
                Y_dve.wait(s, b, "xm")
                settle(s, c)
                s.dma_start(xn_rows[0:TOKENS].rearrange("(b n) d -> b n d", n=N)[b], xm[:, par, :]).then_inc(st_x.sem, 16)
            steps.append(("sp", off, store))

        def y_transpose(steps, off, par):
            def pe(t, b):
                Y_dve.wait(t, b, "xm")
                if not L0:
                    Y_dve.wait(t, b - 1, "slot")
                for k in range(2):
                    mm = t.transpose(psY[:, k * N:(k + 1) * N], xm[:, par, k * P:(k + 1) * P], ident[0:N, 0:N])
                Y_pe.post(mm, "xt")

            def ac(s, b):
                Y_pe.wait(s, b, "xt")
                Y_act.post(s.activation(xmT[:, :, :], psY[:, 0:2 * N].rearrange("p (k n) -> p k n", k=2), ACT.Copy), "xt")
            steps += [("pe", off, pe), ("act", off, ac)]

        def y_route(steps, off, par):
            def pe(t, b):
                Y_act.wait(t, b, "xt")
                for k in range(2):
                    mm = t.matmul(psY[0:N, 0:experts_n], xmT[:, k, :], wr[:, k, :], start=k == 0, stop=k == 1)
                Y_pe.post(mm, "lg")

            w = slot_w[:, par, 0:topk]
            values = sc[:, 0, 0:experts_n]

            def chain(*ops):
                for k, (name, op, ready) in enumerate(ops):
                    def one(v, b, k=k, name=name, op=op, ready=ready):
                        if k:
                            Y_dve.wait(v, b, ops[k - 1][0])
                        if ready:
                            ready(v, b)
                        if name in ("top", "idx", "gt", "gi"):
                            settle(v, c)
                        Y_dve.post(op(v), name)
                    steps.append(("dve", off, one))

            def one_hot(v, dst, idx_f, n, m):
                return v.tensor_tensor(dst, c["iota"][:, 0:m].unsqueeze(1).to_broadcast([N, n, m]),
                                       idx_f.unsqueeze(2).to_broadcast([N, n, m]), ALU.is_equal)

            def pick(src):
                return [
                    ("top", lambda v: v.max(top_v[:, :], src), None),
                    ("idx", lambda v: v.max_index(top_i[:, :], top_v[:, :], src), None),
                    ("idf", lambda v: v.tensor_copy(top_f[:, 0:topk], top_i[:, 0:topk]), None),
                    ("hot", lambda v: one_hot(v, hot[:, 0:topk, 0:experts_n], top_f[:, 0:topk], topk, experts_n), None),
                    ("cho", lambda v: v.tensor_reduce(chosen[:, 0:experts_n],
                                                      hot[:, 0:topk, 0:experts_n].rearrange("p k e -> p e k"), AX, ALU.add), None)]

            def slot_free(v, b):
                st_s.wait(v, b - 2, f"k{topk - 1}")

            def ac0(s, b):
                Y_dve.wait(s, b, "d")
                Y_act.post(s.activation(tmp[:, 1:2], tmp[:, 0:1], ACT.Exp), "e")

            def ac1(s, b):
                Y_pe.wait(s, b, "lg")
                Y_act.post(s.activation(sc[:, 1, :], psY[0:N, 0:E1], ACT.Exp, scale=-1.0), "e")

            grouped = sc[:, 0, :].rearrange("p (g e) -> p g e", g=GROUPS)
            steps.append(("pe", off, pe))
            if L0:
                chain(("lg", lambda v: v.tensor_copy(values, psY[0:N, 0:experts_n]), lambda v, b: Y_pe.wait(v, b, "lg")),
                      *pick(values),
                      ("d", lambda v: v.tensor_tensor(tmp[:, 0:1], top_v[:, 1:2], top_v[:, 0:1], ALU.subtract), None),
                      ("w0", lambda v: v.tensor_scalar(tmp[:, 2:3], tmp[:, 1:2], 1.0, None, ALU.add),
                       lambda v, b: Y_act.wait(v, b, "e")),
                      ("w1", lambda v: v.reciprocal(tmp[:, 3:4], tmp[:, 2:3]), None),
                      ("w2", lambda v: v.tensor_scalar(w[:, 0:1], tmp[:, 3:4], tg_f, None, ALU.mult), slot_free),
                      ("w3", lambda v: v.tensor_scalar(w[:, 1:2], w[:, 0:1], tmp[:, 1:2], None, ALU.mult), None))
                steps.append(("act", off, ac0))
            else:
                steps.append(("act", off, ac1))
                chain(("s0", lambda v: v.tensor_scalar(sc[:, 2, :], sc[:, 1, :], 1.0, None, ALU.add),
                       lambda v, b: Y_act.wait(v, b, "e")),
                      ("s1", lambda v: v.reciprocal(values, sc[:, 2, :]), None),
                      ("gm", lambda v: v.tensor_reduce(gmax[:, 0:GROUPS], grouped, AX, ALU.max), None),
                      ("gt", lambda v: v.max(gtop[:, :], gmax[:, :]), None),
                      ("gi", lambda v: v.max_index(gidx[:, :], gtop[:, :], gmax[:, :]), None),
                      ("gf", lambda v: v.tensor_copy(gidf[:, :], gidx[:, 0:TOPG]), None),
                      ("gh", lambda v: one_hot(v, ghot[:, :, :], gidf[:, :], TOPG, GROUPS), None),
                      ("go", lambda v: v.tensor_reduce(gok[:, :], ghot[:, :, :].rearrange("p k g -> p g k"), AX, ALU.add), None),
                      ("gk", lambda v: v.tensor_scalar(gok[:, :], gok[:, :], 2.0, -2.0, ALU.mult, ALU.add), None),
                      ("msk", lambda v: v.tensor_tensor(sc[:, 1, :].rearrange("p (g e) -> p g e", g=GROUPS), grouped,
                                                        gok[:, :].unsqueeze(2).to_broadcast([N, GROUPS, E1 // GROUPS]),
                                                        ALU.add), None),
                      *pick(sc[:, 1, :]),
                      ("sum", lambda v: v.tensor_reduce(tmp[:, 0:1], top_v[:, 0:topk], AX, ALU.add), None),
                      ("rcp", lambda v: v.reciprocal(tmp[:, 1:2], tmp[:, 0:1]), None),
                      ("w2", lambda v: v.tensor_scalar(w, top_v[:, 0:topk], tmp[:, 1:2], ROUTE_SCALE, ALU.mult, ALU.mult), slot_free),
                      ("w3", lambda v: v.tensor_scalar(w, w, tg_f, None, ALU.mult), None))

        def y_dispatch(steps, off, par):
            def pe(t, b):
                Y_dve.wait(t, b, "cho")
                if not L0 and not (isinstance(b, int) and b == B - 1):
                    Y_dve.wait(t, b + 1, "x1")
                t.matmul(psY[0:N, 0:experts_n], c["before"][:, :], chosen[:, 0:experts_n], start=True, stop=True)
                Y_pe.post(t.matmul(psY[:, 2 * E1:2 * E1 + experts_n], c["ones"][:, :], chosen[:, 0:experts_n],
                                   start=True, stop=True, skip_group_check=True), "rk")

            def dv(v, b):
                base = c["base"][:, 0:experts_n]
                Y_pe.wait(v, b, "rk")
                v.tensor_tensor(slot_of[:, 0:experts_n], psY[0:N, 0:experts_n], base[0:N], ALU.add)
                Y_dve.post(v.tensor_scalar(slot[:, par, 0:topk, 0], c["token"][:, 0:1].to_broadcast([N, topk]), 0.0, None,
                                           ALU.add), "tok")
                Y_dve.wait(v, b, "tok")
                v.tensor_scalar(c["token"][:, :], c["token"][:, :], float(N), None, ALU.add)
                Y_dve.post(v.tensor_tensor(base, psY[:, 2 * E1:2 * E1 + experts_n], base, ALU.add), "slot")
                Y_dve.wait(v, b, "slot")
                Y_dve.post(v.tensor_tensor(hit[:, 0:topk, 0:experts_n], hot[:, 0:topk, 0:experts_n],
                                           slot_of[:, 0:experts_n].unsqueeze(1).to_broadcast([N, topk, experts_n]), ALU.mult), "hit")
                Y_dve.wait(v, b, "hit")
                Y_dve.post(v.tensor_reduce(pos_f[:, 0:topk], hit[:, 0:topk, 0:experts_n], AX, ALU.add), "pos")
                Y_dve.wait(v, b, "pos")
                Y_dve.post(v.tensor_copy(pos[:, par, 0:topk], pos_f[:, 0:topk]), "posi")

            def po(g, b):
                Y_dve.wait(g, b, "posi")
                st_s.wait(g, b - 1, f"k{topk - 1}")
                settle(g, c)
                for k in range(topk):
                    g.indirect_dma_start(table, bass.IndirectOffsetOnAxis(pos[:, par, k:k + 1], 0), slot[:, par, k, :], None)\
                        .then_inc(st_s.sem, 16)
            steps += [("pe", off, pe), ("dve", off, dv), ("pool", off, po)]

        def load_x(steps, off, par):
            def sp(s, b):
                P_pool.wait(s, b - 2, "xb")
                N_dve.wait(s, b - 2, "xn")
                ld_x.wait(s, b - 1, "x")
                settle(s, c)
                src = a["x"][b] if L0 else dram["acc0"][0:TOKENS].rearrange("(b n) d -> b n d", n=N)[b]
                s.dma_start(x[:, par, :], src).then_inc(ld_x.sem, 16)
            steps.append(("sp", off, sp))

        def load_c(steps, off, par):
            def sp(s, b):
                if L0:
                    P_pe.wait(s, b - 2, "k3")
                    settle(s, c)
                    C_dve.wait(s, b - 2, "low")
                    ld_c.wait(s, b - 1, "c")
                    settle(s, c)
                    s.dma_start(cT[:, par, :, 0:S], a["ctxT"][b].rearrange("(k p) s -> p k s", p=CK)).then_inc(ld_c.sem, 16)
                    return
                P_pe.wait(s, b - 2, "ct1")
                settle(s, c)
                N_pool.wait(s, b - 2, "mb")
                ld_c.wait(s, b - 1, "m")
                settle(s, c)
                rows = a["ctx_768"][b]
                s.dma_start(ctx[:, par, 0:2, :], rows[0:2 * CH].rearrange("(j p) c -> p j c", p=CH)).then_inc(ld_c.sem, 16)
                s.dma_start(ctx[0:S - 2 * CH, par, 2, :], rows[2 * CH:S]).then_inc(ld_c.sem, 16)
                s.dma_start(m8[:, par, :], a["mask"][b].partition_broadcast(N)).then_inc(ld_c.sem, 16)
            steps.append(("sp", off, sp))

        def project(steps, off, par, part):
            for f, *args in ([[(p_xt0,), (p_k0, 0), (p_k0, 1)], [(p_split0,), (p_q0,)], [(p_bias,), (p_k0, 2), (p_k0, 3), (p_v0, 0)],
                              [(p_v0, 1), (p_v0, 2)]] if L0 else
                             [[(p_t1,), (p_qkv1, 0), (p_qkv1, 1), (p_qkv1, 2), (p_rms, "A"), (p_qkv1, 3), (p_qkv1, 4),
                               (p_rms, "B"), (p_bias,)]])[part]:
                f(steps, off, par, *args)
        p_norm = p_norm0 if L0 else p_norm1

        def prologue():
            steps = []
            for b in range(3):
                load_x(steps, b, b % 2)
                load_c(steps, b, b % 2)
            p_norm(steps, 0, 0)
            for part in range(pairs if L0 else 1):
                project(steps, 0, 0, part)
            if L0:
                x_scores(steps, 0, 0, 0)
            p_norm(steps, 1, 1)
            return steps

        def iteration(i, par):
            par %= 2
            nxt, nx2, nx3 = (i is None or i + k < B for k in (1, 2, 3))
            prv, pr2 = (i is None or i >= k for k in (1, 2))
            steps = []

            def last(fn):
                if prv:
                    fn(steps, -1, 1 - par)

            def scores(p):
                if p < pairs:
                    x_scores(steps, 0, par, p)
                elif nxt:
                    x_scores(steps, 1, 1 - par, 0)

            def values(p):
                if p >= 0:
                    x_values(steps, 0, par, p)
                elif prv:
                    x_values(steps, -1, 1 - par, pairs - 1)

            if nx3 and not L0:
                load_c(steps, 3, 1 - par)
            if nx3:
                load_x(steps, 3, 1 - par)
            if L0:
                for p in range(pairs):
                    x_norm(steps, 0, par, p)
                    if nxt:
                        project(steps, 1, 1 - par, p)
                    if p == 1:
                        last(y_out)
                    if p == 2:
                        last(y_transpose)
                    scores(p + 1)
                    if p == 2:
                        last(y_route)
                    values(p - 1)
                    x_transpose(steps, 0, par, p)
                    if p == 1 and nx2:
                        p_norm(steps, 2, par)
                last(y_dispatch)
            else:
                def made(ok, fn, off, half, *args):
                    got = []
                    if ok:
                        fn(got, off, half, *args)
                    return {e: [x for x in got if x[0] == e] for e in ("pe", "dve", "act", "pool")}
                s0, s1 = (made(True, x_scores, 0, par, p) for p in range(2))
                n0, n1 = (made(True, x_norm, 0, par, p) for p in range(2))
                t0, t1 = (made(True, x_transpose, 0, par, p) for p in range(2))
                v0, v1 = made(True, x_values, 0, par, 0), made(prv, x_values, -1, 1 - par, 1)
                tr = made(nxt, p_t1, 1, 1 - par)
                q, kv0, kv1, kv2, kv3 = (made(nxt, p_qkv1, 1, 1 - par, j) for j in range(nch + 1))
                ra, rb = (made(nxt, p_rms, 1, 1 - par, part) for part in "AB")
                xbias, kt = made(nxt, p_bias, 1, 1 - par), made(True, p_qkt1, 0, par)
                norm = made(nx2, p_norm, 2, par)
                yo, yt, yr = (made(prv, fn, -1, 1 - par) for fn in (y_out, y_transpose, y_route))
                yd = made(pr2, y_dispatch, -2, par)

                trp, ktp = tr["pe"], kt["pe"]
                for part in (trp[:2], v1["pe"], trp[2:], ktp[:1], yo["pe"], ktp[1:]):
                    steps += part
                for stage in (s0, yd, q, kv0, s1, yt, kv1, yr, t0, kv2, kv3, v0, t1):
                    steps += stage["pe"]
                for part in (tr["act"][:2], v1["act"], tr["act"][2:]):
                    steps += part
                for stage in (kt, q, s0, kv0, yt, kv1, yr, ra, s1, t0, kv2, kv3, rb, v0, t1):
                    steps += stage["act"]
                nd, rad, rbd, yod = norm["dve"], ra["dve"], rb["dve"], yo["dve"]
                route = list(yr["dve"])

                def with_route(part, each):
                    for st in part:
                        steps.append(st)
                        steps.extend(route[:each])
                        del route[:each]
                for part in (yod[:2], s0["dve"], yod[2:], nd[:2], yd["dve"], nd[2:3], n0["dve"], nd[3:4], s1["dve"],
                             nd[4:6], rad[:1], n1["dve"]):
                    steps += part
                with_route(nd[6:], 8)
                steps += rbd[:1] + rad[1:]
                steps += route[:-4]
                steps += rbd[1:]
                steps += route[-4:]
                ng = norm["pool"]
                for part in (yo["pool"], ng[:1], n0["pool"], ng[1:3], n1["pool"], ra["pool"], rb["pool"], xbias["pool"],
                             ng[3:], yd["pool"]):
                    steps += part
            last(y_store)
            if nx3 and L0:
                load_c(steps, 3, 1 - par)
            if i == B - 4:
                steps.append(("sp", 0, lambda s, b: c.update({f"n_w{layer}": load_expert_weights(s, a, c, layer)})))
            return steps

        def epilogue():
            steps = []
            last = (B - 1) % 2
            x_values(steps, -1, last, pairs - 1)
            if not L0:
                y_out(steps, -1, last)
                y_dispatch(steps, -2, 1 - last)
            for f in ((y_out,) if L0 else ()) + (y_store, y_transpose, y_route, y_dispatch):
                f(steps, -1, last)
            return steps

        def rounds(name, eng):
            run_rounds(name, eng, prologue(), iteration, epilogue(), B, 2, 4, 4)

        with nc.Block() as block:

            @block.sync
            def _(s):
                init.wait(s, 0, "i")
                rounds("sp", s)
                s.wait_ge(st_x.sem, B * 32)

            @block.scalar
            def _(s):
                init.wait(s, 0, "i")
                rounds("act", s)

            @block.vector
            def _(v):
                for half in range(2):
                    v.memset(qz[(1 - half) * DH:(2 - half) * DH, :, half:heads:2, :], 0.0)
                for e in range(experts_n):
                    v.memset(c["base"][:, e:e + 1], float(e * REGION))
                if L0:
                    v.memset(prob[:, :, S:SP], 0.0)
                    init.post(v.memset(cT[:, :, :, S:SP], 0.0), "i")
                else:
                    v.memset(kv[96:CH, :, :, :], 0.0)
                    v.memset(ctx[96:CH, :, NCH - 1, :], 0.0)
                    v.memset(mb[:, :, 0:N], 0.0)
                    v.memset(mb[:, :, N:CH], NEG)
                    v.memset(mb[:, :, CH + S:K1], NEG)
                    v.memset(gmax[:, :], -1.0)
                    init.post(v.tensor_scalar(c["token"][:, :], c["token"][:, :], float(-TOKENS), None, ALU.add), "i")
                init.wait(v, 0, "i")
                if L0:
                    W_dve.post(v.tensor_copy(wv_hl[:, 0], c["wv0"][:, :, :]), "high")
                    W_dve.wait(v, 0, "high")
                    W_dve.post(v.tensor_tensor(wv_hl[:, 1], c["wv0"][:, :, :], wv_hl[:, 0].bitcast(F32), ALU.subtract), "low")
                rounds("dve", v)

            @block.tensor
            def _(t):
                init.wait(t, 0, "i")
                if L0:
                    W_dve.wait(t, 0, "low")
                rounds("pe", t)

            @block.gpsimd
            def _(g):
                init.wait(g, 0, "i")
                rounds("pool", g)
                g.wait_ge(st_s.sem, B * topk * 16)

        for g in (N_dve, N_pool, P_dve, P_act, P_pool, P_pe, X_pool, Y_pe, Y_dve, Y_act, Y_pool, X_pe, X_dve, X_act):
            for l in g.lanes if isinstance(g, Group) else [g]:
                assert l.seen % len(l.events) == 0, l.events


def experts(nc, maker, a, dram, c, layer):
    L0 = layer == 0
    L = str(layer)
    E, topk, F = (E0, TOP0, F0) if L0 else (E1, TOP1, F1)
    NT = most_tiles(E, topk)
    table, acc, xn_rows = dram[f"table{layer}"], dram[f"acc{layer}"], dram[f"xn{layer}"]
    ident = c["ident"]
    w = c["expert_w"]
    w13 = w[:, 0:E * 4 * F].rearrange("p (e k f) -> p e k f", e=E, k=2)
    w2 = w[:, E * 4 * F:E * 4 * F + E * (F // P) * D].rearrange("p (e k d) -> p e k d", e=E, k=F // P)
    KF = F // P
    LOOK = 3
    assert NT + LOOK <= P
    RING = 8
    stack = ExitStack()
    with stack:
        sb, ps, lane = maker(stack)
        psX = ps("psX" + L, [P, 512])
        psG = ps("psG" + L, [P, 2, 512])
        psU = ps("psU" + L, [P, 2, 512])
        psH = ps("psH" + L, [P, 512])
        psD = ps("psD" + L, [P, 2, 512])
        slots = sb("slots" + L, [P, RING, 2], I32)
        slot_w = slots[:, :, 1].bitcast(F32)
        xg = sb("xg" + L, [P, 4, D])
        xT = sb("xgT" + L, [P, 2, 2, P])
        gate = sb("gate" + L, [P, 2, F])
        hid = sb("hid" + L, [P, 2, F])
        hT = sb("hT" + L, [P, 2, KF, P])
        y = sb("y" + L, [P, 2, D])
        f = sb("tilef" + L, [P, 3, E])
        fi = sb("tilei" + L, [P, 2, E], I32)
        ahead = sb("tileu" + L, [P, E, E])
        past = sb("tilege" + L, [P, 2, E])
        tf = sb("tilet" + L, [P, 4])
        tile_e = sb("tile_e" + L, [1, P], I32)
        tile_r = sb("tile_r" + L, [1, P], I32)
        if not L0:
            bias = sb("bias1", [P, E, 3, F])
            pre = sb("pre1", [P, 2, 2 * F])
            yb = sb("yb1", [P, 2, D])

        setup_d = lane("tile_d" + L, ["n", "i", "sh", "f", "ahead", "cum", "ge", "e", "tb", "tbs", "tr", "tr2", "row", "cols", "done"])
        setup_t = lane("tile_t" + L, ["row"])
        ld_s = [lane(f"ld_s{q}_{L}", ["s"], 16).sem for q in range(4)]
        ga = lane("ga" + L, ["g"], 16)
        sc = lane("sc" + L, ["s"], 16)
        ld_b = lane("ld_b" + L, ["b"], 16)
        pe_tx, pe_g, pe_u, pe_th, pe_o = (lane(f"pe_{n}{L}", [n]) for n in ("tx", "g", "u", "th", "o"))
        act_xt, act_g, act_h = (lane(f"act_{n}{L}", [n]) for n in ("xt", "g", "h"))
        dve_h = lane("dve_h" + L, ["h"] if L0 else ["pre", "h"])
        dve_y = lane("dve_y" + L, ["y"] if L0 else ["yb", "y"])

        def slots_loaded(eng, j, r):
            eng.wait_ge(ld_s[r % 4], (j - r % 4) * 4 + 16)

        def gather(steps, off, r):
            def po(g, j):
                slots_loaded(g, j, r)
                pe_tx.wait(g, j - 4, "tx")
                ga.wait(g, j - 1, "g")
                settle(g, c)
                g.indirect_dma_start(xg[:, r % 4, :], None, xn_rows, bass.IndirectOffsetOnAxis(slots[:, r, 0:1].bitcast(U32), 0))\
                    .then_inc(ga.sem, 16)
            steps.append(("pool", off, po))

        def tx(steps, off, r):
            def t1(t, j):
                ga.wait(t, j, "g")
                act_xt.wait(t, j - 1, "xt")
                for k in range(2):
                    mm = t.transpose(psX[:, k * P:(k + 1) * P], xg[:, r % 4, k * P:(k + 1) * P], ident[:, :])
                pe_tx.post(mm, "tx")

            def a1(s, j):
                pe_tx.wait(s, j, "tx")
                pe_g.wait(s, j - 2, "g") if not L0 else pe_u.wait(s, j - 2, "u")
                act_xt.post(s.activation(xT[:, r % 2, :, :], psX[:, 0:2 * P].rearrange("p (k n) -> p k n", k=2), ACT.Copy), "xt")
            steps += [("pe", off, t1), ("act", off, a1)]

        expert = {}

        def which(steps, off, use):
            def t1(t, j):
                expert[use] = t.value_load(tile_e[0:1, bass.ds(j, 1)], min_val=0, max_val=E - 1)
            steps.append(("pe", off, t1))

        def up(steps, off, r, part):
            pst, lan = ((psG, pe_g), (psU, pe_u))[part]

            def t1(t, j):
                act_xt.wait(t, j, "xt")
                if L0:
                    (act_g if part == 0 else dve_h).wait(t, j - 2, "g" if part == 0 else "h")
                else:
                    dve_h.wait(t, j - 2, "pre")
                e = expert["up"]
                for k in range(2):
                    mm = t.matmul(pst[:, r % 2, :], xT[:, r % 2, k, :], w13[:, bass.ds(e, 1), k, part * 512:(part + 1) * 512],
                                  start=k == 0, stop=k == 1)
                lan.post(mm, "gu"[part])
            steps.append(("pe", off, t1))
            if L0 and part == 0:
                def a1(s, j):
                    pe_g.wait(s, j, "g")
                    dve_h.wait(s, j - 2, "h")
                    act_g.post(s.activation(gate[:, r % 2, :], psG[:, r % 2, :], ACT.Silu), "g")
                steps.append(("act", off, a1))
            elif L0:
                def d1(v, j):
                    pe_u.wait(v, j, "u")
                    act_g.wait(v, j, "g")
                    pe_th.wait(v, j - 2, "th")
                    dve_h.post(v.tensor_tensor(hid[:, r % 2, :], psU[:, r % 2, :], gate[:, r % 2, :], ALU.mult), "h")
                steps.append(("dve", off, d1))
            else:
                def d0(v, j):
                    e = v.value_load(tile_e[0:1, bass.ds(j, 1)], min_val=0, max_val=E - 1)
                    pe_g.wait(v, j, "g")
                    dve_h.post(v.tensor_tensor(pre[:, r % 2, :], psG[:, r % 2, :],
                                               bias[:, bass.ds(e, 1), 0:2, :].rearrange("p e k f -> p (e k f)"), ALU.add), "pre")

                def a1(s, j):
                    dve_h.wait(s, j, "pre")
                    act_g.post(s.activation(gate[:, r % 2, :], pre[:, r % 2, 0:F], ACT.Silu), "g")

                def d1(v, j):
                    act_g.wait(v, j, "g")
                    pe_th.wait(v, j - 2, "th")
                    dve_h.post(v.tensor_tensor(hid[:, r % 2, :], pre[:, r % 2, F:2 * F], gate[:, r % 2, :], ALU.mult), "h")
                steps += [("dve", off, d0), ("act", off, a1), ("dve", off, d1)]

        def th(steps, off, r):
            def t1(t, j):
                dve_h.wait(t, j, "h")
                act_h.wait(t, j - 1, "h")
                for k in range(KF):
                    mm = t.transpose(psH[:, k * P:(k + 1) * P], hid[:, r % 2, k * P:(k + 1) * P], ident[:, :])
                pe_th.post(mm, "th")

            def a1(s, j):
                pe_th.wait(s, j, "th")
                pe_o.wait(s, j - 2, "o")
                act_h.post(s.activation(hT[:, r % 2, :, :], psH[:, 0:F].rearrange("p (k n) -> p k n", k=KF), ACT.Copy), "h")
            steps += [("pe", off, t1), ("act", off, a1)]

        def down(steps, off, r):
            def t1(t, j):
                act_h.wait(t, j, "h")
                dve_y.wait(t, j - 2, "y" if L0 else "yb")
                e = expert["down"]
                for k in range(KF):
                    mm = t.matmul(psD[:, r % 2, 0:D], hT[:, r % 2, k, :], w2[:, bass.ds(e, 1), k, :], start=k == 0, stop=k == KF - 1)
                pe_o.post(mm, "o")

            def d1(v, j):
                src = psD[:, r % 2, 0:D]
                if L0:
                    pe_o.wait(v, j, "o")
                if not L0:
                    e = v.value_load(tile_e[0:1, bass.ds(j, 1)], min_val=0, max_val=E - 1)
                    pe_o.wait(v, j, "o")
                    dve_y.post(v.tensor_tensor(yb[:, r % 2, :], src, bias[:, bass.ds(e, 1), 2, :].rearrange("p e f -> p (e f)"),
                                               ALU.add), "yb")
                    dve_y.wait(v, j, "yb")
                    src = yb[:, r % 2, :]
                sc.wait(v, j - 2, "s")
                dve_y.post(v.tensor_scalar(y[:, r % 2, :], src, slot_w[:, r:r + 1], None, ALU.mult), "y")

            def po(g, j):
                dve_y.wait(g, j, "y")
                sc.wait(g, j - 1, "s")
                settle(g, c)
                g.indirect_dma_start(acc, bass.IndirectOffsetOnAxis(slots[:, r, 0:1].bitcast(U32), 0), y[:, r % 2, :], None,
                                     compute_op=ALU.add).then_inc(sc.sem, 16)
            steps += [("pe", off, t1), ("dve", off, d1), ("pool", off, po)]

        def prologue():
            steps = []
            gather(steps, 0, 0)
            gather(steps, 1, 1)
            gather(steps, 2, 2)
            tx(steps, 0, 0)
            which(steps, 0, "up")
            up(steps, 0, 0, 0)
            if L0:
                up(steps, 0, 0, 1)
            else:
                steps.remove(next(st for st in reversed(steps) if st[0] == "act"))
            return steps

        def iteration(i, r):
            def made(ok, fn, off, *args):
                got = []
                if ok:
                    fn(got, off, (r + off) % RING, *args)
                return {e: [x for x in got if x[0] == e] for e in ("pe", "dve", "act", "pool")}
            nxt, prv, old = i is None or i + 1 < NT, i is None or i > 0, i is None or i > 1
            ga, x = made(True, gather, LOOK), made(nxt, tx, 1)
            u0, u1 = made(nxt, up, 1, 0), made(nxt and L0, up, 1, 1)
            h, d = made(prv, th, -1), made(old, down, -2)
            steps = []
            if old:
                which(steps, -2, "down")
            if nxt:
                which(steps, 1, "up")
            steps += [st for part in (x, d, h, u0, u1) for st in part["pe"]]
            silu = u0 if L0 else made(True, up, 0, 0)
            steps += [st for part in ((x, h, silu) if L0 else (x, silu, h)) for st in part["act"]]
            steps += [st for part in (d, u0, u1) for st in part["dve"]] + ga["pool"] + d["pool"]
            return steps

        def epilogue():
            steps = []
            which(steps, -2, "down")
            down(steps, -2, (NT - 2) % RING)
            th(steps, -1, (NT - 1) % RING)
            which(steps, -1, "down")
            down(steps, -1, (NT - 1) % RING)
            return steps

        head = 4 + (NT - 5) % RING

        def rounds(name, eng):
            run_rounds(name, eng, prologue(), iteration, epilogue(), NT, RING, head, 1)

        with nc.Block() as block:

            @block.gpsimd
            def _(g):
                rounds("pool", g)
                g.wait_ge(sc.sem, 16 * NT)
                g.wait_ge(ga.sem, 16 * (NT + LOOK))

            @block.vector
            def _(v):
                def seq(ins, name):
                    setup_d.post(ins, name)
                    setup_d.wait(v, 0, name)
                seq(v.tensor_tensor(f[:, 0, :], c["base"][:, 0:E], c["region"][:, 0:E], ALU.subtract), "n")
                seq(v.tensor_copy(fi[:, 0, :], f[:, 0, :]), "i")
                seq(v.tensor_scalar(fi[:, 1, :], fi[:, 0, :], P.bit_length() - 1, None, ALU.arith_shift_right), "sh")
                seq(v.tensor_copy(f[:, 1, :], fi[:, 1, :]), "f")
                seq(v.tensor_tensor(ahead[:, :, :], c["upto"][:, 0:E, 0:E], f[:, 1, :].unsqueeze(1).to_broadcast([P, E, E]),
                                    ALU.mult), "ahead")
                seq(v.tensor_reduce(f[:, 2, :], ahead[:, :, :], AX, ALU.add), "cum")
                seq(v.tensor_tensor(past[:, 0, :], c["tile"][:, :].to_broadcast([P, E]), f[:, 2, :], ALU.is_ge), "ge")
                seq(v.tensor_reduce(tf[:, 0:1], past[:, 0, :], AX, ALU.add), "e")
                seq(v.tensor_tensor(past[:, 1, :], past[:, 0, :], f[:, 1, :], ALU.mult), "tb")
                seq(v.tensor_reduce(tf[:, 1:2], past[:, 1, :], AX, ALU.add), "tbs")
                seq(v.tensor_tensor(tf[:, 2:3], c["tile"][:, :], tf[:, 1:2], ALU.subtract), "tr")
                seq(v.tensor_scalar(tf[:, 2:3], tf[:, 2:3], float(P), None, ALU.mult), "tr2")
                seq(v.scalar_tensor_tensor(tf[:, 3:4], tf[:, 0:1], float(REGION), tf[:, 2:3], ALU.mult, ALU.add), "row")
                seq(v.tensor_scalar(tf[:, 2:3], tf[:, 0:1], float(E - 1), None, ALU.min), "cols")
                setup_t.wait(v, 0, "row")
                v.tensor_copy(tile_e[:, :], psX[0:1, 0:P])
                seq(v.tensor_copy(tile_r[:, :], psX[0:1, P:2 * P]), "done")
                if not L0:
                    v.wait_ge(ld_b.sem, 16 * 3)
                rounds("dve", v)

            @block.sync
            def _(s):
                setup_d.wait(s, 0, "done")

                def load(j, r):
                    sc.wait(s, j - RING, "s")
                    settle(s, c)
                    if not isinstance(j, int) or j >= 4:
                        slots_loaded(s, j - 4, r)
                    settle(s, c)
                    row = s.value_load(tile_r[0:1, bass.ds(j, 1)], min_val=0, max_val=table.shape[0] - P)
                    s.dma_start(slots[:, r, :], table[bass.ds(row, P), :]).then_inc(ld_s[r % 4], 16)
                total = NT + LOOK
                first = RING + total % RING
                for j in range(4):
                    load(j, j)
                if not L0:
                    for k, n in enumerate(("b1", "b3", "b2")):
                        s.dma_start(bias[:, :, k, :], a[f"L1_ffn_{n}"].partition_broadcast(P)).then_inc(ld_b.sem, 16)
                for j in range(4, first):
                    load(j, j % RING)
                with s.Fori(first, total - RING + 1, RING) as j:
                    for k in range(RING):
                        load(j + k, (first + k) % RING)

            @block.scalar
            def _(s):
                rounds("act", s)

            @block.tensor
            def _(t):
                setup_d.wait(t, 0, "cols")
                t.matmul(psX[0:1, 0:P], tf[:, 2:3], ident[:, :], start=True, stop=True)
                setup_t.post(t.matmul(psX[0:1, P:2 * P], tf[:, 3:4], ident[:, :], start=True, stop=True), "row")
                setup_d.wait(t, 0, "done")
                t.wait_ge(c[f"x{layer}_ready"].sem, 16 * c[f"n_w{layer}"])
                rounds("pe", t)


_SAME = ["x", "ctx_768", "g_xattn", "g_ffn", "L0_xattn_Wq", "L0_xattn_Wk", "L0_xattn_Wv", "L0_xattn_Wo", "L0_xattn_bo",
         "L0_ffn_moe_router", "L0_ffn_moe_w13", "L0_ffn_moe_w2", "L1_xattn_ln_x_g", "L1_xattn_ln_x_b",
         "L1_xattn_ln_l_g", "L1_xattn_ln_l_b", "L1_xattn_qn_g", "L1_xattn_kn_g", "L1_xattn_bo",
         "L1_ffn_b1", "L1_ffn_b2", "L1_ffn_b3"]


def kernel(**inputs):
    import numpy as _np
    import concourse.bacc as _bacc
    from concourse import mybir as _mybir
    from concourse.bass_utils import run_bass_kernel_spmd as _run

    i = {k: _np.asarray(v) for k, v in inputs.items()}
    laid = {n: i[n] for n in _SAME}
    laid["ctxT"] = i["ctx_768"].transpose(0, 2, 1)
    laid["mask"] = i["mask_BxS2_bk0"]
    for n in ("L1_xattn_Wq", "L1_xattn_Wkv", "L1_xattn_Wlkv", "L1_xattn_Wo", "L1_ffn_Wg"):
        laid[n + "T"] = i[n].T
    for n in ("L1_ffn_W1", "L1_ffn_W2", "L1_ffn_W3"):
        laid[n + "T"] = i[n].transpose(0, 2, 1)
    laid = {n: _np.ascontiguousarray(v) for n, v in laid.items()}

    nc = _bacc.Bacc("TRN2", target_bir_lowering=False, num_devices=1)
    args = {n: nc.dram_tensor(f"in_{n}", v.shape, _mybir.dt.from_np(v.dtype), kind="ExternalInput").ap()
            for n, v in laid.items()}
    out = nc.dram_tensor("out", (TOKENS + SPARE, D), F32, kind="ExternalOutput").ap()
    build(nc, args, out)
    r = _run(nc, [{f"in_{n}": v for n, v in laid.items()}], core_ids=[0])
    return r.results[0]["out"][0:TOKENS].reshape(B, N, D)
```
